# Optimizing a Trainium2 kernel written in Bass

```python
import numpy as np
import jax
import jax.numpy as jnp

def _softmax(x, axis=-1):
    return jax.nn.softmax(x, axis=axis)

def _gelu(x):
    return jax.nn.gelu(x, approximate=True)

def _silu(x):
    return jax.nn.silu(x)

def _sigmoid(x):
    return jax.nn.sigmoid(x)

def _layernorm(x, axis=-1, eps=1e-05):
    m = jnp.mean(x, axis=axis, keepdims=True)
    v = jnp.var(x, axis=axis, keepdims=True)
    return (x - m) / jnp.sqrt(v + eps)

def _scatter_add(tgt, idx, src, axis=0):
    return tgt.at[idx].add(src)

def _segment_sum(src, seg, n):
    return jax.ops.segment_sum(src, seg, n)
kernel_name = 'mk_adj_resnorm_d4_adj_r2_a53bdd'

def setup_inputs(seed: int=0):
    np.random.seed(seed)
    _w = jnp.asarray

    def _rec_inputs():
        import jax
        import jax.numpy as jnp
        _gk = jax.random.key(seed)
        x = -0.0005207 + 1.001 * jax.random.normal(jax.random.fold_in(_gk, 1), (2048, 256), jnp.float32)
        _a = jax.random.bernoulli(jax.random.fold_in(_gk, 2), 0.00390625, (2048, 2048))
        adj = _a.astype(jnp.int32)
        return (x, adj)
    x, adj = _rec_inputs()

    def _L0_gnn_setup():
        import jax, jax.numpy as jnp
        import numpy as np
        HEAD_SIZE = 8
        QK_DIM = 256
        V_DIM = 256
        N = 2048
        ATT_DIM = QK_DIM // HEAD_SIZE
        SCALE = ATT_DIM ** (-0.5)
        NEG_FILL = jnp.float32(-9000000000000000.0)
        key = jax.random.key(seed)
        k1, k2, k3, k4 = jax.random.split(key, 4)
        x1 = jax.random.normal(k1, (N, QK_DIM), dtype=jnp.float32)
        x2 = jax.random.normal(k2, (N, QK_DIM), dtype=jnp.float32)
        v = jax.random.normal(k3, (N, V_DIM), dtype=jnp.float32)
        adj = jax.random.randint(k4, (N, N), 0, 2, dtype=jnp.int32)
        return {'x1': x1, 'x2': x2, 'v': v, 'adj': adj}
    _L0_gnn_all = _L0_gnn_setup()
    _L0_gnn_in = {k: v for k, v in _L0_gnn_all.items() if k in ('x2', 'v')}
    del _L0_gnn_all

    def _L1_gnn_setup():
        import jax, jax.numpy as jnp
        import numpy as np
        N = 2048
        STATE_DIM = 256
        OUTPUT_DIM = 256
        N_STEPS = 5
        W_STD = 0.02

        def _lin_params(key, out_dim, in_dim):
            W = jax.random.normal(key, (out_dim, in_dim), dtype=jnp.float32) * W_STD
            b = jnp.zeros((out_dim,), dtype=jnp.float32)
            return (W, b)
        key = jax.random.key(seed)
        ks = jax.random.split(key, 10)
        prop_state = jax.random.normal(ks[0], (N, STATE_DIM), dtype=jnp.float32)
        A = jax.random.randint(ks[1], (N, N), 0, 2, dtype=jnp.int64)
        in_W, in_b = _lin_params(ks[2], STATE_DIM, STATE_DIM)
        out_W, out_b = _lin_params(ks[3], STATE_DIM, STATE_DIM)
        r_W, r_b = _lin_params(ks[4], STATE_DIM, 3 * STATE_DIM)
        z_W, z_b = _lin_params(ks[5], STATE_DIM, 3 * STATE_DIM)
        h_W, h_b = _lin_params(ks[6], STATE_DIM, 3 * STATE_DIM)
        o1_W, o1_b = _lin_params(ks[7], STATE_DIM, STATE_DIM)
        o2_W, o2_b = _lin_params(ks[8], OUTPUT_DIM, STATE_DIM)
        return {'prop_state': prop_state, 'A': A, 'in_W': in_W, 'in_b': in_b, 'out_W': out_W, 'out_b': out_b, 'r_W': r_W, 'r_b': r_b, 'z_W': z_W, 'z_b': z_b, 'h_W': h_W, 'h_b': h_b, 'o1_W': o1_W, 'o1_b': o1_b, 'o2_W': o2_W, 'o2_b': o2_b}
    _L1_gnn_all = _L1_gnn_setup()
    _L1_gnn_in = {k: v for k, v in _L1_gnn_all.items() if k in ('in_W', 'in_b', 'out_W', 'out_b', 'r_W', 'r_b', 'z_W', 'z_b', 'h_W', 'h_b', 'o1_W', 'o1_b', 'o2_W', 'o2_b')}
    del _L1_gnn_all

    def _L2_gnn_setup():
        import jax, jax.numpy as jnp
        import numpy as np
        N, D_IN, D_OUT = (4096, 256, 256)
        key = jax.random.key(seed)
        ks = jax.random.split(key, 8)
        scale_in = 1.0 / np.sqrt(D_IN)
        scale_cat = 1.0 / np.sqrt(2 * D_OUT)
        return {'x': jax.random.normal(ks[0], (N, D_IN), dtype=jnp.float32), 'adj': jax.random.randint(ks[1], (N, N), 0, 2, dtype=jnp.int32), 'W_self': jax.random.uniform(ks[2], (D_IN, D_OUT), jnp.float32, -scale_in, scale_in), 'b_self': jax.random.uniform(ks[3], (D_OUT,), jnp.float32, -scale_in, scale_in), 'W_nb': jax.random.uniform(ks[4], (D_IN, D_OUT), jnp.float32, -scale_in, scale_in), 'b_nb': jax.random.uniform(ks[5], (D_OUT,), jnp.float32, -scale_in, scale_in), 'W_comb': jax.random.uniform(ks[6], (2 * D_OUT, D_OUT), jnp.float32, -scale_cat, scale_cat), 'b_comb': jax.random.uniform(ks[7], (D_OUT,), jnp.float32, -scale_cat, scale_cat)}
    _L2_gnn_all = _L2_gnn_setup()
    _L2_gnn_in = {k: v for k, v in _L2_gnn_all.items() if k in ('W_self', 'b_self', 'W_nb', 'b_nb', 'W_comb', 'b_comb')}
    del _L2_gnn_all

    def _L3_gnn_setup():
        import jax, jax.numpy as jnp
        import numpy as np
        N = 2048
        IN_FEAT = 256
        EMBED = 256
        HEADS = 8
        HEAD_DIM = EMBED // HEADS
        SCALING = HEAD_DIM ** (-0.5)
        key = jax.random.key(seed)
        ks = jax.random.split(key, 7)
        x = jax.random.normal(ks[0], (N, IN_FEAT), dtype=jnp.float32)
        adj = jax.random.randint(ks[1], (N, N), 0, 2, dtype=jnp.int32)
        s = 0.04
        WQ = jax.random.normal(ks[2], (EMBED, IN_FEAT), dtype=jnp.float32) * s
        WK = jax.random.normal(ks[3], (EMBED, IN_FEAT), dtype=jnp.float32) * s
        WV = jax.random.normal(ks[4], (EMBED, IN_FEAT), dtype=jnp.float32) * s
        we = jax.random.normal(ks[5], (1, HEAD_DIM), dtype=jnp.float32) * 0.1
        be = jnp.zeros((1,), dtype=jnp.float32)
        return {'x': x, 'adj': adj, 'WQ': WQ, 'WK': WK, 'WV': WV, 'we': we, 'be': be}
    _L3_gnn_all = _L3_gnn_setup()
    _L3_gnn_in = {k: v for k, v in _L3_gnn_all.items() if k in ('WQ', 'WK', 'WV', 'we', 'be')}
    del _L3_gnn_all
    return {'x': x, 'adj': adj, 'L0_gnn_x2': _L0_gnn_in['x2'], 'L0_gnn_v': _L0_gnn_in['v'], 'L1_gnn_in_W': _L1_gnn_in['in_W'], 'L1_gnn_in_b': _L1_gnn_in['in_b'], 'L1_gnn_out_W': _L1_gnn_in['out_W'], 'L1_gnn_out_b': _L1_gnn_in['out_b'], 'L1_gnn_r_W': _L1_gnn_in['r_W'], 'L1_gnn_r_b': _L1_gnn_in['r_b'], 'L1_gnn_z_W': _L1_gnn_in['z_W'], 'L1_gnn_z_b': _L1_gnn_in['z_b'], 'L1_gnn_h_W': _L1_gnn_in['h_W'], 'L1_gnn_h_b': _L1_gnn_in['h_b'], 'L1_gnn_o1_W': _L1_gnn_in['o1_W'], 'L1_gnn_o1_b': _L1_gnn_in['o1_b'], 'L1_gnn_o2_W': _L1_gnn_in['o2_W'], 'L1_gnn_o2_b': _L1_gnn_in['o2_b'], 'L2_gnn_W_self': _L2_gnn_in['W_self'], 'L2_gnn_b_self': _L2_gnn_in['b_self'], 'L2_gnn_W_nb': _L2_gnn_in['W_nb'], 'L2_gnn_b_nb': _L2_gnn_in['b_nb'], 'L2_gnn_W_comb': _L2_gnn_in['W_comb'], 'L2_gnn_b_comb': _L2_gnn_in['b_comb'], 'L3_gnn_WQ': _L3_gnn_in['WQ'], 'L3_gnn_WK': _L3_gnn_in['WK'], 'L3_gnn_WV': _L3_gnn_in['WV'], 'L3_gnn_we': _L3_gnn_in['we'], 'L3_gnn_be': _L3_gnn_in['be']}

def reference(x, adj, L0_gnn_x2, L0_gnn_v, L1_gnn_in_W, L1_gnn_in_b, L1_gnn_out_W, L1_gnn_out_b, L1_gnn_r_W, L1_gnn_r_b, L1_gnn_z_W, L1_gnn_z_b, L1_gnn_h_W, L1_gnn_h_b, L1_gnn_o1_W, L1_gnn_o1_b, L1_gnn_o2_W, L1_gnn_o2_b, L2_gnn_W_self, L2_gnn_b_self, L2_gnn_W_nb, L2_gnn_b_nb, L2_gnn_W_comb, L2_gnn_b_comb, L3_gnn_WQ, L3_gnn_WK, L3_gnn_WV, L3_gnn_we, L3_gnn_be):
    import jax
    import jax.numpy as jnp

    def _L0_gnn_ref(x1, x2, v, adj):
        import jax, jax.numpy as jnp
        import numpy as np
        HEAD_SIZE = 8
        QK_DIM = 256
        V_DIM = 256
        N = 2048
        ATT_DIM = QK_DIM // HEAD_SIZE
        SCALE = ATT_DIM ** (-0.5)
        NEG_FILL = jnp.float32(-9000000000000000.0)
        n = x1.shape[0]
        q = x1.reshape(n, HEAD_SIZE, -1).transpose(1, 0, 2) * SCALE
        k = x2.reshape(n, HEAD_SIZE, -1).transpose(1, 0, 2)
        vv = v.reshape(n, HEAD_SIZE, -1).transpose(1, 0, 2)
        scores = jnp.einsum('hnd,hmd->hnm', q, k)
        scores = jnp.where(adj > 0, scores, NEG_FILL)
        attn = jax.nn.softmax(scores, axis=-1)
        out = jnp.einsum('hnm,hmd->hnd', attn, vv)
        return out.transpose(1, 0, 2).reshape(n, -1)

    def _L1_gnn_ref(prop_state, A, in_W, in_b, out_W, out_b, r_W, r_b, z_W, z_b, h_W, h_b, o1_W, o1_b, o2_W, o2_b):
        import jax, jax.numpy as jnp
        import numpy as np
        N = 2048
        STATE_DIM = 256
        OUTPUT_DIM = 256
        N_STEPS = 5
        W_STD = 0.02

        def _lin_params(key, out_dim, in_dim):
            W = jax.random.normal(key, (out_dim, in_dim), dtype=jnp.float32) * W_STD
            b = jnp.zeros((out_dim,), dtype=jnp.float32)
            return (W, b)
        Af = A.astype(prop_state.dtype)
        AfT = Af.T
        state = prop_state
        for _ in range(N_STEPS):
            s_in = state @ in_W.T + in_b
            s_out = state @ out_W.T + out_b
            a_in = Af @ s_in
            a_out = AfT @ s_out
            a = jnp.concatenate([a_in, a_out, state], axis=-1)
            r = jax.nn.sigmoid(a @ r_W.T + r_b)
            z = jax.nn.sigmoid(a @ z_W.T + z_b)
            joined = jnp.concatenate([a_in, a_out, r * state], axis=-1)
            h_hat = jnp.tanh(joined @ h_W.T + h_b)
            state = (1.0 - z) * state + z * h_hat
        out = jnp.tanh(state @ o1_W.T + o1_b) @ o2_W.T + o2_b
        return out

    def _L2_gnn_ref(x, adj, W_self, b_self, W_nb, b_nb, W_comb, b_comb):
        import jax, jax.numpy as jnp
        import numpy as np
        N, D_IN, D_OUT = (4096, 256, 256)
        mask = (adj > 0).astype(x.dtype)
        deg = jnp.sum(mask, axis=1, keepdims=True)
        agg = mask @ x / jnp.maximum(deg, 1.0)
        self_f = x @ W_self + b_self
        nb_f = agg @ W_nb + b_nb
        combined = jnp.concatenate([self_f, nb_f], axis=-1)
        out = combined @ W_comb + b_comb
        return jax.nn.relu(out)

    def _L3_gnn_ref(x, adj, WQ, WK, WV, we, be):
        import jax, jax.numpy as jnp
        import numpy as np
        N = 2048
        IN_FEAT = 256
        EMBED = 256
        HEADS = 8
        HEAD_DIM = EMBED // HEADS
        SCALING = HEAD_DIM ** (-0.5)
        n = x.shape[0]
        Q = (x @ WQ.T).reshape(n, HEADS, HEAD_DIM).transpose(1, 0, 2)
        K = (x @ WK.T).reshape(n, HEADS, HEAD_DIM).transpose(1, 0, 2)
        V = (x @ WV.T).reshape(n, HEADS, HEAD_DIM).transpose(1, 0, 2)
        energy = Q @ we.T + be
        attn = jnp.einsum('hqd,hkd->hqk', Q, K) * SCALING + energy
        attn = attn + jnp.where(adj > 0, 0.0, -jnp.inf)
        attn = jax.nn.softmax(attn, axis=-1)
        hard = (attn == jnp.max(attn, axis=-1, keepdims=True)).astype(jnp.float32) / HEADS
        out = jnp.einsum('hqk,hkd->hqd', hard, V)
        return out.transpose(1, 0, 2).reshape(n, EMBED)
    x = _layernorm(x + _L0_gnn_ref(x, L0_gnn_x2, L0_gnn_v, adj), axis=-1)
    x = _layernorm(x + _L1_gnn_ref(x, adj, L1_gnn_in_W, L1_gnn_in_b, L1_gnn_out_W, L1_gnn_out_b, L1_gnn_r_W, L1_gnn_r_b, L1_gnn_z_W, L1_gnn_z_b, L1_gnn_h_W, L1_gnn_h_b, L1_gnn_o1_W, L1_gnn_o1_b, L1_gnn_o2_W, L1_gnn_o2_b), axis=-1)
    x = _layernorm(x + _L2_gnn_ref(x, adj, L2_gnn_W_self, L2_gnn_b_self, L2_gnn_W_nb, L2_gnn_b_nb, L2_gnn_W_comb, L2_gnn_b_comb), axis=-1)
    x = _layernorm(x + _L3_gnn_ref(x, adj, L3_gnn_WQ, L3_gnn_WK, L3_gnn_WV, L3_gnn_we, L3_gnn_be), axis=-1)
    return x

_drawn_inputs = setup_inputs


def setup_inputs(seed=0):
    import zlib

    import numpy as np

    out = dict(_drawn_inputs(seed))
    spreads = {'L1_gnn_in_b': (0.0, 0.1),
     'L1_gnn_out_b': (0.0, 0.1),
     'L1_gnn_r_b': (0.0, 2.0),
     'L1_gnn_z_b': (0.0, 2.0),
     'L1_gnn_h_b': (0.0, 0.494),
     'L1_gnn_o1_b': (0.0, 0.1),
     'L1_gnn_o2_b': (0.0, 0.1)}
    factors = {'L1_gnn_r_W': 52.609, 'L1_gnn_z_W': 4.423, 'L2_gnn_b_self': 4.488, 'L2_gnn_b_nb': 3.919}
    for name, (base, spread) in spreads.items():
        noise = np.random.default_rng([zlib.crc32(name.encode()), seed]).standard_normal(out[name].shape)
        drawn = base * np.exp(spread * noise) if base else spread * noise
        out[name] = jnp.asarray(drawn.astype(out[name].dtype))
    for name, factor in factors.items():
        out[name] = (out[name] * factor).astype(out[name].dtype)
    return out
```

```python
from contextlib import ExitStack

import concourse.bass as bass
from concourse import mybir

ALU = mybir.AluOpType
ACT = mybir.ActivationFunctionType
F32 = mybir.dt.float32
F16 = mybir.dt.float16
BF16 = mybir.dt.bfloat16
I32 = mybir.dt.int32
AX_X = mybir.AxisListType.X

P = 128
N = 2048
D = 256
H = 8
HD = D // H
NT = N // P
DC = D // P
CW = 512
NC = N // CW
STEPS = 5
GATES = 3
EPS = 1e-5
BIG = 2.0 ** 100
STATE_SCALE = 1024.0


def split_halves(nc, eng, hi, lo, src, scale, hi_done):
    nc.vector.tensor_scalar(hi, src, scale, None, ALU.mult).then_inc(hi_done[0], 1)
    hi_done[1] += 1
    eng.wait_ge(hi_done[0], hi_done[1])
    return nc.vector.scalar_tensor_tensor(lo, src, scale, hi, ALU.mult, ALU.subtract)


def stack_halves(queue, stack, hi, lo, order, done):
    for h in range(H):
        rows = slice((h % 4) * HD, (h % 4 + 1) * HD)
        for g, half in enumerate(order):
            queue.dma_start(stack[g * HD:(g + 1) * HD, h, :], (hi, lo)[half][rows, h // 4, :]).then_inc(done, 16)
    return 16 * H * len(order)


Q_ORDER = (0, 0, 1, 1)
K_ORDER = (0, 1, 0, 1)


def masked_attention(nc, name, qs, ks, vs, X, adj, hard, scale, out_scale, score_bias):
    adj_tiles = adj.rearrange("(t p) n -> t p n", p=P)
    PAIRS = NT // 2
    UNITS = 2 * H
    LAST = PAIRS - 1
    TW = 1024 if hard else 512
    TC = N // TW
    SC = 2
    SW = N // SC
    NB = 4
    CREDIT = 2 * SC * H
    BANKS = [0, 1] if hard else [0, 1, 2, 0, 1, 2, 0, 2]
    EARLY = 2 if hard else 3
    OB = 2 if hard else 1
    low = -2.0 ** 60 if hard else -BIG
    PT = F16 if hard else F32
    with ExitStack() as ctx:
        def sb(n, shape, dt):
            return ctx.enter_context(nc.sbuf_tensor(name + n, shape, dt))

        def sem(n):
            return ctx.enter_context(nc.semaphore(name + n))

        adj_in = sb("adj_in", [P, 2, N], I32)
        mask = sb("mask", [P, 2, N], F32)
        S = sb("S", [P, NB, N], F32)
        hot = sb("hot", [P, NB, N], F16) if hard else None
        pt_hi = sb("pt_hi", [P, 2, N], F16)
        pt_lo = None if hard else sb("pt_lo", [P, 2, N], F16)
        mx = sb("mx", [P, NB, SC], F32)
        lim = sb("lim", [P, NB], F32)
        sums = sb("sums", [P, 2, H], F32)
        rinv = sb("rinv", [P, 2, H], F32)
        o_low = sb("o_low", [P, 2, H, HD], F32)
        o_sum = sb("o_sum", [P, 2, H, HD], F32)
        ident = sb("ident", [P, P], PT)
        ps_S = ctx.enter_context(nc.psum_tensor(name + "psS", [P, SC, SW], F32))
        ps_T = ctx.enter_context(nc.psum_tensor(name + "psT", [P, max(BANKS) + 1, TW], PT))
        ps_O = ctx.enter_context(nc.psum_tensor(name + "psO", [P, OB, H, 2 * HD], F32))

        adj_landed = [sem(f"adj_landed{b}") for b in range(2)]
        adj_used = sem("adj_used")
        scores_ready = sem("scores_ready")
        masked = sem("masked")
        lim_ready = sem("lim_ready")
        probs_ready = sem("probs_ready")
        transposed = sem("transposed")
        hi_ready = sem("hi_ready")
        banks_used = sem("banks_used")
        half_read = [sem(f"half_read{c}") for c in range(2)]
        pv_done = sem("pv_done")
        olow_ready = sem("olow_ready")
        o_used = sem("o_used")
        ident_ready = sem("ident_ready")
        passed_dve = sem("passed_dve")
        passed_pool = sem("passed_pool")
        tail = sem("tail")

        block = ctx.enter_context(nc.Block())

        def spot(i, j):
            return UNITS * i + j, j, j % H, 2 * i + j // H

        def bank(b, c):
            n = (TC * b + c) % len(BANKS)
            back = next(d for d in range(1, len(BANKS) + 1) if BANKS[(n - d) % len(BANKS)] == BANKS[n])
            return BANKS[n], back

        def valid(i, j):
            return not isinstance(i, int) or UNITS * i + j < UNITS * PAIRS

        def run(eng, prologue, slot):
            prologue()
            slot(0, 0)
            with eng.Fori(0, LAST) as i:
                for j in range(1, UNITS + 1):
                    slot(i, j)
            for j in range(1, UNITS + 1):
                slot(LAST, j)

        @block.sync
        def _(sp):
            def load(q, b, wait):
                if wait:
                    sp.wait_ge(adj_used, q - 1)
                sp.dma_start(adj_in[:, b, :], adj_tiles[q]).then_inc(adj_landed[b], 16)
            for b in range(2):
                load(b, b, False)
            with sp.Fori(1, PAIRS) as i:
                for b in range(2):
                    sp.wait_ge(adj_used, 2 * i + b - 1)
                    sp.dma_start(adj_in[:, b, :],
                                 adj_tiles[bass.ds(2 * i + b, 1)].rearrange("o p n -> (o p) n")
                                 ).then_inc(adj_landed[b], 16)

        @block.gpsimd
        def _(pool):
            pool.memset(ident[:], 0.0).then_inc(ident_ready, 1)
            pool.wait_ge(ident_ready, 1)
            pool.affine_select(out=ident[:], in_=ident[:], compare_op=ALU.not_equal, fill=1.0, base=0,
                               pattern=[[-1, P]], channel_multiplier=1).then_inc(ident_ready, 1)
            with pool.Fori(0, PAIRS) as i:
                for b in range(2):
                    pool.wait_ge(adj_landed[b], 16 * (i + 1))
                    pool.wait_ge(masked, CREDIT + SC * H * (2 * i + b - 1))
                    pool.sem_inc(passed_pool, 1)
                    if hard:
                        nc.gpsimd.tensor_scalar(mask[:, b, :], adj_in[:, b, :], 0.0, low, ALU.is_le, ALU.mult
                                                ).then_inc(ident_ready, 1)
                        pool.wait_ge(ident_ready, 2 + 2 * i + b + 1)
                        pool.sem_inc(passed_pool, 1)
                        nc.gpsimd.tensor_scalar(mask[:, b, :], mask[:, b, :], score_bias, None, ALU.add
                                                ).then_inc(adj_used, 1)
                    else:
                        nc.gpsimd.tensor_scalar(mask[:, b, :], adj_in[:, b, :], 0.0, low, ALU.is_le, ALU.mult
                                                ).then_inc(adj_used, 1)

        @block.tensor
        def _(pe):
            def scores(i, j, chunks):
                u, b, h, q = spot(i, j)
                for c in chunks:
                    pe.wait_ge(masked, CREDIT - SC + SC * u + c + 1)
                    for k in range(SW // CW):
                        col = c * SW + k * CW
                        last = nc.tensor.matmul(ps_S[:, c, k * CW:(k + 1) * CW],
                                                qs[:, h, bass.ds(q * P, P)] if not isinstance(q, int)
                                                else qs[:, h, q * P:(q + 1) * P],
                                                ks[:, h, col:col + CW], start=True, stop=True)
                    last.then_inc(scores_ready, 1)

            def flip(i, j, c):
                u, b, h, q = spot(i, j)
                src = hot[:, b % NB, :] if hard else S[:, b % NB, :]
                at, back = bank(b, c)
                pe.wait_ge(probs_ready, (NB if hard else 0) + u + 1)
                if hard:
                    pe.wait_ge(half_read[c], u + 1)
                else:
                    pe.wait_ge(banks_used, len(BANKS) + TC * u + c + 1 - back)
                for k in range(TW // P):
                    last = nc.tensor.transpose(ps_T[:, at, k * P:(k + 1) * P],
                                               src[:, c * TW + k * P:c * TW + (k + 1) * P], ident[:])
                last.then_inc(transposed, 1)

            def weigh(i, j):
                u, b, h, q = spot(i, j)
                if hard:
                    for c in range(TC):
                        pe.wait_ge(half_read[c], u + 2)
                else:
                    pe.wait_ge(banks_used, len(BANKS) + TC * (u + 1))
                if h == 0:
                    pe.wait_ge(o_used, q + 1)
                halves = [pt_hi] if hard else [pt_hi, pt_lo]
                for t in range(NT):
                    for half in halves:
                        last = nc.tensor.matmul(ps_O[:, (j // H) % OB, h, :], half[:, b % 2, t * P:(t + 1) * P],
                                                vs[:, t, h, :], start=(t == 0 and half is pt_hi),
                                                stop=(t == NT - 1 and half is halves[-1]))
                last.then_inc(pv_done, 1)

            def slot(i, j):
                if valid(i, j):
                    for c in range(EARLY):
                        flip(i, j, c)
                if valid(i, j + 2):
                    scores(i, j + 2, [1])
                if not (isinstance(i, int) and i == 0 and j == 0):
                    weigh(i, j - 1)
                if valid(i, j):
                    for c in range(EARLY, TC):
                        flip(i, j, c)
                if valid(i, j + 3):
                    scores(i, j + 3, [0])

            def prologue():
                pe.sem_inc(transposed, NB * TC)
                pe.sem_inc(pv_done, 2)
                pe.wait_ge(ident_ready, 2)
                for j in range(2):
                    scores(0, j, [0, 1])
                scores(0, 2, [0])

            run(pe, prologue, slot)

        @block.scalar
        def _(act):
            def exponent(i, j):
                u, b, h, q = spot(i, j)
                at = b % NB
                act.wait_ge(lim_ready, u + 1)
                if hard:
                    act.wait_ge(transposed, TC * (u + 1))
                    nc.scalar.activation(hot[:, at, :], S[:, at, :], ACT.Exp, bias=lim[:, at:at + 1],
                                         scale=scale).then_inc(probs_ready, 1)
                else:
                    nc.scalar.activation(S[:, at, :], S[:, at, :], ACT.Exp, bias=lim[:, at:at + 1], scale=scale,
                                         accum_out=sums[:, (j // H) % 2, h:h + 1]).then_inc(probs_ready, 1)

            def high(i, j, c):
                u, b, h, q = spot(i, j)
                act.wait_ge(transposed, NB * TC + TC * u + c + 1)
                if c == 0:
                    act.wait_ge(pv_done, u + 1)
                nc.scalar.activation(pt_hi[:, b % 2, c * TW:(c + 1) * TW], ps_T[:, bank(b, c)[0], :], ACT.Copy
                                     ).then_inc(half_read[c] if hard else hi_ready, 1)

            def low_out(i, j):
                u, b, h, q = spot(i, j)
                act.wait_ge(pv_done, 2 + u + 1)
                nc.scalar.activation(o_low[:, (j // H) % 2, :, :], ps_O[:, (j // H) % OB, :, HD:2 * HD], ACT.Copy
                                     ).then_inc(olow_ready, 1)

            def slot(i, j):
                if not hard and valid(i, j):
                    for c in range(TC - 1):
                        high(i, j, c)
                if valid(i, j + 1):
                    exponent(i, j + 1)
                if valid(i, j):
                    high(i, j, 0 if hard else TC - 1)
                if not (isinstance(i, int) and i == 0 and j == 0) and (j - 1) % H == H - 1:
                    low_out(i, j - 1)

            def prologue():
                if hard:
                    act.sem_inc(half_read[0], 1)
                    act.sem_inc(probs_ready, NB)
                exponent(0, 0)

            run(act, prologue, slot)

        @block.vector
        def _(dve):
            def mask_chunk(i, j, c):
                u, b, h, q = spot(i, j)
                if h == 0 and c == 0:
                    dve.wait_ge(adj_used, q + 1)
                if c == 0:
                    if hard:
                        dve.wait_ge(probs_ready, u + 1)
                    else:
                        dve.wait_ge(transposed, TC * (u + 1))
                dve.wait_ge(scores_ready, SC * u + c + 1)
                dve.sem_inc(passed_dve, 1)
                cols = slice(c * SW, (c + 1) * SW)
                nc.vector.tensor_tensor_reduce(S[:, b % NB, cols], ps_S[:, c, :], mask[:, (j // H) % 2, cols], 1.0,
                                               low / 2 if hard else -3.0e38, ALU.add, ALU.max, accum_out=mx[:, b % NB, c:c + 1]
                                               ).then_inc(masked, 1)

            def limit(i, j):
                u, b, h, q = spot(i, j)
                dve.wait_ge(masked, CREDIT + SC * (u + 1))
                at = b % NB
                nc.vector.tensor_scalar(lim[:, at:at + 1], mx[:, at, 0:1], mx[:, at, 1:2], -scale,
                                        ALU.max, ALU.mult).then_inc(lim_ready, 1)

            def take_half(i, j):
                u, b, h, q = spot(i, j)
                dve.wait_ge(transposed, NB * TC + TC * (u + 1))
                dve.wait_ge(pv_done, u + 1)
                nc.vector.tensor_copy(pt_hi[:, b % 2, TW:2 * TW], ps_T[:, bank(b, 1)[0], :]).then_inc(half_read[1], 1)

            def low_half(i, j, c):
                u, b, h, q = spot(i, j)
                cols = slice(c * TW, (c + 1) * TW)
                dve.wait_ge(hi_ready, TC * u + c + 1)
                nc.vector.tensor_tensor(pt_lo[:, b % 2, cols], ps_T[:, bank(b, c)[0], :], pt_hi[:, b % 2, cols],
                                        ALU.subtract).then_inc(banks_used, 1)

            def finish(i, j):
                u, b, h, q = spot(i, j)
                at = (j // H) % 2
                dve.wait_ge(olow_ready, q + 1)
                nc.vector.tensor_tensor(o_sum[:, at], ps_O[:, (j // H) % OB, :, 0:HD], o_low[:, at], ALU.add
                                        ).then_inc(o_used, 1)
                if not hard:
                    nc.vector.reciprocal(rinv[:, at, :], sums[:, at, :]).then_inc(tail, 1)
                    dve.wait_ge(tail, 2 * q + 1)
                dve.wait_ge(o_used, OB + q + 1)
                if not hard:
                    nc.vector.tensor_tensor(o_sum[:, at], o_sum[:, at],
                                            rinv[:, at, :].rearrange("p (h o) -> p h o", o=1).broadcast_to([P, H, HD]),
                                            ALU.mult).then_inc(tail, 1)
                    dve.wait_ge(tail, 2 * q + 2)
                xq = X[:, q, :] if isinstance(q, int) else X[:, bass.ds(q, 1), :].rearrange("p o d -> p (o d)")
                nc.vector.scalar_tensor_tensor(xq, o_sum[:, at].rearrange("p h d -> p (h d)"), out_scale, xq,
                                               ALU.mult, ALU.add)

            def slot(i, j):
                if valid(i, j + 2):
                    mask_chunk(i, j + 2, 0)
                if not hard and valid(i, j):
                    low_half(i, j, 0)
                    low_half(i, j, 1)
                if hard and valid(i, j):
                    take_half(i, j)
                if valid(i, j + 2):
                    mask_chunk(i, j + 2, 1)
                if not hard and valid(i, j):
                    low_half(i, j, 2)
                    low_half(i, j, 3)
                if valid(i, j + 2):
                    limit(i, j + 2)
                if not (isinstance(i, int) and i == 0 and j == 0) and (j - 1) % H == H - 1:
                    finish(i, j - 1)

            def prologue():
                dve.sem_inc(masked, CREDIT)
                if hard:
                    dve.sem_inc(half_read[1], 1)
                else:
                    dve.sem_inc(banks_used, len(BANKS))
                dve.sem_inc(o_used, OB)
                for j in range(2):
                    for c in range(SC):
                        mask_chunk(0, j, c)
                    limit(0, j)

            run(dve, prologue, slot)


def layer_norm(nc, name, X):
    with ExitStack() as ctx:
        def sb(n, shape, dt):
            return ctx.enter_context(nc.sbuf_tensor(name + n, shape, dt))

        def sem(n):
            return ctx.enter_context(nc.semaphore(name + n))

        stats = sb("stats", [P, NT, 6], F32)
        mean_var = sb("mean_var", [P, NT, 2], F32)
        eps = sb("eps", [P, 1], F32)
        std = sb("std", [P, NT], F32)
        rstd = sb("rstd", [P, NT], F32)
        stats_done = sem("stats_done")
        moments_done = sem("moments_done")
        std_done = sem("std_done")
        rstd_done = sem("rstd_done")
        eps_done = sem("eps_done")
        block = ctx.enter_context(nc.Block())

        @block.vector
        def _(dve):
            nc.vector.memset(eps[:], EPS).then_inc(eps_done, 1)
            for t in range(NT):
                nc.vector.bn_stats(stats[:, t, :], X[:, t, :]).then_inc(stats_done, 1)
            for t in range(NT):
                dve.wait_ge(stats_done, t + 1)
                nc.vector.bn_aggr(mean_var[:, t, :], stats[:, t, :]).then_inc(moments_done, 1)
            dve.wait_ge(std_done, 1)
            nc.vector.reciprocal(rstd[:], std[:]).then_inc(rstd_done, 1)
            dve.wait_ge(rstd_done, 1)
            for t in range(NT):
                nc.vector.tensor_scalar(X[:, t, :], X[:, t, :], mean_var[:, t, 0:1], rstd[:, t:t + 1],
                                        ALU.subtract, ALU.mult)

        @block.scalar
        def _(act):
            act.wait_ge(eps_done, 1)
            act.wait_ge(moments_done, NT)
            nc.scalar.activation(std[:], mean_var[:, :, 1], ACT.Sqrt, bias=eps[:], scale=1.0).then_inc(std_done, 1)


def to_features(nc, name, X, XT, halves, ident):
    with ExitStack() as ctx:
        ps = ctx.enter_context(nc.psum_tensor(name + "ps", [P, 2, CW], F32))
        flipped = ctx.enter_context(nc.semaphore(name + "flipped"))
        read = ctx.enter_context(nc.semaphore(name + "read"))
        hi_done = ctx.enter_context(nc.semaphore(name + "hi_done"))
        block = ctx.enter_context(nc.Block())
        groups = [(fc, c) for c in range(NC) for fc in range(DC)]

        @block.tensor
        def _(pe):
            for n, (fc, c) in enumerate(groups):
                if n >= 2:
                    pe.wait_ge(read, n - 1)
                for k in range(CW // P):
                    last = nc.tensor.transpose(ps[:, n % 2, k * P:(k + 1) * P],
                                               X[:, c * (CW // P) + k, fc * P:(fc + 1) * P], ident[:])
                last.then_inc(flipped, 1)

        @block.scalar
        def _(act):
            for n, (fc, c) in enumerate(groups):
                act.wait_ge(flipped, n + 1)
                nc.scalar.activation(XT[:, fc, c * CW:(c + 1) * CW], ps[:, n % 2, :], ACT.Copy).then_inc(read, 1)

        if halves is not None:
            @block.vector
            def _(dve):
                nc.vector.tensor_scalar(halves[:, :, 0, :], X[:, :, :], STATE_SCALE, None, ALU.mult
                                        ).then_inc(hi_done, 1)
                dve.wait_ge(hi_done, 1)
                nc.vector.scalar_tensor_tensor(halves[:, :, 1, :], X[:, :, :], STATE_SCALE, halves[:, :, 0, :],
                                               ALU.mult, ALU.subtract)


def soft_inputs(nc, xT, x2T, v, x, qs, ks, vs, X, in_scale):
    with ExitStack() as ctx:
        def sb(n, shape, dt):
            return ctx.enter_context(nc.sbuf_tensor("si_" + n, shape, dt))

        def sem(n):
            return ctx.enter_context(nc.semaphore("si_" + n))

        raw = [sb(f"raw{n}", [P, DC, N], F32) for n in range(2)]
        hi = [sb(f"hi{n}", [P, DC, N], F16) for n in range(2)]
        lo = [sb(f"lo{n}", [P, DC, N], F16) for n in range(2)]
        vraw = sb("vraw", [P, NT, D], F32)
        landed = [sem(f"landed{n}") for n in range(4)]
        hi_done = [sem("hi_done"), 0]
        halves_done = sem("halves_done")
        stacked = sem("stacked")
        block = ctx.enter_context(nc.Block())

        @block.sync
        def _(sp):
            for n, src in enumerate((x2T, xT)):
                sp.dma_start(raw[n][:], src.rearrange("(c p) n -> p c n", p=P)).then_inc(landed[n], 16)
            sp.dma_start(vraw[:], v.rearrange("(t p) d -> p t d", p=P)).then_inc(landed[2], 16)
            sp.dma_start(X[:], x.rearrange("(t p) d -> p t d", p=P)).then_inc(landed[3], 16)
            total = 0
            for n, (stack, order) in enumerate(((ks, K_ORDER), (qs, Q_ORDER))):
                sp.wait_ge(halves_done, n + 1)
                total += stack_halves(sp, stack, hi[n], lo[n], order, stacked)
            sp.wait_ge(stacked, total)
            sp.wait_ge(landed[3], 16)

        @block.vector
        def _(dve):
            for n in range(2):
                dve.wait_ge(landed[n], 16)
                split_halves(nc, dve, hi[n][:], lo[n][:], raw[n][:], in_scale, hi_done).then_inc(halves_done, 1)
            dve.wait_ge(landed[2], 16)
            vr = vraw[:].rearrange("p t (h d) -> p (t h) d", h=H)
            vv = vs[:].rearrange("p t h e -> p (t h) e")
            split_halves(nc, dve, vv[:, :, 0:HD], vv[:, :, HD:2 * HD], vr, in_scale, hi_done)


def build_adjacency(nc, adj, A, AT, deg_rows, halves_of_ones, ident16):
    with ExitStack() as ctx:
        stage = ctx.enter_context(nc.sbuf_tensor("ba_stage", [P, 2, N], I32))
        ps_T = ctx.enter_context(nc.psum_tensor("ba_ps", [P, 4, 8 * P], F16))
        ps_deg = ctx.enter_context(nc.psum_tensor("ba_deg", [6, NC, CW], F32))
        landed = [ctx.enter_context(nc.semaphore(f"ba_landed{b}")) for b in range(2)]
        cast = ctx.enter_context(nc.semaphore("ba_cast"))
        flipped = ctx.enter_context(nc.semaphore("ba_flipped"))
        read = [ctx.enter_context(nc.semaphore(f"ba_read{b}")) for b in range(2)]
        summed = ctx.enter_context(nc.semaphore("ba_summed"))
        block = ctx.enter_context(nc.Block())
        adj_tiles = adj.rearrange("(t p) n -> t p n", p=P)

        @block.sync
        def _(sp):
            for t in range(NT):
                if t >= 2:
                    sp.wait_ge(cast, t - 1)
                sp.dma_start(stage[:, t % 2, :], adj_tiles[t]).then_inc(landed[t % 2], 16)

        @block.gpsimd
        def _(pool):
            for t in range(NT):
                pool.wait_ge(landed[t % 2], 16 * (t // 2 + 1))
                nc.gpsimd.tensor_copy(A[:, t, :], stage[:, t % 2, :]).then_inc(cast, 1)

        @block.tensor
        def _(pe):
            for t in range(NT):
                pe.wait_ge(cast, t + 1)
                for g in range(2):
                    n = 2 * t + g
                    if n >= 4:
                        pe.wait_ge(read[g], t - 1)
                    for k in range(8):
                        last = nc.tensor.transpose(ps_T[:, n % 4, k * P:(k + 1) * P],
                                                   A[:, t, (8 * g + k) * P:(8 * g + k + 1) * P], ident16[:])
                    last.then_inc(flipped, 1)
            pe.wait_ge(read[0], NT)
            pe.wait_ge(read[1], NT)
            for c in range(NC):
                for n, (src, ones) in enumerate(((AT, 0), (A, 1))):
                    for t in range(NT):
                        last = nc.tensor.matmul(ps_deg[:, c, :], halves_of_ones[:, ones, :],
                                                src[:, t, c * CW:(c + 1) * CW], start=(n == 0 and t == 0),
                                                stop=(n == 1 and t == NT - 1))
            last.then_inc(summed, 1)

        def take(g, engine_copy, eng):
            for t in range(NT):
                n = 2 * t + g
                eng.wait_ge(flipped, n + 1)
                engine_copy(AT[:, 8 * g:8 * g + 8, t * P:(t + 1) * P],
                            ps_T[:, n % 4, :].rearrange("p (k i) -> p k i", i=P)).then_inc(read[g], 1)

        @block.vector
        def _(dve):
            take(0, nc.vector.tensor_copy, dve)
            dve.wait_ge(summed, 1)
            nc.vector.tensor_copy(deg_rows[:], ps_deg[:].rearrange("p c w -> p (c w)"))

        @block.scalar
        def _(act):
            take(1, lambda o, i: nc.scalar.activation(o, i, ACT.Copy), act)


def gated_weights(nc, wts, G, cparts, sel, bias_cols):
    in_W, in_b, out_W, out_b, gWT = wts
    with ExitStack() as ctx:
        def sb(n, shape, dt):
            return ctx.enter_context(nc.sbuf_tensor("gw_" + n, shape, dt))

        def sem(n):
            return ctx.enter_context(nc.semaphore("gw_" + n))

        W = [sb("W0", [P, DC, D], F32), sb("W1", [P, DC, D], F32)]
        part = sb("part", [P, 2 * DC, GATES, D], F32)
        bcol = sb("bcol", [P, 2, DC, 6], F32)
        c_all = sb("c_all", [6, GATES * D], F32)
        rest = sb("rest", [6, GATES * D], F32)
        piece = sb("piece", [6, 3, GATES * D], BF16)
        acc = sb("acc", [6, GATES * D], F32)
        bload = sb("bload", [P, 2, DC], F32)
        ps = ctx.enter_context(nc.psum_tensor("gw_ps", [P, 2, 2, CW], F32))
        psc = ctx.enter_context(nc.psum_tensor("gw_psc", [6, 2, CW], F32))
        landed = sem("landed")
        cols_ready = sem("cols_ready")
        made = sem("made")
        taken = sem("taken")
        cmade = sem("cmade")
        chain = sem("chain")
        block = ctx.enter_context(nc.Block())
        EACH = GATES * D // 2

        @block.sync
        def _(sp):
            n = 0
            for s, (w, b) in enumerate(((in_W, in_b), (out_W, out_b))):
                sp.dma_start(W[s][:], w.rearrange("(c p) f -> p c f", p=P)).then_inc(landed, 16)
                sp.dma_start(bload[:, s, :], b).then_inc(landed, 16)
                n += 2
            for g in range(GATES):
                sp.dma_start(part[:, :, g, :], gWT[g][0:2 * D, :].rearrange("(c p) f -> p c f", p=P)
                             ).then_inc(landed, 16)
                sp.dma_start(G[:, 2 * DC:3 * DC, g, :], gWT[g][2 * D:3 * D, :].rearrange("(c p) f -> p c f", p=P)
                             ).then_inc(landed, 16)
                n += 2
            for tile, src in bias_cols:
                sp.dma_start(tile, src).then_inc(landed, 16)
                n += 1
            sp.wait_ge(landed, 16 * n)
            sp.sem_inc(cols_ready, 1)

        pflat = part[:].rearrange("p c g f -> p c (g f)")
        Gflat = G[:].rearrange("p c g f -> p c (g f)")

        @block.tensor
        def _(pe):
            pe.wait_ge(cols_ready, 1)
            for n in range(2 * DC):
                s, fc = divmod(n, DC)
                if n >= 2:
                    pe.wait_ge(taken, n - 1)
                for half in range(2):
                    for kc in range(DC):
                        last = nc.tensor.matmul(ps[:, n % 2, half, 0:EACH], W[s][:, kc, fc * P:(fc + 1) * P],
                                                pflat[:, s * DC + kc, half * EACH:(half + 1) * EACH],
                                                start=(kc == 0), stop=(kc == DC - 1))
                last.then_inc(made, 1)
            pe.wait_ge(chain, 2)
            for half in range(2):
                for s in range(2):
                    for kc in range(DC):
                        last = nc.tensor.matmul(psc[:, half, 0:EACH], bcol[:, s, kc, :],
                                                pflat[:, s * DC + kc, half * EACH:(half + 1) * EACH],
                                                start=(s == 0 and kc == 0), stop=(s == 1 and kc == DC - 1))
            last.then_inc(cmade, 1)

        @block.scalar
        def _(act):
            for n in range(2 * DC):
                act.wait_ge(made, n + 1)
                nc.scalar.activation(Gflat[:, n, :].rearrange("p (a e) -> p a e", a=2), ps[:, n % 2, :, 0:EACH],
                                     ACT.Copy).then_inc(taken, 1)

        @block.vector
        def _(dve):
            count = [0]

            def link(ins):
                ins.then_inc(chain, 1)
                count[0] += 1
                dve.wait_ge(chain, count[0])

            link(nc.vector.memset(bcol[:], 0.0))
            dve.wait_ge(cols_ready, 1)
            for s in range(2):
                b = bload[:, s, :].rearrange("p (c o) -> p c o", o=1).broadcast_to([P, DC, 3])
                ins = nc.vector.tensor_copy(bcol[:, s, :, 3 * s:3 * s + 3], b)
            link(ins)
            dve.wait_ge(cmade, 1)
            link(nc.vector.tensor_copy(c_all[:].rearrange("p (a e) -> p a e", a=2), psc[:, :, 0:EACH]))
            link(nc.vector.tensor_copy(piece[:, 0, :], c_all[:]))
            link(nc.vector.tensor_tensor(rest[:], c_all[:], piece[:, 0, :], ALU.subtract))
            link(nc.vector.tensor_copy(piece[:, 1, :], rest[:]))
            link(nc.vector.tensor_tensor(piece[:, 2, :], rest[:], piece[:, 1, :], ALU.subtract))
            link(nc.vector.tensor_scalar(acc[:], piece[:, 0, :], sel[:, 0:1], None, ALU.mult))
            for k in (1, 2):
                link(nc.vector.scalar_tensor_tensor(acc[:], piece[:, k, :], sel[:, k:k + 1], acc[:],
                                                    ALU.mult, ALU.add))
            link(nc.vector.tensor_copy(cparts[:], acc[:]))


def gated_steps(nc, A, AT, ST, halves, G, cparts, deg_rows, gate_bias, ident):
    with ExitStack() as ctx:
        def sb(n, shape, dt):
            return ctx.enter_context(nc.sbuf_tensor("gs_" + n, shape, dt))

        def sem(n):
            return ctx.enter_context(nc.semaphore("gs_" + n))

        msg = sb("msg", [P, 2 * DC, CW], F32)
        r = sb("r", [P, DC, CW], F32)
        z = sb("z", [P, DC, CW], F32)
        cand = sb("cand", [P, DC, CW], F32)
        ps_msg = ctx.enter_context(nc.psum_tensor("gs_ps_msg", [P, 2 * DC, CW], F32))
        ps_gate = ctx.enter_context(nc.psum_tensor("gs_ps_gate", [P, 2, CW], F32))
        ps_T = ctx.enter_context(nc.psum_tensor("gs_ps_T", [P, 2, CW], F32))
        summed = sem("summed")
        msg_ready = sem("msg_ready")
        gate_ready = sem("gate_ready")
        gate_read = sem("gate_read")
        rs_ready = sem("rs_ready")
        delta = sem("delta")
        passed_pe = sem("passed_pe")
        flipped = sem("flipped")
        hi_done = sem("hi_done")
        lo_done = sem("lo_done")
        block = ctx.enter_context(nc.Block())
        MB = 2 * DC
        GB = GATES * DC
        TB = NT // 2

        def loops(eng, chunk, end):
            with eng.Fori(0, STEPS) as s:
                with eng.Fori(0, NC) as c:
                    chunk(s, c, s * NC + c)
                end(s)

        @block.tensor
        def _(pe):
            pe.sem_inc(gate_read, 2)
            pe.sem_inc(gate_ready, 1)

            def chunk(s, c, n):
                pe.wait_ge(lo_done, 1 + TB * s)
                pe.wait_ge(msg_ready, 1 + MB * n)
                for m in range(MB):
                    src, fc = (AT, A)[m // DC], m % DC
                    for t in range(NT):
                        for half in range(2):
                            last = nc.tensor.matmul(ps_msg[:, m, :], halves[:, t, half, fc * P:(fc + 1) * P],
                                                    src[:, t, bass.ds(c * CW, CW)], start=(t == 0 and half == 0),
                                                    stop=(t == NT - 1 and half == 1))
                    last.then_inc(summed, 1)
                for g in range(GATES):
                    for oc in range(DC):
                        k = g * DC + oc
                        pe.wait_ge(gate_read, GB * n + k + 1)
                        pe.sem_inc(passed_pe, 1)
                        out = ps_gate[:, k % 2, :]
                        cols = slice(oc * P, (oc + 1) * P)
                        nc.tensor.matmul(out, cparts[:, g * D + oc * P:g * D + (oc + 1) * P],
                                         deg_rows[:, bass.ds(c * CW, CW)], start=True, stop=False)
                        if g < 2:
                            for kc in range(DC):
                                nc.tensor.matmul(out, G[:, 2 * DC + kc, g, cols], ST[:, kc, bass.ds(c * CW, CW)],
                                                 start=False, stop=False)
                        for m in range(MB):
                            pe.wait_ge(msg_ready, 1 + MB * n + m + 1)
                            last = nc.tensor.matmul(out, G[:, m, g, cols], msg[:, m, :], start=False,
                                                    stop=(g < 2 and m == MB - 1))
                        if g == 2:
                            pe.wait_ge(rs_ready, DC * (n + 1))
                            for kc in range(DC):
                                last = nc.tensor.matmul(out, G[:, 2 * DC + kc, g, cols], r[:, kc, :],
                                                        start=False, stop=(kc == DC - 1))
                        last.then_inc(gate_ready, 1)

            def end(s):
                pe.wait_ge(delta, 1 + 3 * NC * (s + 1))
                for b in range(TB):
                    if b >= 2:
                        pe.wait_ge(lo_done, 1 + TB * s + b - 1)
                    for k in range(2):
                        for fc in range(DC):
                            at = (k * DC + fc) * P
                            t = 2 * b + k
                            last = nc.tensor.transpose(ps_T[:, b % 2, at:at + P], ST[:, fc, t * P:(t + 1) * P],
                                                       ident[:])
                    last.then_inc(flipped, 1)

            loops(pe, chunk, end)

        @block.scalar
        def _(act):
            act.sem_inc(msg_ready, 1)

            def chunk(s, c, n):
                for m in range(MB):
                    act.wait_ge(summed, MB * n + m + 1)
                    if m == 0:
                        act.wait_ge(gate_ready, 1 + GB * n)
                    nc.scalar.activation(msg[:, m, :], ps_msg[:, m, :], ACT.Copy, scale=1.0 / STATE_SCALE
                                         ).then_inc(msg_ready, 1)
                act.wait_ge(delta, 1 + 3 * n)
                for g, (out, func) in enumerate(((r, ACT.Sigmoid), (z, ACT.Sigmoid), (cand, ACT.Tanh))):
                    for oc in range(DC):
                        k = g * DC + oc
                        act.wait_ge(gate_ready, 1 + GB * n + k + 1)
                        nc.scalar.activation(out[:, oc, :], ps_gate[:, k % 2, :], func,
                                             bias=gate_bias[:, g, oc:oc + 1], scale=1.0).then_inc(gate_read, 1)

            def end(s):
                for b in range(TB):
                    act.wait_ge(flipped, TB * s + b + 1)
                    nc.scalar.activation(halves[:, 2 * b:2 * b + 2, 0, :],
                                         ps_T[:, b % 2, :].rearrange("p (k f) -> p k f", k=2), ACT.Copy,
                                         scale=STATE_SCALE).then_inc(hi_done, 1)

            loops(act, chunk, end)

        @block.vector
        def _(dve):
            dve.sem_inc(delta, 1)
            dve.sem_inc(lo_done, 1)

            def chunk(s, c, n):
                st = ST[:, :, bass.ds(c * CW, CW)]
                for oc in range(DC):
                    dve.wait_ge(gate_read, 2 + GB * n + oc + 1)
                    nc.vector.tensor_tensor(r[:, oc, :], r[:, oc, :], ST[:, oc, bass.ds(c * CW, CW)], ALU.mult
                                            ).then_inc(rs_ready, 1)
                dve.wait_ge(gate_read, 2 + GB * (n + 1))
                nc.vector.tensor_tensor(cand[:], cand[:], st, ALU.subtract).then_inc(delta, 1)
                dve.wait_ge(delta, 1 + 3 * n + 1)
                nc.vector.tensor_tensor(cand[:], cand[:], z[:], ALU.mult).then_inc(delta, 1)
                dve.wait_ge(delta, 1 + 3 * n + 2)
                nc.vector.tensor_tensor(st, st, cand[:], ALU.add).then_inc(delta, 1)

            def end(s):
                for b in range(TB):
                    dve.wait_ge(hi_done, TB * s + b + 1)
                    nc.vector.scalar_tensor_tensor(halves[:, 2 * b:2 * b + 2, 1, :],
                                                   ps_T[:, b % 2, :].rearrange("p (k f) -> p k f", k=2), STATE_SCALE,
                                                   halves[:, 2 * b:2 * b + 2, 0, :], ALU.mult, ALU.subtract
                                                   ).then_inc(lo_done, 1)

            loops(dve, chunk, end)


def feature_matmul(nc, name, YT, jobs, funcs):
    func, bias = funcs
    with ExitStack() as ctx:
        ps = ctx.enter_context(nc.psum_tensor(name + "ps", [P, 4, CW], F32))
        made = ctx.enter_context(nc.semaphore(name + "made"))
        read = ctx.enter_context(nc.semaphore(name + "read"))
        block = ctx.enter_context(nc.Block())
        banks = [(c, oc) for c in range(NC) for oc in range(DC)]

        @block.tensor
        def _(pe):
            for n, (c, oc) in enumerate(banks):
                if n >= 4:
                    pe.wait_ge(read, n - 3)
                for k, (W, XT) in enumerate(jobs):
                    for kc in range(DC):
                        last = nc.tensor.matmul(ps[:, n % 4, :], W[:, kc, oc * P:(oc + 1) * P],
                                                XT[:, kc, c * CW:(c + 1) * CW], start=(k == 0 and kc == 0),
                                                stop=(k == len(jobs) - 1 and kc == DC - 1))
                last.then_inc(made, 1)

        @block.scalar
        def _(act):
            for n, (c, oc) in enumerate(banks):
                act.wait_ge(made, n + 1)
                nc.scalar.activation(YT[:, oc, c * CW:(c + 1) * CW], ps[:, n % 4, :], func,
                                     bias=bias[:, oc:oc + 1], scale=1.0).then_inc(read, 1)


def add_residual(nc, name, X, YT, ident):
    with ExitStack() as ctx:
        ps = ctx.enter_context(nc.psum_tensor(name + "ps", [P, 4, 2, D], F32))
        flipped = ctx.enter_context(nc.semaphore(name + "flipped"))
        read = ctx.enter_context(nc.semaphore(name + "read"))
        block = ctx.enter_context(nc.Block())

        @block.tensor
        def _(pe):
            for n in range(NT // 2):
                if n >= 4:
                    pe.wait_ge(read, n - 3)
                for k in range(2):
                    t = 2 * n + k
                    for fc in range(DC):
                        last = nc.tensor.transpose(ps[:, n % 4, k, fc * P:(fc + 1) * P],
                                                   YT[:, fc, t * P:(t + 1) * P], ident[:])
                last.then_inc(flipped, 1)

        @block.vector
        def _(dve):
            for n in range(NT // 2):
                dve.wait_ge(flipped, n + 1)
                nc.vector.tensor_tensor(X[:, 2 * n:2 * n + 2, :], ps[:, n % 4], X[:, 2 * n:2 * n + 2, :], ALU.add
                                        ).then_inc(read, 1)


def mean_neighbours(nc, AT, halves, agg, ones16):
    with ExitStack() as ctx:
        rdeg = ctx.enter_context(nc.sbuf_tensor("mn_rdeg", [P, 2, CW], F32))
        top = ctx.enter_context(nc.sbuf_tensor("mn_top", [P, 2, CW], F32))
        ps = ctx.enter_context(nc.psum_tensor("mn_ps", [P, 2, 3, CW], F32))
        made = ctx.enter_context(nc.semaphore("mn_made"))
        read = ctx.enter_context(nc.semaphore("mn_read"))
        chain = ctx.enter_context(nc.semaphore("mn_chain"))
        block = ctx.enter_context(nc.Block())

        @block.tensor
        def _(pe):
            for c in range(NC):
                if c >= 2:
                    pe.wait_ge(read, 2 * (c - 1))
                cols = slice(c * CW, (c + 1) * CW)
                for t in range(NT):
                    last = nc.tensor.matmul(ps[:, c % 2, 2, :], ones16[:], AT[:, t, cols], start=(t == 0),
                                            stop=(t == NT - 1))
                last.then_inc(made, 1)
                for fc in range(DC):
                    for t in range(NT):
                        for half in range(2):
                            last = nc.tensor.matmul(ps[:, c % 2, fc, :], halves[:, t, half, fc * P:(fc + 1) * P],
                                                    AT[:, t, cols], start=(t == 0 and half == 0),
                                                    stop=(t == NT - 1 and half == 1))
                    last.then_inc(made, 1)

        @block.vector
        def _(dve):
            for c in range(NC):
                dve.wait_ge(made, 3 * c + 1)
                nc.vector.tensor_scalar(top[:, c % 2, :], ps[:, c % 2, 2, :], 1.0, STATE_SCALE, ALU.max, ALU.mult
                                        ).then_inc(chain, 1)
                dve.wait_ge(chain, 2 * c + 1)
                nc.vector.reciprocal(rdeg[:, c % 2, :], top[:, c % 2, :]).then_inc(chain, 1)
                dve.wait_ge(chain, 2 * c + 2)
                for fc in range(DC):
                    dve.wait_ge(made, 3 * c + 2 + fc)
                    nc.vector.tensor_tensor(agg[:, fc, c * CW:(c + 1) * CW], ps[:, c % 2, fc, :], rdeg[:, c % 2, :],
                                            ALU.mult).then_inc(read, 1)


def mean_weights(nc, srcs, Wx, Wa, bias, ident):
    W_selfT, b_self, W_nbT, b_nb, W_comb, b_comb = srcs
    with ExitStack() as ctx:
        def sb(n, shape, dt):
            return ctx.enter_context(nc.sbuf_tensor("mw_" + n, shape, dt))

        WT = [sb("WT0", [P, DC, D], F32), sb("WT1", [P, DC, D], F32)]
        C = sb("C", [P, 2 * DC, D], F32)
        b = sb("b", [P, 2, DC], F32)
        bc = sb("bc", [P, DC], F32)
        ps = ctx.enter_context(nc.psum_tensor("mw_ps", [P, 2, DC, D], F32))
        psb = ctx.enter_context(nc.psum_tensor("mw_psb", [P, DC], F32))
        landed = ctx.enter_context(nc.semaphore("mw_landed"))
        made = ctx.enter_context(nc.semaphore("mw_made"))
        block = ctx.enter_context(nc.Block())

        @block.sync
        def _(sp):
            for s, (w, bb) in enumerate(((W_selfT, b_self), (W_nbT, b_nb))):
                sp.dma_start(WT[s][:], w.rearrange("(c p) f -> p c f", p=P)).then_inc(landed, 16)
                sp.dma_start(b[:, s, :], bb).then_inc(landed, 16)
            sp.dma_start(C[:], W_comb.rearrange("(c p) f -> p c f", p=P)).then_inc(landed, 16)
            sp.dma_start(bc[:], b_comb).then_inc(landed, 16)

        @block.tensor
        def _(pe):
            pe.wait_ge(landed, 16 * 6)
            for s in range(2):
                for fc in range(DC):
                    for kc in range(DC):
                        nc.tensor.matmul(ps[:, s, fc, :], WT[s][:, kc, fc * P:(fc + 1) * P], C[:, s * DC + kc, :],
                                         start=(kc == 0), stop=(kc == DC - 1))
            for oc in range(DC):
                for s in range(2):
                    for kc in range(DC):
                        last = nc.tensor.matmul(psb[:, oc:oc + 1], C[:, s * DC + kc, oc * P:(oc + 1) * P],
                                                b[:, s, kc:kc + 1], start=(s == 0 and kc == 0),
                                                stop=(s == 1 and kc == DC - 1))
            last.then_inc(made, 1)

        @block.vector
        def _(dve):
            dve.wait_ge(made, 1)
            nc.vector.tensor_copy(Wx[:], ps[:, 0])
            nc.vector.tensor_copy(Wa[:], ps[:, 1])
            dve.wait_ge(landed, 16 * 6)
            nc.vector.tensor_tensor(bias[:], psb[:], bc[:], ALU.add)


def hard_inputs(nc, XT, WQT, WKT, WVT, we, be, qs, ks, vs, score_bias, q_scale, k_scale, v_scale):
    SCALING = float(HD) ** -0.5
    with ExitStack() as ctx:
        def sb(n, shape, dt):
            return ctx.enter_context(nc.sbuf_tensor("hi_" + n, shape, dt))

        def sem(n):
            return ctx.enter_context(nc.semaphore("hi_" + n))

        W = [sb(f"W{n}", [P, DC, D], F32) for n in range(3)]
        full = [sb(f"full{n}", [P, DC, N], F32) for n in range(2)]
        hi = [sb(f"hi{n}", [P, DC, N], F16) for n in range(2)]
        lo = [sb(f"lo{n}", [P, DC, N], F16) for n in range(2)]
        we_col = sb("we_col", [P, 2], F32)
        zero = sb("zero", [P, 1], F32)
        be_raw = sb("be_raw", [P, 1], F32)
        ps = ctx.enter_context(nc.psum_tensor("hi_ps", [P, 4, CW], F32))
        psv = ctx.enter_context(nc.psum_tensor("hi_psv", [P, 2, CW], F32))
        landed = sem("landed")
        consts = sem("consts")
        made = sem("made")
        read = sem("read")
        hi_done = [sem("hi_done"), 0]
        halves_done = sem("halves_done")
        stacked = sem("stacked")
        vmade = sem("vmade")
        vread = sem("vread")
        block = ctx.enter_context(nc.Block())
        banks = [(n, c, oc) for n in (1, 0) for c in range(NC) for oc in range(DC)]
        LOADS = 3 + 5

        @block.sync
        def _(sp):
            for n, w in enumerate((WQT, WKT, WVT)):
                sp.dma_start(W[n][:], w.rearrange("(c p) f -> p c f", p=P)).then_inc(landed, 16)
            for g in range(4):
                sp.dma_start(we_col[g * HD:(g + 1) * HD, 0:1], we).then_inc(landed, 16)
            sp.dma_start(be_raw[:], be.rearrange("(o d) -> o d", o=1).broadcast_to([P, 1])).then_inc(landed, 16)
            total = 0
            for m, (n, stack, order) in enumerate(((1, ks, K_ORDER), (0, qs, Q_ORDER))):
                sp.wait_ge(halves_done, m + 1)
                total += stack_halves(sp, stack, hi[n], lo[n], order, stacked)
            sp.wait_ge(stacked, total)

        @block.tensor
        def _(pe):
            pe.wait_ge(landed, 16 * LOADS)
            for m, (n, c, oc) in enumerate(banks):
                if m >= 4:
                    pe.wait_ge(read, m - 3)
                for kc in range(DC):
                    last = nc.tensor.matmul(ps[:, m % 4, :], W[n][:, kc, oc * P:(oc + 1) * P],
                                            XT[:, kc, c * CW:(c + 1) * CW], start=(kc == 0), stop=(kc == DC - 1))
                last.then_inc(made, 1)
            for t in range(NT):
                if t >= 2:
                    pe.wait_ge(vread, t - 1)
                for kc in range(DC):
                    last = nc.tensor.matmul(psv[:, t % 2, 0:D], XT[:, kc, t * P:(t + 1) * P], W[2][:, kc, :],
                                            start=(kc == 0), stop=(kc == DC - 1))
                last.then_inc(vmade, 1)

        @block.scalar
        def _(act):
            act.wait_ge(consts, 1)
            for m, (n, c, oc) in enumerate(banks):
                act.wait_ge(made, m + 1)
                nc.scalar.activation(full[n][:, oc, c * CW:(c + 1) * CW], ps[:, m % 4, :], ACT.Identity,
                                     bias=(zero[:] if n == 0 else we_col[:, 1:2]),
                                     scale=(q_scale if n == 0 else SCALING * k_scale)).then_inc(read, 1)

        @block.vector
        def _(dve):
            dve.wait_ge(landed, 16 * LOADS)
            nc.vector.memset(zero[:], 0.0)
            nc.vector.tensor_scalar(score_bias[:], be_raw[:], q_scale * k_scale, None, ALU.mult)
            nc.vector.tensor_scalar(we_col[:, 1:2], we_col[:, 0:1], k_scale, None, ALU.mult).then_inc(consts, 1)
            for m, n in enumerate((1, 0)):
                dve.wait_ge(read, (m + 1) * NC * DC)
                split_halves(nc, dve, hi[n][:], lo[n][:], full[n][:], 1.0, hi_done).then_inc(halves_done, 1)
            for t in range(NT):
                dve.wait_ge(vmade, t + 1)
                pv = psv[:, t % 2, 0:D].rearrange("p (h d) -> p h d", h=H)
                split_halves(nc, dve, vs[:, t, :, 0:HD], vs[:, t, :, HD:2 * HD], pv, v_scale, hi_done
                             ).then_inc(vread, 1)


def move(nc, name, pairs):
    with ExitStack() as ctx:
        moved = ctx.enter_context(nc.semaphore(name + "moved"))
        block = ctx.enter_context(nc.Block())

        @block.sync
        def _(sp):
            for dst, src in pairs:
                sp.dma_start(dst, src).then_inc(moved, 16)
            sp.wait_ge(moved, 16 * len(pairs))


def resnorm_kernel(nc, ins, out, spill, dbg=None, upto=99):
    rows = "(t p) d -> p t d"
    ctx = ExitStack()
    with ctx:
        def sb(scope, name, shape, dt):
            return scope.enter_context(nc.sbuf_tensor(name, shape, dt))

        def dump(tile, k):
            if dbg is not None and k in dbg:
                move(nc, f"dbg{k}", [(dbg[k], tile)])

        ident = sb(ctx, "ident", [P, P], F32)
        ident16 = sb(ctx, "ident16", [P, P], F16)
        ones16 = sb(ctx, "ones16", [P, P], F16)
        ones_sel = sb(ctx, "ones_sel", [P, 2, 6], F16)
        sel = sb(ctx, "sel", [6, 3], F32)
        move(nc, "consts", [(ident[:], ins["c_ident"]), (ident16[:], ins["c_ident16"]), (ones16[:], ins["c_ones"]),
                            (ones_sel[:], ins["c_ones_sel"]), (sel[:], ins["c_sel"])])

        IN_SCALE = 16.0
        with ExitStack() as att:
            X = sb(att, "X0", [P, NT, D], F32)
            qs = sb(att, "qs0", [P, H, N], F16)
            ks = sb(att, "ks0", [P, H, N], F16)
            vs = sb(att, "vs0", [P, NT, H, 2 * HD], F16)
            soft_inputs(nc, ins["xT"], ins["x2T"], ins["L0_gnn_v"], ins["x"], qs, ks, vs, X, IN_SCALE)
            masked_attention(nc, "a0_", qs, ks, vs, X, ins["adj"], False, float(HD) ** -0.5 / IN_SCALE ** 2,
                             1.0 / IN_SCALE, None)
            layer_norm(nc, "n0_", X)
            move(nc, "sp0", [(spill.rearrange(rows, p=P), X[:])])
        if upto == 0:
            with ExitStack() as e:
                X = sb(e, "Xd", [P, NT, D], F32)
                move(nc, "d0", [(X[:], spill.rearrange(rows, p=P))])
                move(nc, "d1", [(out.rearrange(rows, p=P), X[:])])
            return

        with ExitStack() as graph:
            AT = sb(graph, "AT", [P, NT, N], F16)
            halves = sb(graph, "halves", [P, NT, 2, D], F16)
            ST = sb(graph, "ST", [P, DC, N], F32)
            YT = None
            with ExitStack() as gated:
                G = sb(gated, "G", [P, 3 * DC, GATES, D], F32)
                cparts = sb(gated, "cparts", [6, GATES * D], BF16)
                gate_bias = sb(gated, "gate_bias", [P, GATES, DC], F32)
                gated_weights(nc, (ins["L1_gnn_in_W"], ins["L1_gnn_in_b"], ins["L1_gnn_out_W"], ins["L1_gnn_out_b"],
                                   (ins["rWT"], ins["zWT"], ins["hWT"])), G, cparts, sel,
                              [(gate_bias[:, g, :], ins[f"L1_gnn_{n}_b"]) for g, n in enumerate("rzh")])
                A = sb(gated, "A", [P, NT, N], F16)
                deg_rows = sb(gated, "deg_rows", [6, N], F16)
                with ExitStack() as first:
                    X = sb(first, "X1", [P, NT, D], F32)
                    move(nc, "ld0", [(X[:], spill.rearrange(rows, p=P))])
                    to_features(nc, "f1_", X, ST, halves, ident)
                build_adjacency(nc, ins["adj"], A, AT, deg_rows, ones_sel, ident16)
                gated_steps(nc, A, AT, ST, halves, G, cparts, deg_rows, gate_bias, ident)
            X = sb(graph, "X2", [P, NT, D], F32)
            with ExitStack() as read_out:
                o1 = sb(read_out, "o1", [P, DC, D], F32)
                o2 = sb(read_out, "o2", [P, DC, D], F32)
                ob = sb(read_out, "ob", [P, 2, DC], F32)
                HT = sb(read_out, "HT", [P, DC, N], F32)
                move(nc, "ld1", [(o1[:], ins["o1T"].rearrange("(c p) f -> p c f", p=P)),
                                 (o2[:], ins["o2T"].rearrange("(c p) f -> p c f", p=P)),
                                 (ob[:, 0, :], ins["L1_gnn_o1_b"]),
                                 (ob[:, 1, :], ins["L1_gnn_o2_b"]),
                                 (X[:], spill.rearrange(rows, p=P))])
                feature_matmul(nc, "r1_", HT, [(o1, ST)], (ACT.Tanh, ob[:, 0, :]))
                feature_matmul(nc, "r2_", ST, [(o2, HT)], (ACT.Identity, ob[:, 1, :]))
                add_residual(nc, "r3_", X, ST, ident)
            layer_norm(nc, "n1_", X)
            if upto == 1:
                move(nc, "d1", [(out.rearrange(rows, p=P), X[:])])
                return
            to_features(nc, "f2_", X, ST, halves, ident)
            with ExitStack() as mean:
                agg = sb(mean, "agg", [P, DC, N], F32)
                YT = sb(mean, "YT", [P, DC, N], F32)
                Wx = sb(mean, "Wx", [P, DC, D], F32)
                Wa = sb(mean, "Wa", [P, DC, D], F32)
                mb = sb(mean, "mb", [P, DC], F32)
                mean_weights(nc, (ins["WselfT"], ins["L2_gnn_b_self"], ins["WnbT"], ins["L2_gnn_b_nb"],
                                  ins["L2_gnn_W_comb"], ins["L2_gnn_b_comb"]), Wx, Wa, mb, ident)
                mean_neighbours(nc, AT, halves, agg, ones16)
                feature_matmul(nc, "m1_", YT, [(Wx, ST), (Wa, agg)], (ACT.Relu, mb))
                add_residual(nc, "m2_", X, YT, ident)
            layer_norm(nc, "n2_", X)
            move(nc, "sp1", [((out if upto == 2 else spill).rearrange(rows, p=P), X[:])])
            if upto == 2:
                return

        Q_SCALE, K_SCALE, V_SCALE = 64.0, 256.0, 64.0
        with ExitStack() as att:
            X = sb(att, "X3", [P, NT, D], F32)
            qs = sb(att, "qs3", [P, H, N], F16)
            ks = sb(att, "ks3", [P, H, N], F16)
            vs = sb(att, "vs3", [P, NT, H, 2 * HD], F16)
            score_bias = sb(att, "score_bias", [P, 1], F32)
            move(nc, "ld2", [(X[:], spill.rearrange(rows, p=P))])
            with ExitStack() as proj:
                XT = sb(proj, "XT", [P, DC, N], F32)
                to_features(nc, "f3_", X, XT, None, ident)
                hard_inputs(nc, XT, ins["WQT"], ins["WKT"], ins["WVT"], ins["L3_gnn_we"], ins["L3_gnn_be"],
                            qs, ks, vs, score_bias, Q_SCALE, K_SCALE, V_SCALE)
            masked_attention(nc, "a3_", qs, ks, vs, X, ins["adj"], True, 2.0 ** 66, 1.0 / (V_SCALE * H), score_bias[:])
            layer_norm(nc, "n3_", X)
            move(nc, "fin", [(out.rearrange(rows, p=P), X[:])])


_T = {"xT": "x", "x2T": "L0_gnn_x2", "rWT": "L1_gnn_r_W", "zWT": "L1_gnn_z_W", "hWT": "L1_gnn_h_W",
      "o1T": "L1_gnn_o1_W", "o2T": "L1_gnn_o2_W", "WselfT": "L2_gnn_W_self", "WnbT": "L2_gnn_W_nb",
      "WQT": "L3_gnn_WQ", "WKT": "L3_gnn_WK", "WVT": "L3_gnn_WV"}
_PLAIN = ["x", "adj", "L0_gnn_v", "L1_gnn_in_W", "L1_gnn_in_b", "L1_gnn_out_W", "L1_gnn_out_b", "L1_gnn_r_b",
          "L1_gnn_z_b", "L1_gnn_h_b", "L1_gnn_o1_b", "L1_gnn_o2_b", "L2_gnn_b_self", "L2_gnn_b_nb",
          "L2_gnn_W_comb", "L2_gnn_b_comb", "L3_gnn_we", "L3_gnn_be"]


def kernel(**inputs):
    import numpy as _np
    import concourse.bacc as _bacc
    from concourse import mybir as _mybir
    from concourse.bass_utils import run_bass_kernel_spmd as _run

    host = {n: _np.ascontiguousarray(_np.asarray(inputs[n])) for n in _PLAIN}
    host.update({n: _np.ascontiguousarray(_np.asarray(inputs[s]).T) for n, s in _T.items()})
    for n, a in host.items():
        if a.shape == (256,):
            host[n] = _np.ascontiguousarray(a.reshape(2, 128).T)
    host["L3_gnn_we"] = host["L3_gnn_we"].reshape(32, 1)
    host["c_ident"] = _np.eye(128, dtype=_np.float32)
    host["c_ident16"] = _np.eye(128, dtype=_np.float16)
    host["c_ones"] = _np.ones((128, 128), _np.float16)
    ones_sel = _np.zeros((128, 2, 6), _np.float16)
    ones_sel[:, 0, 0:3] = 1
    ones_sel[:, 1, 3:6] = 1
    host["c_ones_sel"] = ones_sel
    host["c_sel"] = _np.concatenate([_np.eye(3, dtype=_np.float32)] * 2)

    nc = _bacc.Bacc("TRN2", target_bir_lowering=False, num_devices=1)
    arrays, args = {}, {}
    for n, a in host.items():
        arrays[f"in_{n}_dram"] = a
        args[n] = nc.dram_tensor(f"in_{n}_dram", a.shape, _mybir.dt.from_np(a.dtype), kind="ExternalInput").ap()
    out = nc.dram_tensor("out_0_dram", (2048, 256), _mybir.dt.float32, kind="ExternalOutput").ap()
    spill = nc.dram_tensor("spill_dram", (2048, 256), _mybir.dt.float32, kind="Internal").ap()
    resnorm_kernel(nc, args, out, spill)
    r = _run(nc, [arrays], core_ids=[0])
    return r.results[0]["out_0_dram"]
```

```python
from contextlib import ExitStack

import concourse.bass as bass
from concourse import mybir

ALU = mybir.AluOpType
ACT = mybir.ActivationFunctionType
F32 = mybir.dt.float32
F16 = mybir.dt.float16
BF16 = mybir.dt.bfloat16
I32 = mybir.dt.int32
AX_X = mybir.AxisListType.X

P = 128
N = 2048
D = 256
H = 8
HD = D // H
NT = N // P
DC = D // P
CW = 512
NC = N // CW
STEPS = 5
GATES = 3
EPS = 1e-5
BIG = 2.0 ** 100
STATE_SCALE = 1024.0


def split_halves(nc, eng, hi, lo, src, scale, hi_done):
    nc.vector.tensor_scalar(hi, src, scale, None, ALU.mult).then_inc(hi_done[0], 1)
    hi_done[1] += 1
    eng.wait_ge(hi_done[0], hi_done[1])
    return nc.vector.scalar_tensor_tensor(lo, src, scale, hi, ALU.mult, ALU.subtract)


HG = P // HD


def stack_halves(queue, stack, hi, lo, order, heads, done):
    for h in heads:
        rows = slice(h * HD, (h + 1) * HD)
        for g, half in enumerate(order):
            queue.dma_start(stack[g * HD:(g + 1) * HD, h::HG, :], (hi, lo)[half][rows, :, :]).then_inc(done, 16)
    return 16 * len(heads) * len(order)


Q_ORDER = (0, 0, 1, 1)
K_ORDER = (0, 1, 0, 1)


def masked_attention(nc, name, qs, ks, vs, X, adj, hard, scale, out_scale, score_bias):
    adj_tiles = adj.rearrange("(t p) n -> t p n", p=P)
    PAIRS = NT // 2
    UNITS = 2 * H
    LAST = PAIRS - 1
    TW = 1024 if hard else 512
    TC = N // TW
    SC = 2
    SW = N // SC
    NB = 4
    CREDIT = 2 * SC * H
    BANKS = [0, 1] if hard else [0, 1, 2, 0, 1, 2, 0, 2]
    EARLY = 2 if hard else 3
    OB = 2 if hard else 1
    low = -2.0 ** 60 if hard else -BIG
    PT = F16 if hard else F32
    with ExitStack() as ctx:
        def sb(n, shape, dt):
            return ctx.enter_context(nc.sbuf_tensor(name + n, shape, dt))

        def sem(n):
            return ctx.enter_context(nc.semaphore(name + n))

        adj_in = sb("adj_in", [P, 2, N], I32)
        mask = sb("mask", [P, 2, N], F32)
        S = sb("S", [P, NB, N], F32)
        hot = sb("hot", [P, NB, N], F16) if hard else None
        pt_hi = sb("pt_hi", [P, 2, N], F16)
        pt_lo = None if hard else sb("pt_lo", [P, 2, N], F16)
        mn = sb("mn", [P, NB, SC], F32)
        sums = sb("sums", [P, 2, H], F32)
        rinv = sb("rinv", [P, 2, H], F32)
        o_low = sb("o_low", [P, 2, H, HD], F32)
        o_sum = sb("o_sum", [P, 2, H, HD], F32)
        ident = sb("ident", [P, P], PT)
        ps_S = ctx.enter_context(nc.psum_tensor(name + "psS", [P, SC, SW], F32))
        ps_T = ctx.enter_context(nc.psum_tensor(name + "psT", [P, max(BANKS) + 1, TW], PT))
        ps_O = ctx.enter_context(nc.psum_tensor(name + "psO", [P, OB, H, 2 * HD], F32))

        adj_landed = [sem(f"adj_landed{b}") for b in range(2)]
        adj_used = sem("adj_used")
        scores_ready = sem("scores_ready")
        masked = sem("masked")
        probs_ready = sem("probs_ready")
        transposed = sem("transposed")
        hi_ready = sem("hi_ready")
        banks_used = sem("banks_used")
        half_read = [sem(f"half_read{c}") for c in range(2)]
        pv_done = sem("pv_done")
        olow_ready = sem("olow_ready")
        o_used = sem("o_used")
        ident_ready = sem("ident_ready")
        passed_dve = sem("passed_dve")
        passed_pool = sem("passed_pool")
        tail = sem("tail")

        block = ctx.enter_context(nc.Block())

        def spot(i, j):
            return UNITS * i + j, j, j % H, 2 * i + j // H

        def bank(b, c):
            n = (TC * b + c) % len(BANKS)
            back = next(d for d in range(1, len(BANKS) + 1) if BANKS[(n - d) % len(BANKS)] == BANKS[n])
            return BANKS[n], back

        def valid(i, j):
            return not isinstance(i, int) or UNITS * i + j < UNITS * PAIRS

        def run(eng, prologue, slot):
            prologue()
            slot(0, 0)
            slot(0, 1)
            with eng.Fori(0, LAST) as i:
                for j in range(2, UNITS + 2):
                    slot(i, j)
            for j in range(2, UNITS + 2):
                slot(LAST, j)

        def previous(i, j, n):
            return not isinstance(i, int) or 0 <= UNITS * i + j - n < UNITS * PAIRS

        @block.sync
        def _(sp):
            def load(q, b, wait):
                if wait:
                    sp.wait_ge(adj_used, q - 1)
                sp.dma_start(adj_in[:, b, :], adj_tiles[q]).then_inc(adj_landed[b], 16)
            for b in range(2):
                load(b, b, False)
            with sp.Fori(1, PAIRS) as i:
                for b in range(2):
                    sp.wait_ge(adj_used, 2 * i + b - 1)
                    sp.dma_start(adj_in[:, b, :],
                                 adj_tiles[bass.ds(2 * i + b, 1)].rearrange("o p n -> (o p) n")
                                 ).then_inc(adj_landed[b], 16)

        @block.gpsimd
        def _(pool):
            pool.memset(ident[:], 0.0).then_inc(ident_ready, 1)
            pool.wait_ge(ident_ready, 1)
            pool.affine_select(out=ident[:], in_=ident[:], compare_op=ALU.not_equal, fill=1.0, base=0,
                               pattern=[[-1, P]], channel_multiplier=1).then_inc(ident_ready, 1)
            with pool.Fori(0, PAIRS) as i:
                for b in range(2):
                    pool.wait_ge(adj_landed[b], 16 * (i + 1))
                    pool.wait_ge(masked, CREDIT + SC * H * (2 * i + b - 1))
                    pool.sem_inc(passed_pool, 1)
                    if hard:
                        nc.gpsimd.tensor_scalar(mask[:, b, :], adj_in[:, b, :], 0.0, low, ALU.is_le, ALU.mult
                                                ).then_inc(ident_ready, 1)
                        pool.wait_ge(ident_ready, 2 + 2 * i + b + 1)
                        pool.sem_inc(passed_pool, 1)
                        nc.gpsimd.tensor_scalar(mask[:, b, :], mask[:, b, :], score_bias, None, ALU.add
                                                ).then_inc(adj_used, 1)
                    else:
                        nc.gpsimd.tensor_scalar(mask[:, b, :], adj_in[:, b, :], 0.0, low, ALU.is_le, ALU.mult
                                                ).then_inc(adj_used, 1)

        @block.tensor
        def _(pe):
            def scores(i, j, chunks):
                u, b, h, q = spot(i, j)
                for c in chunks:
                    pe.wait_ge(masked, CREDIT - SC + SC * u + c + 1)
                    for k in range(SW // CW):
                        col = c * SW + k * CW
                        last = nc.tensor.matmul(ps_S[:, c, k * CW:(k + 1) * CW],
                                                qs[:, h, bass.ds(q * P, P)] if not isinstance(q, int)
                                                else qs[:, h, q * P:(q + 1) * P],
                                                ks[:, h, col:col + CW], start=True, stop=True)
                    last.then_inc(scores_ready, 1)

            def flip(i, j, c):
                u, b, h, q = spot(i, j)
                src = hot[:, b % NB, :] if hard else S[:, b % NB, :]
                at, back = bank(b, c)
                pe.wait_ge(probs_ready, (NB if hard else 0) + u + 1)
                if hard:
                    pe.wait_ge(half_read[c], u + 1)
                else:
                    pe.wait_ge(banks_used, len(BANKS) + TC * u + c + 1 - back)
                for k in range(TW // P):
                    last = nc.tensor.transpose(ps_T[:, at, k * P:(k + 1) * P],
                                               src[:, c * TW + k * P:c * TW + (k + 1) * P], ident[:])
                last.then_inc(transposed, 1)

            def weigh(i, j):
                u, b, h, q = spot(i, j)
                if hard:
                    for c in range(TC):
                        pe.wait_ge(half_read[c], u + 2)
                else:
                    pe.wait_ge(banks_used, len(BANKS) + TC * (u + 1))
                if h == 0:
                    pe.wait_ge(o_used, q + 1)
                halves = [pt_hi] if hard else [pt_hi, pt_lo]
                for t in range(NT):
                    for half in halves:
                        last = nc.tensor.matmul(ps_O[:, (j // H) % OB, h, :], half[:, b % 2, t * P:(t + 1) * P],
                                                vs[:, t, h, :], start=(t == 0 and half is pt_hi),
                                                stop=(t == NT - 1 and half is halves[-1]))
                last.then_inc(pv_done, 1)

            def slot(i, j):
                if valid(i, j):
                    for c in range(EARLY):
                        flip(i, j, c)
                if valid(i, j + 2):
                    scores(i, j + 2, [1])
                if previous(i, j, 1):
                    weigh(i, j - 1)
                if valid(i, j):
                    for c in range(EARLY, TC):
                        flip(i, j, c)
                if valid(i, j + 3):
                    scores(i, j + 3, [0])

            def prologue():
                pe.sem_inc(transposed, NB * TC)
                pe.sem_inc(pv_done, 2)
                pe.wait_ge(ident_ready, 2)
                for j in range(2):
                    scores(0, j, [0, 1])
                scores(0, 2, [0])

            run(pe, prologue, slot)

        @block.scalar
        def _(act):
            def exponent(i, j):
                u, b, h, q = spot(i, j)
                at = b % NB
                act.wait_ge(masked, CREDIT + SC * (u + 1))
                if hard:
                    act.wait_ge(transposed, TC * (u + 1))
                    nc.scalar.activation(hot[:, at, :], S[:, at, :], ACT.Exp, bias=mn[:, at, 1:2],
                                         scale=-1.0).then_inc(probs_ready, 1)
                else:
                    nc.scalar.activation(S[:, at, :], S[:, at, :], ACT.Exp, bias=mn[:, at, 1:2], scale=-1.0,
                                         accum_out=sums[:, (j // H) % 2, h:h + 1]).then_inc(probs_ready, 1)

            def high(i, j, c):
                u, b, h, q = spot(i, j)
                act.wait_ge(transposed, NB * TC + TC * u + c + 1)
                if c == 0:
                    act.wait_ge(pv_done, u + 1)
                nc.scalar.activation(pt_hi[:, b % 2, c * TW:(c + 1) * TW], ps_T[:, bank(b, c)[0], :], ACT.Copy
                                     ).then_inc(half_read[c] if hard else hi_ready, 1)

            def low_out(i, j):
                u, b, h, q = spot(i, j)
                act.wait_ge(pv_done, 2 + u + 1)
                nc.scalar.activation(o_low[:, (j // H) % 2, :, :], ps_O[:, (j // H) % OB, :, HD:2 * HD], ACT.Copy
                                     ).then_inc(olow_ready, 1)

            def slot(i, j):
                if not hard and valid(i, j):
                    for c in range(TC - 1):
                        high(i, j, c)
                if valid(i, j + 1):
                    exponent(i, j + 1)
                if valid(i, j):
                    high(i, j, 0 if hard else TC - 1)
                if previous(i, j, 1) and (j - 1) % H == H - 1:
                    low_out(i, j - 1)

            def prologue():
                if hard:
                    act.sem_inc(half_read[0], 1)
                    act.sem_inc(probs_ready, NB)
                exponent(0, 0)

            run(act, prologue, slot)

        @block.vector
        def _(dve):
            def mask_chunk(i, j, c):
                u, b, h, q = spot(i, j)
                if h == 0 and c == 0:
                    dve.wait_ge(adj_used, q + 1)
                if c == 0:
                    if hard:
                        dve.wait_ge(probs_ready, u + 1)
                    else:
                        dve.wait_ge(transposed, TC * (u + 1))
                if c:
                    dve.wait_ge(masked, CREDIT + SC * u + c)
                dve.wait_ge(scores_ready, SC * u + c + 1)
                dve.sem_inc(passed_dve, 1)
                cols = slice(c * SW, (c + 1) * SW)
                nc.vector.tensor_tensor_reduce(S[:, b % NB, cols], ps_S[:, c, :], mask[:, (j // H) % 2, cols], -scale,
                                               mn[:, b % NB, 0:1] if c else -scale * low / 2 if hard else 3.0e38,
                                               ALU.add, ALU.min, accum_out=mn[:, b % NB, c:c + 1]).then_inc(masked, 1)

            def take_half(i, j):
                u, b, h, q = spot(i, j)
                dve.wait_ge(transposed, NB * TC + TC * (u + 1))
                dve.wait_ge(pv_done, u + 1)
                nc.vector.tensor_copy(pt_hi[:, b % 2, TW:2 * TW], ps_T[:, bank(b, 1)[0], :]).then_inc(half_read[1], 1)

            def low_half(i, j, c):
                u, b, h, q = spot(i, j)
                cols = slice(c * TW, (c + 1) * TW)
                dve.wait_ge(hi_ready, TC * u + c + 1)
                nc.vector.tensor_tensor(pt_lo[:, b % 2, cols], ps_T[:, bank(b, c)[0], :], pt_hi[:, b % 2, cols],
                                        ALU.subtract).then_inc(banks_used, 1)

            def add_halves(i, j):
                u, b, h, q = spot(i, j)
                at = (j // H) % 2
                dve.wait_ge(olow_ready, q + 1)
                nc.vector.tensor_tensor(o_sum[:, at], ps_O[:, (j // H) % OB, :, 0:HD], o_low[:, at], ALU.add
                                        ).then_inc(o_used, 1)
                if not hard:
                    nc.vector.reciprocal(rinv[:, at, :], sums[:, at, :]).then_inc(tail, 1)

            def normalise(i, j):
                u, b, h, q = spot(i, j)
                at = (j // H) % 2
                dve.wait_ge(tail, 2 * q + 1)
                dve.wait_ge(o_used, OB + q + 1)
                nc.vector.tensor_tensor(o_sum[:, at], o_sum[:, at],
                                        rinv[:, at, :].rearrange("p (h o) -> p h o", o=1).broadcast_to([P, H, HD]),
                                        ALU.mult).then_inc(tail, 1)

            def add_to_x(i, j):
                u, b, h, q = spot(i, j)
                at = (j // H) % 2
                if hard:
                    dve.wait_ge(o_used, OB + q + 1)
                else:
                    dve.wait_ge(tail, 2 * q + 2)
                xq = X[:, q, :] if isinstance(q, int) else X[:, bass.ds(q, 1), :].rearrange("p o d -> p (o d)")
                nc.vector.scalar_tensor_tensor(xq, o_sum[:, at].rearrange("p h d -> p (h d)"), out_scale, xq,
                                               ALU.mult, ALU.add)

            def slot(i, j):
                ending = previous(i, j, 2) and (j - 2) % H == H - 1
                if valid(i, j + 2):
                    mask_chunk(i, j + 2, 0)
                if ending:
                    add_halves(i, j - 2)
                if not hard and valid(i, j):
                    low_half(i, j, 0)
                    low_half(i, j, 1)
                if hard and valid(i, j):
                    take_half(i, j)
                if ending and not hard:
                    normalise(i, j - 2)
                if valid(i, j + 2):
                    mask_chunk(i, j + 2, 1)
                if not hard and valid(i, j):
                    low_half(i, j, 2)
                    low_half(i, j, 3)
                if ending:
                    add_to_x(i, j - 2)

            def prologue():
                dve.sem_inc(masked, CREDIT)
                if hard:
                    dve.sem_inc(half_read[1], 1)
                else:
                    dve.sem_inc(banks_used, len(BANKS))
                dve.sem_inc(o_used, OB)
                for j in range(2):
                    for c in range(SC):
                        mask_chunk(0, j, c)

            run(dve, prologue, slot)


def layer_norm(nc, name, X):
    with ExitStack() as ctx:
        def sb(n, shape, dt):
            return ctx.enter_context(nc.sbuf_tensor(name + n, shape, dt))

        def sem(n):
            return ctx.enter_context(nc.semaphore(name + n))

        stats = sb("stats", [P, NT, 6], F32)
        mean_var = sb("mean_var", [P, NT, 2], F32)
        eps = sb("eps", [P, 1], F32)
        std = sb("std", [P, NT], F32)
        rstd = sb("rstd", [P, NT], F32)
        stats_done = sem("stats_done")
        moments_done = sem("moments_done")
        std_done = sem("std_done")
        rstd_done = sem("rstd_done")
        eps_done = sem("eps_done")
        block = ctx.enter_context(nc.Block())

        @block.vector
        def _(dve):
            nc.vector.memset(eps[:], EPS).then_inc(eps_done, 1)
            for t in range(NT):
                nc.vector.bn_stats(stats[:, t, :], X[:, t, :]).then_inc(stats_done, 1)
            for t in range(NT):
                dve.wait_ge(stats_done, t + 1)
                nc.vector.bn_aggr(mean_var[:, t, :], stats[:, t, :]).then_inc(moments_done, 1)
            dve.wait_ge(std_done, 1)
            nc.vector.reciprocal(rstd[:], std[:]).then_inc(rstd_done, 1)
            dve.wait_ge(rstd_done, 1)
            for t in range(NT):
                nc.vector.tensor_scalar(X[:, t, :], X[:, t, :], mean_var[:, t, 0:1], rstd[:, t:t + 1],
                                        ALU.subtract, ALU.mult)

        @block.scalar
        def _(act):
            act.wait_ge(eps_done, 1)
            act.wait_ge(moments_done, NT)
            nc.scalar.activation(std[:], mean_var[:, :, 1], ACT.Sqrt, bias=eps[:], scale=1.0).then_inc(std_done, 1)


def to_features(nc, name, X, XT, halves, ident):
    with ExitStack() as ctx:
        ps = ctx.enter_context(nc.psum_tensor(name + "ps", [P, 2, CW], F32))
        flipped = ctx.enter_context(nc.semaphore(name + "flipped"))
        read = ctx.enter_context(nc.semaphore(name + "read"))
        hi_done = ctx.enter_context(nc.semaphore(name + "hi_done"))
        block = ctx.enter_context(nc.Block())
        groups = [(fc, c) for c in range(NC) for fc in range(DC)]

        @block.tensor
        def _(pe):
            for n, (fc, c) in enumerate(groups):
                if n >= 2:
                    pe.wait_ge(read, n - 1)
                for k in range(CW // P):
                    last = nc.tensor.transpose(ps[:, n % 2, k * P:(k + 1) * P],
                                               X[:, c * (CW // P) + k, fc * P:(fc + 1) * P], ident[:])
                last.then_inc(flipped, 1)

        @block.scalar
        def _(act):
            for n, (fc, c) in enumerate(groups):
                act.wait_ge(flipped, n + 1)
                nc.scalar.activation(XT[:, fc, c * CW:(c + 1) * CW], ps[:, n % 2, :], ACT.Copy).then_inc(read, 1)

        if halves is not None:
            @block.vector
            def _(dve):
                nc.vector.tensor_scalar(halves[:, :, 0, :], X[:, :, :], STATE_SCALE, None, ALU.mult
                                        ).then_inc(hi_done, 1)
                dve.wait_ge(hi_done, 1)
                nc.vector.scalar_tensor_tensor(halves[:, :, 1, :], X[:, :, :], STATE_SCALE, halves[:, :, 0, :],
                                               ALU.mult, ALU.subtract)


class GatedWeights:

    EACH = GATES * D // 2

    def __init__(self, nc, ctx, ins, G, cparts, gate_bias, sel):
        def sb(n, shape, dt):
            return ctx.enter_context(nc.sbuf_tensor("gw_" + n, shape, dt))

        def sem(n):
            return ctx.enter_context(nc.semaphore("gw_" + n))

        self.nc, self.ins, self.G, self.cparts, self.gate_bias, self.sel = nc, ins, G, cparts, gate_bias, sel
        self.W = [sb("W0", [P, DC, D], F32), sb("W1", [P, DC, D], F32)]
        self.part = sb("part", [P, 2 * DC, GATES, D], F32)
        self.bcol = sb("bcol", [P, 2, DC, 6], F32)
        self.bload = sb("bload", [P, 2, DC], F32)
        self.c_all = sb("c_all", [6, GATES * D], F32)
        self.piece = sb("piece", [6, 3, GATES * D], BF16)
        self.ps = ctx.enter_context(nc.psum_tensor("gw_ps", [P, 2, 2, CW], F32))
        self.psc = ctx.enter_context(nc.psum_tensor("gw_psc", [6, 2, CW], F32))
        self.landed = sem("landed")
        self.made = sem("made")
        self.taken = sem("taken")
        self.cmade = sem("cmade")
        self.chain = sem("chain")
        self.loads = 4 + 3 * GATES

    def load(self, sp):
        ins = self.ins
        for s, n in enumerate(("in", "out")):
            sp.dma_start(self.W[s][:], ins[f"L1_gnn_{n}_W"].rearrange("(c p) f -> p c f", p=P)
                         ).then_inc(self.landed, 16)
            sp.dma_start(self.bload[:, s, :], ins[f"L1_gnn_{n}_b"]).then_inc(self.landed, 16)
        for g, n in enumerate("rzh"):
            w = ins[n + "WT"]
            sp.dma_start(self.part[:, :, g, :], w[0:2 * D, :].rearrange("(c p) f -> p c f", p=P)
                         ).then_inc(self.landed, 16)
            sp.dma_start(self.G[:, 2 * DC:3 * DC, g, :], w[2 * D:3 * D, :].rearrange("(c p) f -> p c f", p=P)
                         ).then_inc(self.landed, 16)
            sp.dma_start(self.gate_bias[:, g, :], ins[f"L1_gnn_{n}_b"]).then_inc(self.landed, 16)

    def products(self, pe):
        nc, EACH = self.nc, self.EACH
        pflat = self.part[:].rearrange("p c g f -> p c (g f)")
        pe.wait_ge(self.landed, 16 * self.loads)
        for n in range(2 * DC):
            s, fc = divmod(n, DC)
            if n >= 2:
                pe.wait_ge(self.taken, n - 1)
            for half in range(2):
                for kc in range(DC):
                    last = nc.tensor.matmul(self.ps[:, n % 2, half, 0:EACH], self.W[s][:, kc, fc * P:(fc + 1) * P],
                                            pflat[:, s * DC + kc, half * EACH:(half + 1) * EACH],
                                            start=(kc == 0), stop=(kc == DC - 1))
            last.then_inc(self.made, 1)
        pe.wait_ge(self.chain, 2)
        for half in range(2):
            for s in range(2):
                for kc in range(DC):
                    last = nc.tensor.matmul(self.psc[:, half, 0:EACH], self.bcol[:, s, kc, :],
                                            pflat[:, s * DC + kc, half * EACH:(half + 1) * EACH],
                                            start=(s == 0 and kc == 0), stop=(s == 1 and kc == DC - 1))
        last.then_inc(self.cmade, 1)

    def copies(self, act):
        Gflat = self.G[:].rearrange("p c g f -> p c (g f)")
        for n in range(2 * DC):
            act.wait_ge(self.made, n + 1)
            self.nc.scalar.activation(Gflat[:, n, :].rearrange("p (a e) -> p a e", a=2),
                                      self.ps[:, n % 2, :, 0:self.EACH], ACT.Copy).then_inc(self.taken, 1)

    def degree_parts(self, dve):
        nc, piece, sel, c_all = self.nc, self.piece, self.sel, self.c_all
        count = [0]

        def link(ins):
            ins.then_inc(self.chain, 1)
            count[0] += 1
            dve.wait_ge(self.chain, count[0])

        link(nc.vector.memset(self.bcol[:], 0.0))
        dve.wait_ge(self.landed, 16 * self.loads)
        for s in range(2):
            b = self.bload[:, s, :].rearrange("p (c o) -> p c o", o=1).broadcast_to([P, DC, 3])
            ins = nc.vector.tensor_copy(self.bcol[:, s, :, 3 * s:3 * s + 3], b)
        link(ins)
        dve.wait_ge(self.cmade, 1)
        link(nc.vector.tensor_copy(c_all[:].rearrange("p (a e) -> p a e", a=2), self.psc[:, :, 0:self.EACH]))
        link(nc.vector.tensor_copy(piece[:, 0, :], c_all[:]))
        link(nc.vector.tensor_tensor(c_all[:], c_all[:], piece[:, 0, :], ALU.subtract))
        link(nc.vector.tensor_copy(piece[:, 1, :], c_all[:]))
        link(nc.vector.tensor_tensor(piece[:, 2, :], c_all[:], piece[:, 1, :], ALU.subtract))
        link(nc.vector.tensor_scalar(c_all[:], piece[:, 0, :], sel[:, 0:1], None, ALU.mult))
        for k in (1, 2):
            link(nc.vector.scalar_tensor_tensor(c_all[:], piece[:, k, :], sel[:, k:k + 1], c_all[:],
                                                ALU.mult, ALU.add))
        nc.vector.tensor_copy(self.cparts[:], c_all[:])


def soft_inputs(nc, ins, weights, qs, ks, vs, X, in_scale):
    xT, x2T, v, x = ins["xT"], ins["x2T"], ins["L0_gnn_v"], ins["x"]
    with ExitStack() as ctx:
        def sb(n, shape, dt):
            return ctx.enter_context(nc.sbuf_tensor("si_" + n, shape, dt))

        def sem(n):
            return ctx.enter_context(nc.semaphore("si_" + n))

        raw = [sb(f"raw{n}", [P, DC, N], F32) for n in range(2)]
        hi = [sb(f"hi{n}", [P, DC, N], F16) for n in range(2)]
        lo = [sb(f"lo{n}", [P, DC, N], F16) for n in range(2)]
        gated = GatedWeights(nc, ctx, ins, *weights)
        landed = [sem(f"landed{n}") for n in range(4)]
        hi_done = [sem("hi_done"), 0]
        halves_done = sem("halves_done")
        stacked = [sem(f"stacked{n}") for n in range(2)]
        block = ctx.enter_context(nc.Block())

        @block.sync
        def _(sp):
            for n, src in enumerate((x2T, xT)):
                sp.dma_start(raw[n][:], src.rearrange("(c p) n -> p c n", p=P)).then_inc(landed[n], 16)
            sp.dma_start(X[:], x.rearrange("(t p) d -> p t d", p=P)).then_inc(landed[3], 16)
            gated.load(sp)
            sp.wait_ge(halves_done, 1)
            sp.dma_start(raw[0][:].rearrange("p c n -> p (c n)").rearrange("p (t d) -> p t d", d=D),
                         v.rearrange("(t p) d -> p t d", p=P)).then_inc(landed[2], 16)
            total = 0
            for n, (stack, order) in enumerate(((ks, K_ORDER), (qs, Q_ORDER))):
                sp.wait_ge(halves_done, n + 1)
                total += stack_halves(sp, stack, hi[n], lo[n], order, range(0, HG // 2), stacked[0])
            sp.wait_ge(stacked[0], total)
            sp.wait_ge(landed[3], 16)

        @block.scalar
        def _(act):
            total = 0
            for n, (stack, order) in enumerate(((ks, K_ORDER), (qs, Q_ORDER))):
                act.wait_ge(halves_done, n + 1)
                total += stack_halves(act, stack, hi[n], lo[n], order, range(HG // 2, HG), stacked[1])
            gated.copies(act)
            act.wait_ge(stacked[1], total)

        @block.tensor
        def _(pe):
            gated.products(pe)

        @block.vector
        def _(dve):
            for n in range(2):
                dve.wait_ge(landed[n], 16)
                split_halves(nc, dve, hi[n][:], lo[n][:], raw[n][:], in_scale, hi_done).then_inc(halves_done, 1)
            dve.wait_ge(landed[2], 16)
            vr = raw[0][:].rearrange("p c n -> p (c n)").rearrange("p (t d) -> p t d", d=HD)
            vv = vs[:].rearrange("p t h e -> p (t h) e")
            split_halves(nc, dve, vv[:, :, 0:HD], vv[:, :, HD:2 * HD], vr, in_scale, hi_done)
            gated.degree_parts(dve)


def build_adjacency(nc, adj, A, AT, deg_rows, ones_sel, ident16):
    with ExitStack() as ctx:
        stage = ctx.enter_context(nc.sbuf_tensor("ba_stage", [P, 2, N], I32))
        row_sum = ctx.enter_context(nc.sbuf_tensor("ba_row_sum", [P, NT], F32))
        row_cols = ctx.enter_context(nc.sbuf_tensor("ba_row_cols", [P, NT, 6], F16))
        ps_T = ctx.enter_context(nc.psum_tensor("ba_ps", [P, 4, 8 * P], F16))
        ps_deg = ctx.enter_context(nc.psum_tensor("ba_deg", [6, NC, CW], F32))
        landed = [ctx.enter_context(nc.semaphore(f"ba_landed{b}")) for b in range(2)]
        cast = ctx.enter_context(nc.semaphore("ba_cast"))
        cols_ready = ctx.enter_context(nc.semaphore("ba_cols"))
        flipped = ctx.enter_context(nc.semaphore("ba_flipped"))
        read = ctx.enter_context(nc.semaphore("ba_read"))
        summed = ctx.enter_context(nc.semaphore("ba_summed"))
        block = ctx.enter_context(nc.Block())
        adj_tiles = adj.rearrange("(t p) n -> t p n", p=P)

        @block.sync
        def _(sp):
            for t in range(NT):
                if t >= 2:
                    sp.wait_ge(cast, t - 1)
                sp.dma_start(stage[:, t % 2, :], adj_tiles[t]).then_inc(landed[t % 2], 16)

        @block.scalar
        def _(act):
            for t in range(NT):
                act.wait_ge(landed[t % 2], 16 * (t // 2 + 1))
                nc.scalar.activation(A[:, t, :], stage[:, t % 2, :], ACT.Copy, accum_out=row_sum[:, t:t + 1]
                                     ).then_inc(cast, 1)

        @block.tensor
        def _(pe):
            for t in range(NT):
                pe.wait_ge(cast, t + 1)
                for g in range(2):
                    n = 2 * t + g
                    if n >= 4:
                        pe.wait_ge(read, n - 3)
                    for k in range(8):
                        last = nc.tensor.transpose(ps_T[:, n % 4, k * P:(k + 1) * P],
                                                   A[:, t, (8 * g + k) * P:(8 * g + k + 1) * P], ident16[:])
                    last.then_inc(flipped, 1)
                for row_t in ([t - 1] if 0 < t < NT - 1 else [t - 1, t] if t else []):
                    pe.wait_ge(cols_ready, row_t + 2)
                    c, k = divmod(row_t, CW // P)
                    nc.tensor.matmul(ps_deg[:, c, k * P:(k + 1) * P], row_cols[:, row_t, :], ident16[:],
                                     start=False, stop=False)
                for c in range(NC):
                    last = nc.tensor.matmul(ps_deg[:, c, :], ones_sel[:, 1, :], A[:, t, c * CW:(c + 1) * CW],
                                            start=(t == 0), stop=(t == NT - 1))
            last.then_inc(summed, 1)

        @block.vector
        def _(dve):
            nc.vector.memset(row_cols[:], 0.0).then_inc(cols_ready, 1)
            dve.wait_ge(cols_ready, 1)
            for t in range(NT):
                dve.wait_ge(cast, t + 1)
                nc.vector.tensor_copy(row_cols[:, t, 0:3], row_sum[:, t:t + 1].broadcast_to([P, 3])
                                      ).then_inc(cols_ready, 1)
                for g in range(2):
                    n = 2 * t + g
                    dve.wait_ge(flipped, n + 1)
                    nc.vector.tensor_copy(AT[:, 8 * g:8 * g + 8, t * P:(t + 1) * P],
                                          ps_T[:, n % 4, :].rearrange("p (k i) -> p k i", i=P)).then_inc(read, 1)
            dve.wait_ge(summed, 1)
            nc.vector.tensor_copy(deg_rows[:], ps_deg[:].rearrange("p c w -> p (c w)"))


def gated_steps(nc, A, AT, ST, halves, G, cparts, deg_rows, gate_bias, ident):
    with ExitStack() as ctx:
        def sb(n, shape, dt):
            return ctx.enter_context(nc.sbuf_tensor("gs_" + n, shape, dt))

        def sem(n):
            return ctx.enter_context(nc.semaphore("gs_" + n))

        msg = sb("msg", [P, 2 * DC, CW], F32)
        r = sb("r", [P, DC, CW], F32)
        z = sb("z", [P, DC, CW], F32)
        cand = sb("cand", [P, DC, CW], F32)
        ps_msg = ctx.enter_context(nc.psum_tensor("gs_ps_msg", [P, 2 * DC, CW], F32))
        ps_gate = ctx.enter_context(nc.psum_tensor("gs_ps_gate", [P, 2, CW], F32))
        ps_T = ctx.enter_context(nc.psum_tensor("gs_ps_T", [P, 2, CW], F32))
        summed = sem("summed")
        msg_ready = sem("msg_ready")
        gate_ready = sem("gate_ready")
        gate_read = sem("gate_read")
        rs_ready = sem("rs_ready")
        delta = sem("delta")
        passed_pe = sem("passed_pe")
        flipped = sem("flipped")
        hi_done = sem("hi_done")
        lo_done = sem("lo_done")
        block = ctx.enter_context(nc.Block())
        MB = 2 * DC
        GB = GATES * DC
        TB = NT // 2
        TC = TB // NC
        LATE = list(range(TB - TC, TB))
        EARLY = list(range(TB - TC))
        READY_TILES = 2 * len(EARLY)

        def steps(eng, chunk):
            with eng.Fori(0, STEPS) as s:
                chunk(s, 0, s * NC, True, False)
                with eng.Fori(1, NC - 1) as c:
                    chunk(s, c, s * NC + c, False, False)
                chunk(s, NC - 1, s * NC + (NC - 1), False, True)

        def turn(s, late, x):
            return TB * s + (x if late else len(LATE) + x)

        def columns(c):
            return slice(c * CW, (c + 1) * CW) if isinstance(c, int) else bass.ds(c * CW, CW)

        @block.tensor
        def _(pe):
            pe.sem_inc(gate_read, 2)
            pe.sem_inc(gate_ready, 1)

            def flip(s, banks, late):
                for x, b in enumerate(banks):
                    k = turn(s, late, x)
                    pe.wait_ge(lo_done, k + 1)
                    for i in range(2):
                        for fc in range(DC):
                            at, t = (i * DC + fc) * P, 2 * b + i
                            last = nc.tensor.transpose(ps_T[:, b % 2, at:at + P], ST[:, fc, t * P:(t + 1) * P],
                                                       ident[:])
                    last.then_inc(flipped, 1)

            def chunk(s, c, n, first, last_chunk):
                if first:
                    pe.wait_ge(lo_done, 2 + TB * s)
                pe.wait_ge(msg_ready, 1 + MB * n)
                for m in range(MB):
                    src, fc = (AT, A)[m // DC], m % DC
                    for t in range(NT):
                        if first and m == 0 and t == READY_TILES:
                            pe.wait_ge(delta, 1 + 3 * NC * s)
                            flip(s, LATE, True)
                            pe.wait_ge(lo_done, 2 + TB * s + len(LATE))
                        for half in range(2):
                            last = nc.tensor.matmul(ps_msg[:, m, :], halves[:, t, half, fc * P:(fc + 1) * P],
                                                    src[:, t, columns(c)], start=(t == 0 and half == 0),
                                                    stop=(t == NT - 1 and half == 1))
                    last.then_inc(summed, 1)
                for g in range(GATES):
                    if last_chunk and g == GATES - 1:
                        pe.wait_ge(delta, 1 + 3 * n)
                        flip(s, EARLY, False)
                    for oc in range(DC):
                        k = g * DC + oc
                        pe.wait_ge(gate_read, GB * n + k + 1)
                        pe.sem_inc(passed_pe, 1)
                        out = ps_gate[:, k % 2, :]
                        cols = slice(oc * P, (oc + 1) * P)
                        nc.tensor.matmul(out, cparts[:, g * D + oc * P:g * D + (oc + 1) * P],
                                         deg_rows[:, columns(c)], start=True, stop=False)
                        if g < 2:
                            for kc in range(DC):
                                nc.tensor.matmul(out, G[:, 2 * DC + kc, g, cols], ST[:, kc, columns(c)],
                                                 start=False, stop=False)
                        for m in range(MB):
                            pe.wait_ge(msg_ready, 1 + MB * n + m + 1)
                            last = nc.tensor.matmul(out, G[:, m, g, cols], msg[:, m, :], start=False,
                                                    stop=(g < 2 and m == MB - 1))
                        if g == 2:
                            pe.wait_ge(rs_ready, DC * (n + 1))
                            for kc in range(DC):
                                last = nc.tensor.matmul(out, G[:, 2 * DC + kc, g, cols], r[:, kc, :],
                                                        start=False, stop=(kc == DC - 1))
                        last.then_inc(gate_ready, 1)

            steps(pe, chunk)

        @block.scalar
        def _(act):
            act.sem_inc(msg_ready, 1)

            def high(s, banks, late):
                for x, b in enumerate(banks):
                    act.wait_ge(flipped, turn(s, late, x) + 1)
                    nc.scalar.activation(halves[:, 2 * b:2 * b + 2, 0, :],
                                         ps_T[:, b % 2, :].rearrange("p (k f) -> p k f", k=2), ACT.Copy,
                                         scale=STATE_SCALE).then_inc(hi_done, 1)

            def chunk(s, c, n, first, last_chunk):
                if first:
                    high(s, LATE, True)
                for m in range(MB):
                    act.wait_ge(summed, MB * n + m + 1)
                    if m == 0:
                        act.wait_ge(gate_ready, 1 + GB * n)
                    nc.scalar.activation(msg[:, m, :], ps_msg[:, m, :], ACT.Copy, scale=1.0 / STATE_SCALE
                                         ).then_inc(msg_ready, 1)
                act.wait_ge(delta, 1 + 3 * n)
                for g, (out, func) in enumerate(((r, ACT.Sigmoid), (z, ACT.Sigmoid), (cand, ACT.Tanh))):
                    if last_chunk and g == GATES - 1:
                        high(s, EARLY, False)
                    for oc in range(DC):
                        k = g * DC + oc
                        act.wait_ge(gate_ready, 1 + GB * n + k + 1)
                        nc.scalar.activation(out[:, oc, :], ps_gate[:, k % 2, :], func,
                                             bias=gate_bias[:, g, oc:oc + 1], scale=1.0).then_inc(gate_read, 1)

            steps(act, chunk)

        @block.vector
        def _(dve):
            dve.sem_inc(delta, 1)
            dve.sem_inc(lo_done, 2)

            def low_half(s, banks, late):
                for x, b in enumerate(banks):
                    dve.wait_ge(hi_done, turn(s, late, x) + 1)
                    nc.vector.scalar_tensor_tensor(halves[:, 2 * b:2 * b + 2, 1, :],
                                                   ps_T[:, b % 2, :].rearrange("p (k f) -> p k f", k=2), STATE_SCALE,
                                                   halves[:, 2 * b:2 * b + 2, 0, :], ALU.mult, ALU.subtract
                                                   ).then_inc(lo_done, 1)

            def chunk(s, c, n, first, last_chunk):
                if first:
                    low_half(s, LATE, True)
                st = ST[:, :, columns(c)]
                for oc in range(DC):
                    dve.wait_ge(gate_read, 2 + GB * n + oc + 1)
                    nc.vector.tensor_tensor(r[:, oc, :], r[:, oc, :], ST[:, oc, columns(c)], ALU.mult
                                            ).then_inc(rs_ready, 1)
                if last_chunk:
                    low_half(s, EARLY, False)
                dve.wait_ge(gate_read, 2 + GB * (n + 1))
                nc.vector.tensor_tensor(cand[:], cand[:], st, ALU.subtract).then_inc(delta, 1)
                dve.wait_ge(delta, 1 + 3 * n + 1)
                nc.vector.tensor_tensor(cand[:], cand[:], z[:], ALU.mult).then_inc(delta, 1)
                dve.wait_ge(delta, 1 + 3 * n + 2)
                nc.vector.tensor_tensor(st, st, cand[:], ALU.add).then_inc(delta, 1)

            steps(dve, chunk)


def feature_matmul(nc, name, YT, jobs, funcs):
    func, bias = funcs
    with ExitStack() as ctx:
        ps = ctx.enter_context(nc.psum_tensor(name + "ps", [P, 4, CW], F32))
        made = ctx.enter_context(nc.semaphore(name + "made"))
        read = ctx.enter_context(nc.semaphore(name + "read"))
        block = ctx.enter_context(nc.Block())
        banks = [(c, oc) for c in range(NC) for oc in range(DC)]

        @block.tensor
        def _(pe):
            for n, (c, oc) in enumerate(banks):
                if n >= 4:
                    pe.wait_ge(read, n - 3)
                for k, (W, XT) in enumerate(jobs):
                    for kc in range(DC):
                        last = nc.tensor.matmul(ps[:, n % 4, :], W[:, kc, oc * P:(oc + 1) * P],
                                                XT[:, kc, c * CW:(c + 1) * CW], start=(k == 0 and kc == 0),
                                                stop=(k == len(jobs) - 1 and kc == DC - 1))
                last.then_inc(made, 1)

        @block.scalar
        def _(act):
            for n, (c, oc) in enumerate(banks):
                act.wait_ge(made, n + 1)
                nc.scalar.activation(YT[:, oc, c * CW:(c + 1) * CW], ps[:, n % 4, :], func,
                                     bias=bias[:, oc:oc + 1], scale=1.0).then_inc(read, 1)


def add_residual(nc, name, X, YT, ident):
    with ExitStack() as ctx:
        ps = ctx.enter_context(nc.psum_tensor(name + "ps", [P, 4, 2, D], F32))
        flipped = ctx.enter_context(nc.semaphore(name + "flipped"))
        read = ctx.enter_context(nc.semaphore(name + "read"))
        block = ctx.enter_context(nc.Block())

        @block.tensor
        def _(pe):
            for n in range(NT // 2):
                if n >= 4:
                    pe.wait_ge(read, n - 3)
                for k in range(2):
                    t = 2 * n + k
                    for fc in range(DC):
                        last = nc.tensor.transpose(ps[:, n % 4, k, fc * P:(fc + 1) * P],
                                                   YT[:, fc, t * P:(t + 1) * P], ident[:])
                last.then_inc(flipped, 1)

        @block.vector
        def _(dve):
            for n in range(NT // 2):
                dve.wait_ge(flipped, n + 1)
                nc.vector.tensor_tensor(X[:, 2 * n:2 * n + 2, :], ps[:, n % 4], X[:, 2 * n:2 * n + 2, :], ALU.add
                                        ).then_inc(read, 1)


def mean_neighbours(nc, AT, halves, agg, ones16):
    with ExitStack() as ctx:
        rdeg = ctx.enter_context(nc.sbuf_tensor("mn_rdeg", [P, 2, CW], F32))
        top = ctx.enter_context(nc.sbuf_tensor("mn_top", [P, 2, CW], F32))
        ps = ctx.enter_context(nc.psum_tensor("mn_ps", [P, 2, 3, CW], F32))
        made = ctx.enter_context(nc.semaphore("mn_made"))
        read = ctx.enter_context(nc.semaphore("mn_read"))
        chain = ctx.enter_context(nc.semaphore("mn_chain"))
        block = ctx.enter_context(nc.Block())

        @block.tensor
        def _(pe):
            for c in range(NC):
                if c >= 2:
                    pe.wait_ge(read, 2 * (c - 1))
                cols = slice(c * CW, (c + 1) * CW)
                for t in range(NT):
                    last = nc.tensor.matmul(ps[:, c % 2, 2, :], ones16[:], AT[:, t, cols], start=(t == 0),
                                            stop=(t == NT - 1))
                last.then_inc(made, 1)
                for fc in range(DC):
                    for t in range(NT):
                        for half in range(2):
                            last = nc.tensor.matmul(ps[:, c % 2, fc, :], halves[:, t, half, fc * P:(fc + 1) * P],
                                                    AT[:, t, cols], start=(t == 0 and half == 0),
                                                    stop=(t == NT - 1 and half == 1))
                    last.then_inc(made, 1)

        @block.vector
        def _(dve):
            for c in range(NC):
                dve.wait_ge(made, 3 * c + 1)
                nc.vector.tensor_scalar(top[:, c % 2, :], ps[:, c % 2, 2, :], 1.0, STATE_SCALE, ALU.max, ALU.mult
                                        ).then_inc(chain, 1)
                dve.wait_ge(chain, 2 * c + 1)
                nc.vector.reciprocal(rdeg[:, c % 2, :], top[:, c % 2, :]).then_inc(chain, 1)
                dve.wait_ge(chain, 2 * c + 2)
                for fc in range(DC):
                    dve.wait_ge(made, 3 * c + 2 + fc)
                    nc.vector.tensor_tensor(agg[:, fc, c * CW:(c + 1) * CW], ps[:, c % 2, fc, :], rdeg[:, c % 2, :],
                                            ALU.mult).then_inc(read, 1)


def mean_weights(nc, srcs, Wx, Wa, bias, ident):
    W_selfT, b_self, W_nbT, b_nb, W_comb, b_comb = srcs
    with ExitStack() as ctx:
        def sb(n, shape, dt):
            return ctx.enter_context(nc.sbuf_tensor("mw_" + n, shape, dt))

        WT = [sb("WT0", [P, DC, D], F32), sb("WT1", [P, DC, D], F32)]
        C = sb("C", [P, 2 * DC, D], F32)
        b = sb("b", [P, 2, DC], F32)
        bc = sb("bc", [P, DC], F32)
        ps = ctx.enter_context(nc.psum_tensor("mw_ps", [P, 2, DC, D], F32))
        psb = ctx.enter_context(nc.psum_tensor("mw_psb", [P, DC], F32))
        landed = ctx.enter_context(nc.semaphore("mw_landed"))
        made = ctx.enter_context(nc.semaphore("mw_made"))
        block = ctx.enter_context(nc.Block())

        @block.sync
        def _(sp):
            for s, (w, bb) in enumerate(((W_selfT, b_self), (W_nbT, b_nb))):
                sp.dma_start(WT[s][:], w.rearrange("(c p) f -> p c f", p=P)).then_inc(landed, 16)
                sp.dma_start(b[:, s, :], bb).then_inc(landed, 16)
            sp.dma_start(C[:], W_comb.rearrange("(c p) f -> p c f", p=P)).then_inc(landed, 16)
            sp.dma_start(bc[:], b_comb).then_inc(landed, 16)

        @block.tensor
        def _(pe):
            pe.wait_ge(landed, 16 * 6)
            for s in range(2):
                for fc in range(DC):
                    for kc in range(DC):
                        nc.tensor.matmul(ps[:, s, fc, :], WT[s][:, kc, fc * P:(fc + 1) * P], C[:, s * DC + kc, :],
                                         start=(kc == 0), stop=(kc == DC - 1))
            for oc in range(DC):
                for s in range(2):
                    for kc in range(DC):
                        last = nc.tensor.matmul(psb[:, oc:oc + 1], C[:, s * DC + kc, oc * P:(oc + 1) * P],
                                                b[:, s, kc:kc + 1], start=(s == 0 and kc == 0),
                                                stop=(s == 1 and kc == DC - 1))
            last.then_inc(made, 1)

        @block.vector
        def _(dve):
            dve.wait_ge(made, 1)
            nc.vector.tensor_copy(Wx[:], ps[:, 0])
            nc.vector.tensor_copy(Wa[:], ps[:, 1])
            dve.wait_ge(landed, 16 * 6)
            nc.vector.tensor_tensor(bias[:], psb[:], bc[:], ALU.add)


def hard_inputs(nc, XT, WQT, WKT, WVT, we, be, qs, ks, vs, score_bias, q_scale, k_scale, v_scale):
    SCALING = float(HD) ** -0.5
    with ExitStack() as ctx:
        def sb(n, shape, dt):
            return ctx.enter_context(nc.sbuf_tensor("hi_" + n, shape, dt))

        def sem(n):
            return ctx.enter_context(nc.semaphore("hi_" + n))

        W = [sb(f"W{n}", [P, DC, D], F32) for n in range(3)]
        full = [sb(f"full{n}", [P, DC, N], F32) for n in range(2)]
        hi = [sb(f"hi{n}", [P, DC, N], F16) for n in range(2)]
        lo = [sb(f"lo{n}", [P, DC, N], F16) for n in range(2)]
        we_col = sb("we_col", [P, 2], F32)
        zero = sb("zero", [P, 1], F32)
        be_raw = sb("be_raw", [P, 1], F32)
        ps = ctx.enter_context(nc.psum_tensor("hi_ps", [P, 4, CW], F32))
        psv = ctx.enter_context(nc.psum_tensor("hi_psv", [P, 2, CW], F32))
        landed = sem("landed")
        consts = sem("consts")
        made = sem("made")
        read = sem("read")
        hi_done = [sem("hi_done"), 0]
        halves_done = sem("halves_done")
        stacked = sem("stacked")
        vmade = sem("vmade")
        vread = sem("vread")
        block = ctx.enter_context(nc.Block())
        banks = [(n, c, oc) for n in (1, 0) for c in range(NC) for oc in range(DC)]
        LOADS = 3 + 5

        @block.sync
        def _(sp):
            for n, w in enumerate((WQT, WKT, WVT)):
                sp.dma_start(W[n][:], w.rearrange("(c p) f -> p c f", p=P)).then_inc(landed, 16)
            for g in range(4):
                sp.dma_start(we_col[g * HD:(g + 1) * HD, 0:1], we).then_inc(landed, 16)
            sp.dma_start(be_raw[:], be.rearrange("(o d) -> o d", o=1).broadcast_to([P, 1])).then_inc(landed, 16)
            total = 0
            for m, (n, stack, order) in enumerate(((1, ks, K_ORDER), (0, qs, Q_ORDER))):
                sp.wait_ge(halves_done, m + 1)
                total += stack_halves(sp, stack, hi[n], lo[n], order, range(HG), stacked)
            sp.wait_ge(stacked, total)

        @block.tensor
        def _(pe):
            pe.wait_ge(landed, 16 * LOADS)
            for m, (n, c, oc) in enumerate(banks):
                if m >= 4:
                    pe.wait_ge(read, m - 3)
                for kc in range(DC):
                    last = nc.tensor.matmul(ps[:, m % 4, :], W[n][:, kc, oc * P:(oc + 1) * P],
                                            XT[:, kc, c * CW:(c + 1) * CW], start=(kc == 0), stop=(kc == DC - 1))
                last.then_inc(made, 1)
            for t in range(NT):
                if t >= 2:
                    pe.wait_ge(vread, t - 1)
                for kc in range(DC):
                    last = nc.tensor.matmul(psv[:, t % 2, 0:D], XT[:, kc, t * P:(t + 1) * P], W[2][:, kc, :],
                                            start=(kc == 0), stop=(kc == DC - 1))
                last.then_inc(vmade, 1)

        @block.scalar
        def _(act):
            act.wait_ge(consts, 1)
            for m, (n, c, oc) in enumerate(banks):
                act.wait_ge(made, m + 1)
                nc.scalar.activation(full[n][:, oc, c * CW:(c + 1) * CW], ps[:, m % 4, :], ACT.Identity,
                                     bias=(zero[:] if n == 0 else we_col[:, 1:2]),
                                     scale=(q_scale if n == 0 else SCALING * k_scale)).then_inc(read, 1)

        @block.vector
        def _(dve):
            dve.wait_ge(landed, 16 * LOADS)
            nc.vector.memset(zero[:], 0.0)
            nc.vector.tensor_scalar(score_bias[:], be_raw[:], q_scale * k_scale, None, ALU.mult)
            nc.vector.tensor_scalar(we_col[:, 1:2], we_col[:, 0:1], k_scale, None, ALU.mult).then_inc(consts, 1)
            for m, n in enumerate((1, 0)):
                dve.wait_ge(read, (m + 1) * NC * DC)
                split_halves(nc, dve, hi[n][:], lo[n][:], full[n][:], 1.0, hi_done).then_inc(halves_done, 1)
            for t in range(NT):
                dve.wait_ge(vmade, t + 1)
                pv = psv[:, t % 2, 0:D].rearrange("p (h d) -> p h d", h=H)
                split_halves(nc, dve, vs[:, t, :, 0:HD], vs[:, t, :, HD:2 * HD], pv, v_scale, hi_done
                             ).then_inc(vread, 1)


def move(nc, name, pairs):
    with ExitStack() as ctx:
        moved = ctx.enter_context(nc.semaphore(name + "moved"))
        block = ctx.enter_context(nc.Block())

        @block.sync
        def _(sp):
            for dst, src in pairs:
                sp.dma_start(dst, src).then_inc(moved, 16)
            sp.wait_ge(moved, 16 * len(pairs))


def resnorm_kernel(nc, ins, out, spill, dbg=None, upto=99):
    rows = "(t p) d -> p t d"
    ctx = ExitStack()
    with ctx:
        def sb(scope, name, shape, dt):
            return scope.enter_context(nc.sbuf_tensor(name, shape, dt))

        def dump(tile, k):
            if dbg is not None and k in dbg:
                move(nc, f"dbg{k}", [(dbg[k], tile)])

        ident = sb(ctx, "ident", [P, P], F32)
        ident16 = sb(ctx, "ident16", [P, P], F16)
        ones16 = sb(ctx, "ones16", [P, P], F16)
        ones_sel = sb(ctx, "ones_sel", [P, 2, 6], F16)
        sel = sb(ctx, "sel", [6, 3], F32)
        move(nc, "consts", [(ident[:], ins["c_ident"]), (ident16[:], ins["c_ident16"]), (ones16[:], ins["c_ones"]),
                            (ones_sel[:], ins["c_ones_sel"]), (sel[:], ins["c_sel"])])

        early = ctx.enter_context(ExitStack())
        G = sb(early, "G", [P, 3 * DC, GATES, D], F32)
        cparts = sb(early, "cparts", [6, GATES * D], BF16)
        gate_bias = sb(early, "gate_bias", [P, GATES, DC], F32)

        IN_SCALE = 16.0
        with ExitStack() as att:
            X = sb(att, "X0", [P, NT, D], F32)
            qs = sb(att, "qs0", [P, H, N], F16)
            ks = sb(att, "ks0", [P, H, N], F16)
            vs = sb(att, "vs0", [P, NT, H, 2 * HD], F16)
            soft_inputs(nc, ins, (G, cparts, gate_bias, sel), qs, ks, vs, X, IN_SCALE)
            masked_attention(nc, "a0_", qs, ks, vs, X, ins["adj"], False, float(HD) ** -0.5 / IN_SCALE ** 2,
                             1.0 / IN_SCALE, None)
            layer_norm(nc, "n0_", X)
            move(nc, "sp0", [(spill.rearrange(rows, p=P), X[:])])
        if upto == 0:
            with ExitStack() as e:
                X = sb(e, "Xd", [P, NT, D], F32)
                move(nc, "d0", [(X[:], spill.rearrange(rows, p=P))])
                move(nc, "d1", [(out.rearrange(rows, p=P), X[:])])
            return

        with ExitStack() as graph:
            AT = sb(graph, "AT", [P, NT, N], F16)
            halves = sb(graph, "halves", [P, NT, 2, D], F16)
            ST = sb(graph, "ST", [P, DC, N], F32)
            YT = None
            with ExitStack() as gated:
                A = sb(gated, "A", [P, NT, N], F16)
                deg_rows = sb(gated, "deg_rows", [6, N], F16)
                with ExitStack() as first:
                    X = sb(first, "X1", [P, NT, D], F32)
                    move(nc, "ld0", [(X[:], spill.rearrange(rows, p=P))])
                    to_features(nc, "f1_", X, ST, halves, ident)
                build_adjacency(nc, ins["adj"], A, AT, deg_rows, ones_sel, ident16)
                gated_steps(nc, A, AT, ST, halves, G, cparts, deg_rows, gate_bias, ident)
            X = sb(graph, "X2", [P, NT, D], F32)
            with ExitStack() as read_out:
                o1 = sb(read_out, "o1", [P, DC, D], F32)
                o2 = sb(read_out, "o2", [P, DC, D], F32)
                ob = sb(read_out, "ob", [P, 2, DC], F32)
                HT = sb(read_out, "HT", [P, DC, N], F32)
                move(nc, "ld1", [(o1[:], ins["o1T"].rearrange("(c p) f -> p c f", p=P)),
                                 (o2[:], ins["o2T"].rearrange("(c p) f -> p c f", p=P)),
                                 (ob[:, 0, :], ins["L1_gnn_o1_b"]),
                                 (ob[:, 1, :], ins["L1_gnn_o2_b"]),
                                 (X[:], spill.rearrange(rows, p=P))])
                feature_matmul(nc, "r1_", HT, [(o1, ST)], (ACT.Tanh, ob[:, 0, :]))
                feature_matmul(nc, "r2_", ST, [(o2, HT)], (ACT.Identity, ob[:, 1, :]))
                add_residual(nc, "r3_", X, ST, ident)
            layer_norm(nc, "n1_", X)
            if upto == 1:
                move(nc, "d1", [(out.rearrange(rows, p=P), X[:])])
                return
            to_features(nc, "f2_", X, ST, halves, ident)
            with ExitStack() as mean:
                agg = sb(mean, "agg", [P, DC, N], F32)
                YT = sb(mean, "YT", [P, DC, N], F32)
                Wx = sb(mean, "Wx", [P, DC, D], F32)
                Wa = sb(mean, "Wa", [P, DC, D], F32)
                mb = sb(mean, "mb", [P, DC], F32)
                mean_weights(nc, (ins["WselfT"], ins["L2_gnn_b_self"], ins["WnbT"], ins["L2_gnn_b_nb"],
                                  ins["L2_gnn_W_comb"], ins["L2_gnn_b_comb"]), Wx, Wa, mb, ident)
                mean_neighbours(nc, AT, halves, agg, ones16)
                feature_matmul(nc, "m1_", YT, [(Wx, ST), (Wa, agg)], (ACT.Relu, mb))
                add_residual(nc, "m2_", X, YT, ident)
            layer_norm(nc, "n2_", X)
            move(nc, "sp1", [((out if upto == 2 else spill).rearrange(rows, p=P), X[:])])
            if upto == 2:
                return

        early.close()

        Q_SCALE, K_SCALE, V_SCALE = 64.0, 256.0, 64.0
        with ExitStack() as att:
            X = sb(att, "X3", [P, NT, D], F32)
            qs = sb(att, "qs3", [P, H, N], F16)
            ks = sb(att, "ks3", [P, H, N], F16)
            vs = sb(att, "vs3", [P, NT, H, 2 * HD], F16)
            score_bias = sb(att, "score_bias", [P, 1], F32)
            move(nc, "ld2", [(X[:], spill.rearrange(rows, p=P))])
            with ExitStack() as proj:
                XT = sb(proj, "XT", [P, DC, N], F32)
                to_features(nc, "f3_", X, XT, None, ident)
                hard_inputs(nc, XT, ins["WQT"], ins["WKT"], ins["WVT"], ins["L3_gnn_we"], ins["L3_gnn_be"],
                            qs, ks, vs, score_bias, Q_SCALE, K_SCALE, V_SCALE)
            masked_attention(nc, "a3_", qs, ks, vs, X, ins["adj"], True, 2.0 ** 66, 1.0 / (V_SCALE * H), score_bias[:])
            layer_norm(nc, "n3_", X)
            move(nc, "fin", [(out.rearrange(rows, p=P), X[:])])


_T = {"xT": "x", "x2T": "L0_gnn_x2", "rWT": "L1_gnn_r_W", "zWT": "L1_gnn_z_W", "hWT": "L1_gnn_h_W",
      "o1T": "L1_gnn_o1_W", "o2T": "L1_gnn_o2_W", "WselfT": "L2_gnn_W_self", "WnbT": "L2_gnn_W_nb",
      "WQT": "L3_gnn_WQ", "WKT": "L3_gnn_WK", "WVT": "L3_gnn_WV"}
_PLAIN = ["x", "adj", "L0_gnn_v", "L1_gnn_in_W", "L1_gnn_in_b", "L1_gnn_out_W", "L1_gnn_out_b", "L1_gnn_r_b",
          "L1_gnn_z_b", "L1_gnn_h_b", "L1_gnn_o1_b", "L1_gnn_o2_b", "L2_gnn_b_self", "L2_gnn_b_nb",
          "L2_gnn_W_comb", "L2_gnn_b_comb", "L3_gnn_we", "L3_gnn_be"]


def kernel(**inputs):
    import numpy as _np
    import concourse.bacc as _bacc
    from concourse import mybir as _mybir
    from concourse.bass_utils import run_bass_kernel_spmd as _run

    host = {n: _np.ascontiguousarray(_np.asarray(inputs[n])) for n in _PLAIN}
    host.update({n: _np.ascontiguousarray(_np.asarray(inputs[s]).T) for n, s in _T.items()})
    for n, a in host.items():
        if a.shape == (256,):
            host[n] = _np.ascontiguousarray(a.reshape(2, 128).T)
    host["L3_gnn_we"] = host["L3_gnn_we"].reshape(32, 1)
    host["c_ident"] = _np.eye(128, dtype=_np.float32)
    host["c_ident16"] = _np.eye(128, dtype=_np.float16)
    host["c_ones"] = _np.ones((128, 128), _np.float16)
    ones_sel = _np.zeros((128, 2, 6), _np.float16)
    ones_sel[:, 0, 0:3] = 1
    ones_sel[:, 1, 3:6] = 1
    host["c_ones_sel"] = ones_sel
    host["c_sel"] = _np.concatenate([_np.eye(3, dtype=_np.float32)] * 2)

    nc = _bacc.Bacc("TRN2", target_bir_lowering=False, num_devices=1)
    arrays, args = {}, {}
    for n, a in host.items():
        arrays[f"in_{n}_dram"] = a
        args[n] = nc.dram_tensor(f"in_{n}_dram", a.shape, _mybir.dt.from_np(a.dtype), kind="ExternalInput").ap()
    out = nc.dram_tensor("out_0_dram", (2048, 256), _mybir.dt.float32, kind="ExternalOutput").ap()
    spill = nc.dram_tensor("spill_dram", (2048, 256), _mybir.dt.float32, kind="Internal").ap()
    resnorm_kernel(nc, args, out, spill)
    r = _run(nc, [arrays], core_ids=[0])
    return r.results[0]["out_0_dram"]
```

```python
from contextlib import ExitStack

import concourse.bass as bass
from concourse import mybir

ALU = mybir.AluOpType
ACT = mybir.ActivationFunctionType
F32 = mybir.dt.float32
F16 = mybir.dt.float16
BF16 = mybir.dt.bfloat16
I32 = mybir.dt.int32
AX_X = mybir.AxisListType.X

P = 128
N = 2048
D = 256
H = 8
HD = D // H
NT = N // P
DC = D // P
CW = 512
NC = N // CW
STEPS = 5
GATES = 3
EPS = 1e-5
BIG = 2.0 ** 100
STATE_SCALE = 1024.0


def split_halves(nc, eng, hi, lo, src, scale, hi_done):
    nc.vector.tensor_scalar(hi, src, scale, None, ALU.mult).then_inc(hi_done[0], 1)
    hi_done[1] += 1
    eng.wait_ge(hi_done[0], hi_done[1])
    return nc.vector.scalar_tensor_tensor(lo, src, scale, hi, ALU.mult, ALU.subtract)


HG = P // HD


def stack_head(queue, h, stack, hi, lo, order, done):
    fc, r = divmod(h, HG)
    for g, half in enumerate(order):
        queue.dma_start(stack[g * HD:(g + 1) * HD, h, :],
                        (hi, lo)[half][r * HD:(r + 1) * HD, fc, :]).then_inc(done, 16)
    return 16 * len(order)


def stack_heads(queue, r, stack, hi, lo, order, done):
    for g, half in enumerate(order):
        queue.dma_start(stack[g * HD:(g + 1) * HD, r::HG, :],
                        (hi, lo)[half][r * HD:(r + 1) * HD, :, :]).then_inc(done, 16)
    return 16 * len(order)


Q_ORDER = (0, 0, 1, 1)
K_ORDER = (0, 1, 0, 1)


def masked_attention(nc, name, qs, ks, vs, X, adj_in, adj, hard, scale, out_scale, score_bias,
                     ident, hot=None, stacks=(), x_rows=None, beside=()):
    adj_tiles = adj.rearrange("(t p) n -> t p n", p=P)
    PAIRS = NT // 2
    UNITS = 2 * H
    LAST = PAIRS - 1
    TW = 1024 if hard else 512
    TC = N // TW
    STACKED = 2
    SC = 2
    SW = N // SC
    NB = 4
    CREDIT = 2 * SC * H
    BANKS = [0, 1] if hard else [0, 1, 2, 0, 1, 2, 0, 2]
    EARLY = 2 if hard else 3
    OB = 2 if hard else 1
    low = -2.0 ** 60 if hard else -BIG
    PT = F16 if hard else F32
    with ExitStack() as ctx:
        def sb(n, shape, dt):
            return ctx.enter_context(nc.sbuf_tensor(name + n, shape, dt))

        def sem(n):
            return ctx.enter_context(nc.semaphore(name + n))

        mask = sb("mask", [P, 2, N], F32)
        S = sb("S", [P, NB, N], F32)
        pt_hi = sb("pt_hi", [P, 2, N], F16)
        pt_lo = None if hard else sb("pt_lo", [P, 2, N], F16)
        mn = sb("mn", [P, NB, SC], F32)
        sums = sb("sums", [P, 2, H], F32)
        rinv = sb("rinv", [P, 2, H], F32)
        o_low = sb("o_low", [P, 2, H, HD], F32)
        o_sum = sb("o_sum", [P, 2, H, HD], F32)
        pt_full = None if hard else sb("pt_full", [P, 2, TW], F32)
        ps_S = ctx.enter_context(nc.psum_tensor(name + "psS", [P, SC, SW], F32))
        ps_T = ctx.enter_context(nc.psum_tensor(name + "psT", [P, max(BANKS) + 1, TW], PT))
        ps_O = ctx.enter_context(nc.psum_tensor(name + "psO", [P, OB, H, 2 * HD], F32))

        adj_landed = [sem(f"adj_landed{b}") for b in range(2)]
        adj_used = sem("adj_used")
        scores_ready = sem("scores_ready")
        masked = sem("masked")
        probs_ready = sem("probs_ready")
        transposed = sem("transposed")
        hi_ready = sem("hi_ready")
        last_used = sem("last_used")
        banks_used = sem("banks_used")
        pool_low = sem("pool_low")
        half_read = [sem(f"half_read{c}") for c in range(2)]
        pv_done = sem("pv_done")
        olow_ready = sem("olow_ready")
        o_used = sem("o_used")
        unbiased = sem("unbiased") if hard else None
        first_mask = sem("first_mask")
        stack_landed = [sem(f"stack_landed{h}") for h in range(STACKED, H)] if stacks else []
        x_landed = sem("x_landed") if x_rows is not None else None
        beside_landed = sem("beside_landed") if beside else None
        passed_dve = sem("passed_dve")
        passed_pool = sem("passed_pool")
        tail = sem("tail")

        block = ctx.enter_context(nc.Block())

        def spot(i, j):
            return UNITS * i + j, j, j % H, 2 * i + j // H

        def bank(b, c):
            n = (TC * b + c) % len(BANKS)
            back = next(d for d in range(1, len(BANKS) + 1) if BANKS[(n - d) % len(BANKS)] == BANKS[n])
            return BANKS[n], back

        def bank_free(pe, i, j, c):
            u, b = spot(i, j)[:2]
            back = bank(b, c)[1]
            if hard:
                pe.wait_ge(half_read[c], u + 1)
                return
            units, user = divmod(c - back, TC)
            if user == TC - 1:
                pe.wait_ge(last_used, 2 + u + units + 1)
            else:
                pe.wait_ge(banks_used, (TC - 1) * (2 + u + units) + user + 1)

        def valid(i, j):
            return not isinstance(i, int) or UNITS * i + j < UNITS * PAIRS

        def run(eng, prologue, slot):
            prologue()
            slot(0, 0)
            slot(0, 1)
            with eng.Fori(0, LAST) as i:
                for j in range(2, UNITS + 2):
                    slot(i, j)
            for j in range(2, UNITS + 2):
                slot(LAST, j)

        def previous(i, j, n):
            return not isinstance(i, int) or 0 <= UNITS * i + j - n < UNITS * PAIRS

        @block.sync
        def _(sp):
            if not stacks:
                sp.dma_start(adj_in[:, 1, :], adj_tiles[1]).then_inc(adj_landed[1], 16)
            else:
                for h in range(STACKED, H):
                    for stack in stacks:
                        stack_head(sp, h, *stack, stack_landed[h - STACKED])
                    if h == STACKED:
                        sp.dma_start(adj_in[:, 1, :], adj_tiles[1]).then_inc(adj_landed[1], 16)
            if x_rows is not None:
                for landed in stack_landed:
                    sp.wait_ge(landed, 16 * 4 * len(stacks))
                sp.dma_start(X[:], x_rows).then_inc(x_landed, 16)
                for dst, src in beside:
                    sp.dma_start(dst, src).then_inc(beside_landed, 16)
            with sp.Fori(1, PAIRS) as i:
                for b in range(2):
                    sp.wait_ge(adj_used, 2 * i + b - 1)
                    sp.dma_start(adj_in[:, b, :],
                                 adj_tiles[bass.ds(2 * i + b, 1)].rearrange("o p n -> (o p) n")
                                 ).then_inc(adj_landed[b], 16)
            if beside:
                sp.wait_ge(beside_landed, 16 * len(beside))

        @block.gpsimd
        def _(pool):
            if hard:
                def make_mask(i, b):
                    pool.wait_ge(adj_landed[b], 16 * (i + b))
                    pool.wait_ge(masked, CREDIT + SC * H * (2 * i + b - 1))
                    pool.sem_inc(passed_pool, 1)
                    nc.gpsimd.tensor_scalar(mask[:, b, :], adj_in[:, b, :], 0.0, low, ALU.is_le, ALU.mult
                                            ).then_inc(unbiased, 1)
                    pool.wait_ge(unbiased, 2 * i + b + 1)
                    pool.sem_inc(passed_pool, 1)
                    nc.gpsimd.tensor_scalar(mask[:, b, :], mask[:, b, :], score_bias, None, ALU.add
                                            ).then_inc(adj_used, 1)

                pool.wait_ge(first_mask, 1)
                pool.sem_inc(adj_used, 1)
                make_mask(0, 1)
                with pool.Fori(1, PAIRS) as i:
                    for b in range(2):
                        make_mask(i, b)
            else:
                PARTS = 4
                MW = N // PARTS

                def low_last(i, j):
                    u, b, h, q = spot(i, j)
                    pool.wait_ge(last_used, 2 + u + 1)
                    nc.gpsimd.tensor_tensor(pt_lo[:, b % 2, N - TW:N], pt_full[:, b % 2, :], pt_hi[:, b % 2, N - TW:N],
                                            ALU.subtract).then_inc(pool_low, 1)

                def mask_part(i, j):
                    u, b, h, q = spot(i, j)
                    at = (j // H + 1) % 2
                    cols = slice(h * MW, (h + 1) * MW)
                    if h == 0:
                        pool.wait_ge(adj_landed[at], 16 * (i + 1))
                        pool.wait_ge(masked, CREDIT + SC * H * q)
                        pool.sem_inc(passed_pool, 1)
                    part = nc.gpsimd.tensor_scalar(mask[:, at, cols], adj_in[:, at, cols], 0.0, low, ALU.is_le,
                                                   ALU.mult)
                    if h == PARTS - 1:
                        part.then_inc(adj_used, 1)

                def pair(i, last):
                    for j in range(UNITS):
                        low_last(i, j)
                        if j % H < PARTS and not (last and j >= H):
                            mask_part(i, j)

                pool.sem_inc(pool_low, 2)
                pool.wait_ge(first_mask, 1)
                pool.sem_inc(adj_used, 1)
                pair(0, False)
                with pool.Fori(1, LAST) as i:
                    pair(i, False)
                pair(LAST, True)

        @block.tensor
        def _(pe):
            def scores(i, j, chunks):
                u, b, h, q = spot(i, j)
                if stacks and STACKED <= j < H and chunks[0] == 0 and (not isinstance(i, int) or i == 0):
                    pe.wait_ge(stack_landed[h - STACKED], 16 * 4 * len(stacks))
                for c in chunks:
                    pe.wait_ge(masked, CREDIT - SC + SC * u + c + 1)
                    for k in range(SW // CW):
                        col = c * SW + k * CW
                        last = nc.tensor.matmul(ps_S[:, c, k * CW:(k + 1) * CW],
                                                qs[:, h, bass.ds(q * P, P)] if not isinstance(q, int)
                                                else qs[:, h, q * P:(q + 1) * P],
                                                ks[:, h, col:col + CW], start=True, stop=True)
                    last.then_inc(scores_ready, 1)

            def flip(i, j, c):
                u, b, h, q = spot(i, j)
                src = hot[:, b % NB, :] if hard else S[:, b % NB, :]
                at, back = bank(b, c)
                pe.wait_ge(probs_ready, (NB if hard else 0) + u + 1)
                bank_free(pe, i, j, c)
                for k in range(TW // P):
                    last = nc.tensor.transpose(ps_T[:, at, k * P:(k + 1) * P],
                                               src[:, c * TW + k * P:c * TW + (k + 1) * P], ident[:])
                last.then_inc(transposed, 1)

            def weigh(i, j):
                u, b, h, q = spot(i, j)
                if hard:
                    for c in range(TC):
                        pe.wait_ge(half_read[c], u + 2)
                else:
                    pe.wait_ge(banks_used, (TC - 1) * (2 + u + 1))
                    pe.wait_ge(pool_low, 2 + u + 1)
                if h == 0:
                    pe.wait_ge(o_used, q + 1)
                halves = [pt_hi] if hard else [pt_hi, pt_lo]
                for t in range(NT):
                    for half in halves:
                        last = nc.tensor.matmul(ps_O[:, (j // H) % OB, h, :], half[:, b % 2, t * P:(t + 1) * P],
                                                vs[:, t, h, :], start=(t == 0 and half is pt_hi),
                                                stop=(t == NT - 1 and half is halves[-1]))
                last.then_inc(pv_done, 1)

            def slot(i, j):
                if valid(i, j):
                    for c in range(EARLY):
                        flip(i, j, c)
                if valid(i, j + 2):
                    scores(i, j + 2, [1])
                if previous(i, j, 1):
                    weigh(i, j - 1)
                if valid(i, j):
                    for c in range(EARLY, TC):
                        flip(i, j, c)
                if valid(i, j + 3):
                    scores(i, j + 3, [0])

            def prologue():
                pe.sem_inc(transposed, NB * TC)
                pe.sem_inc(pv_done, 2)
                for j in range(2):
                    scores(0, j, [0, 1])
                scores(0, 2, [0])

            run(pe, prologue, slot)

        @block.scalar
        def _(act):
            def exponent(i, j):
                u, b, h, q = spot(i, j)
                at = b % NB
                act.wait_ge(masked, CREDIT + SC * (u + 1))
                if hard:
                    act.wait_ge(transposed, TC * (u + 1))
                    nc.scalar.activation(hot[:, at, :], S[:, at, :], ACT.Exp, bias=mn[:, at, 1:2],
                                         scale=-1.0).then_inc(probs_ready, 1)
                else:
                    nc.scalar.activation(S[:, at, :], S[:, at, :], ACT.Exp, bias=mn[:, at, 1:2], scale=-1.0,
                                         accum_out=sums[:, (j // H) % 2, h:h + 1]).then_inc(probs_ready, 1)

            def high(i, j, c):
                u, b, h, q = spot(i, j)
                act.wait_ge(transposed, NB * TC + TC * u + c + 1)
                if c == 0:
                    act.wait_ge(pv_done, u + 1)
                nc.scalar.activation(pt_hi[:, b % 2, c * TW:(c + 1) * TW], ps_T[:, bank(b, c)[0], :], ACT.Copy
                                     ).then_inc(half_read[c] if hard else hi_ready, 1)

            def copy_last(i, j):
                u, b, h, q = spot(i, j)
                act.wait_ge(pool_low, u + 1)
                nc.scalar.activation(pt_full[:, b % 2, :], ps_T[:, bank(b, TC - 1)[0], :], ACT.Copy
                                     ).then_inc(last_used, 1)

            def low_out(i, j):
                u, b, h, q = spot(i, j)
                act.wait_ge(pv_done, 2 + u + 1)
                nc.scalar.activation(o_low[:, (j // H) % 2, :, :], ps_O[:, (j // H) % OB, :, HD:2 * HD], ACT.Copy
                                     ).then_inc(olow_ready, 1)

            def slot(i, j):
                if not hard and valid(i, j):
                    for c in range(TC - 1):
                        high(i, j, c)
                if valid(i, j + 1):
                    exponent(i, j + 1)
                if valid(i, j):
                    high(i, j, 0 if hard else TC - 1)
                    if not hard:
                        copy_last(i, j)
                if previous(i, j, 1) and (j - 1) % H == H - 1:
                    low_out(i, j - 1)

            def prologue():
                if hard:
                    act.sem_inc(half_read[0], 1)
                    act.sem_inc(probs_ready, NB)
                else:
                    act.sem_inc(last_used, 2)
                exponent(0, 0)

            run(act, prologue, slot)

        @block.vector
        def _(dve):
            def mask_chunk(i, j, c):
                u, b, h, q = spot(i, j)
                if h == 0 and c == 0:
                    dve.wait_ge(adj_used, q + 1)
                if c == 0:
                    if hard:
                        dve.wait_ge(probs_ready, u + 1)
                    else:
                        dve.wait_ge(transposed, TC * (u + 1))
                if c:
                    dve.wait_ge(masked, CREDIT + SC * u + c)
                dve.wait_ge(scores_ready, SC * u + c + 1)
                dve.sem_inc(passed_dve, 1)
                cols = slice(c * SW, (c + 1) * SW)
                nc.vector.tensor_tensor_reduce(S[:, b % NB, cols], ps_S[:, c, :], mask[:, (j // H) % 2, cols], -scale,
                                               mn[:, b % NB, 0:1] if c else -scale * low / 2 if hard else 3.0e38,
                                               ALU.add, ALU.min, accum_out=mn[:, b % NB, c:c + 1]).then_inc(masked, 1)

            def take_half(i, j):
                u, b, h, q = spot(i, j)
                dve.wait_ge(transposed, NB * TC + TC * (u + 1))
                dve.wait_ge(pv_done, u + 1)
                nc.vector.tensor_copy(pt_hi[:, b % 2, TW:2 * TW], ps_T[:, bank(b, 1)[0], :]).then_inc(half_read[1], 1)

            def low_half(i, j, c):
                u, b, h, q = spot(i, j)
                cols = slice(c * TW, (c + 1) * TW)
                dve.wait_ge(hi_ready, TC * u + c + 1)
                nc.vector.tensor_tensor(pt_lo[:, b % 2, cols], ps_T[:, bank(b, c)[0], :], pt_hi[:, b % 2, cols],
                                        ALU.subtract).then_inc(banks_used, 1)

            def add_halves(i, j):
                u, b, h, q = spot(i, j)
                at = (j // H) % 2
                dve.wait_ge(olow_ready, q + 1)
                nc.vector.tensor_tensor(o_sum[:, at], ps_O[:, (j // H) % OB, :, 0:HD], o_low[:, at], ALU.add
                                        ).then_inc(o_used, 1)
                if not hard:
                    nc.vector.reciprocal(rinv[:, at, :], sums[:, at, :]).then_inc(tail, 1)

            def normalise(i, j):
                u, b, h, q = spot(i, j)
                at = (j // H) % 2
                dve.wait_ge(tail, 2 * q + 1)
                dve.wait_ge(o_used, OB + q + 1)
                nc.vector.tensor_tensor(o_sum[:, at], o_sum[:, at],
                                        rinv[:, at, :].rearrange("p (h o) -> p h o", o=1).broadcast_to([P, H, HD]),
                                        ALU.mult).then_inc(tail, 1)

            def add_to_x(i, j):
                u, b, h, q = spot(i, j)
                at = (j // H) % 2
                if hard:
                    dve.wait_ge(o_used, OB + q + 1)
                else:
                    dve.wait_ge(tail, 2 * q + 2)
                if x_rows is not None:
                    dve.wait_ge(x_landed, 16)
                xq = X[:, q, :] if isinstance(q, int) else X[:, bass.ds(q, 1), :].rearrange("p o d -> p (o d)")
                nc.vector.scalar_tensor_tensor(xq, o_sum[:, at].rearrange("p h d -> p (h d)"), out_scale, xq,
                                               ALU.mult, ALU.add)

            def slot(i, j):
                ending = previous(i, j, 2) and (j - 2) % H == H - 1
                if valid(i, j + 2):
                    mask_chunk(i, j + 2, 0)
                if ending:
                    add_halves(i, j - 2)
                if not hard and valid(i, j):
                    low_half(i, j, 0)
                    low_half(i, j, 1)
                if hard and valid(i, j):
                    take_half(i, j)
                if ending and not hard:
                    normalise(i, j - 2)
                if valid(i, j + 2):
                    mask_chunk(i, j + 2, 1)
                if not hard and valid(i, j):
                    low_half(i, j, 2)
                if ending:
                    add_to_x(i, j - 2)

            def prologue():
                dve.sem_inc(masked, CREDIT)
                if hard:
                    dve.sem_inc(half_read[1], 1)
                else:
                    dve.sem_inc(banks_used, 2 * (TC - 1))
                dve.sem_inc(o_used, OB)
                first = nc.vector.tensor_scalar(mask[:, 0, :], adj_in[:, 0, :], 0.0, low, ALU.is_le, ALU.mult)
                if hard:
                    first.then_inc(unbiased, 1)
                    dve.wait_ge(unbiased, 1)
                    first = nc.vector.tensor_scalar(mask[:, 0, :], mask[:, 0, :], score_bias, None, ALU.add)
                first.then_inc(first_mask, 1)
                dve.wait_ge(first_mask, 1)
                for j in range(2):
                    for c in range(SC):
                        mask_chunk(0, j, c)

            run(dve, prologue, slot)


def layer_norm(nc, name, X, ident=None, XT=None, halves=None, saved=None, beside=None, update=None,
               loads=()):
    SAVES = 4
    PART = NT // SAVES
    with ExitStack() as ctx:
        def sb(n, shape, dt):
            return ctx.enter_context(nc.sbuf_tensor(name + n, shape, dt))

        def sem(n):
            return ctx.enter_context(nc.semaphore(name + n))

        stats = sb("stats", [P, NT, 6], F32)
        mean_var = sb("mean_var", [P, NT, 2], F32)
        eps = sb("eps", [P, 1], F32)
        std = sb("std", [P, NT], F32)
        rstd = sb("rstd", [P, NT], F32)
        if update is not None:
            jobs, func, bias, YT = update
            ps_y = ctx.enter_context(nc.psum_tensor(name + "ps_y", [P, 4, CW], F32))
            ps_back = ctx.enter_context(nc.psum_tensor(name + "ps_back", [P, 2, 2, D], F32))
            y_made = sem("y_made")
            y_ready = sem("y_ready")
            y_back = sem("y_back")
            x_updated = sem("x_updated")
        stats_done = sem("stats_done")
        moments_done = sem("moments_done")
        std_done = sem("std_done")
        rstd_done = sem("rstd_done")
        eps_done = sem("eps_done")
        normed = sem("normed")
        if XT is not None:
            ps = ctx.enter_context(nc.psum_tensor(name + "ps", [P, 2, CW], F32))
            flipped = sem("flipped")
            read = sem("read")
            hi_done = sem("hi_done")
        if saved is not None:
            written = sem("written")
        if loads:
            loaded = sem("loaded")
        block = ctx.enter_context(nc.Block())
        groups = [(fc, c) for c in range(NC) for fc in range(DC)]

        @block.sync
        def _(sp):
            if beside is not None:
                beside.load(sp)
            for dst, src in loads:
                sp.dma_start(dst, src).then_inc(loaded, 16)
            if saved is not None:
                for k in range(SAVES):
                    tiles = slice(k * PART, (k + 1) * PART)
                    sp.wait_ge(normed, (k + 1) * PART)
                    sp.dma_start(saved[:, tiles, :], X[:, tiles, :]).then_inc(written, 16)
                sp.wait_ge(written, 16 * SAVES)
            if loads:
                sp.wait_ge(loaded, 16 * len(loads))

        @block.tensor
        def _(pe):
            def back(c):
                for n in range(2 * c, 2 * c + 2):
                    pe.wait_ge(y_ready, DC * (c + 1))
                    if n >= 2:
                        pe.wait_ge(x_updated, n - 1)
                    for k in range(2):
                        t = 2 * n + k
                        for fc in range(DC):
                            last = nc.tensor.transpose(ps_back[:, n % 2, k, fc * P:(fc + 1) * P],
                                                       YT[:, fc, t * P:(t + 1) * P], ident[:])
                    last.then_inc(y_back, 1)

            if update is not None:
                for c in range(NC):
                    for oc in range(DC):
                        n = c * DC + oc
                        if n >= 4:
                            pe.wait_ge(y_ready, n - 3)
                        for k, (W, src) in enumerate(jobs):
                            for kc in range(DC):
                                last = nc.tensor.matmul(ps_y[:, n % 4, :], W[:, kc, oc * P:(oc + 1) * P],
                                                        src[:, kc, c * CW:(c + 1) * CW], start=(k == 0 and kc == 0),
                                                        stop=(k == len(jobs) - 1 and kc == DC - 1))
                        last.then_inc(y_made, 1)
                    if c >= 1:
                        back(c - 1)
                back(NC - 1)
            if beside is not None:
                beside.products(pe)
            if XT is not None:
                for n, (fc, c) in enumerate(groups):
                    pe.wait_ge(normed, (c + 1) * (CW // P))
                    if n >= 2:
                        pe.wait_ge(read, n - 1)
                    for k in range(CW // P):
                        last = nc.tensor.transpose(ps[:, n % 2, k * P:(k + 1) * P],
                                                   X[:, c * (CW // P) + k, fc * P:(fc + 1) * P], ident[:])
                    last.then_inc(flipped, 1)
        @block.scalar
        def _(act):
            if update is not None:
                for n in range(NC * DC):
                    c, oc = divmod(n, DC)
                    act.wait_ge(y_made, n + 1)
                    nc.scalar.activation(YT[:, oc, c * CW:(c + 1) * CW], ps_y[:, n % 4, :], func,
                                         bias=bias[:, oc:oc + 1], scale=1.0).then_inc(y_ready, 1)
            act.wait_ge(eps_done, 1)
            act.wait_ge(moments_done, NT)
            nc.scalar.activation(std[:], mean_var[:, :, 1], ACT.Sqrt, bias=eps[:], scale=1.0).then_inc(std_done, 1)
            if beside is not None:
                beside.copy_biases(act)
                beside.copies(act)
            if XT is not None:
                for n, (fc, c) in enumerate(groups):
                    act.wait_ge(flipped, n + 1)
                    nc.scalar.activation(XT[:, fc, c * CW:(c + 1) * CW], ps[:, n % 2, :], ACT.Copy
                                         ).then_inc(read, 1)

        @block.vector
        def _(dve):
            nc.vector.memset(eps[:], EPS).then_inc(eps_done, 1)
            if beside is not None:
                beside.bias_columns(dve)

            def aggregate(tiles):
                for t in tiles:
                    dve.wait_ge(stats_done, t + 1)
                    nc.vector.bn_aggr(mean_var[:, t, :], stats[:, t, :]).then_inc(moments_done, 1)

            for n in range(NT // 2):
                pair = slice(2 * n, 2 * n + 2)
                if update is not None:
                    dve.wait_ge(y_back, n + 1)
                    nc.vector.tensor_tensor(X[:, pair, :], ps_back[:, n % 2], X[:, pair, :], ALU.add
                                            ).then_inc(x_updated, 1)
                    dve.wait_ge(x_updated, n + 1)
                for t in range(2 * n, 2 * n + 2):
                    nc.vector.bn_stats(stats[:, t, :], X[:, t, :]).then_inc(stats_done, 1)
                if n >= 1:
                    aggregate(range(2 * n - 2, 2 * n))
            aggregate(range(NT - 2, NT))
            dve.wait_ge(std_done, 1)
            nc.vector.reciprocal(rstd[:], std[:]).then_inc(rstd_done, 1)
            dve.wait_ge(rstd_done, 1)
            for t in range(NT):
                nc.vector.tensor_scalar(X[:, t, :], X[:, t, :], mean_var[:, t, 0:1], rstd[:, t:t + 1],
                                        ALU.subtract, ALU.mult).then_inc(normed, 1)
            if halves is not None:
                dve.wait_ge(normed, NT)
                nc.vector.tensor_scalar(halves[:, :, 0, :], X[:, :, :], STATE_SCALE, None, ALU.mult
                                        ).then_inc(hi_done, 1)
                dve.wait_ge(hi_done, 1)
                nc.vector.scalar_tensor_tensor(halves[:, :, 1, :], X[:, :, :], STATE_SCALE, halves[:, :, 0, :],
                                               ALU.mult, ALU.subtract)
            if beside is not None:
                beside.degree_parts(dve)


def gated_loads(ins, G, bload, gate_bias):
    loads = [(bload[:, s, :], ins[f"L1_gnn_{n}_b"]) for s, n in enumerate(("in", "out"))]
    for g, n in enumerate("rzh"):
        loads.append((G[:, :, g, :], ins[n + "WT"].rearrange("(c p) f -> p c f", p=P)))
        loads.append((gate_bias[:, g, :], ins[f"L1_gnn_{n}_b"]))
    return loads


class GatedWeights:

    EACH = GATES * D // 2

    def __init__(self, nc, ctx, ins, G, bload, cparts, sel):
        def sb(n, shape, dt):
            return ctx.enter_context(nc.sbuf_tensor("gw_" + n, shape, dt))

        def sem(n):
            return ctx.enter_context(nc.semaphore("gw_" + n))

        self.nc, self.ins, self.bload, self.cparts, self.sel = nc, ins, bload, cparts, sel
        self.Gflat = G[:].rearrange("p c g f -> p c (g f)")
        self.W = [sb("W0", [P, DC, D], F32), sb("W1", [P, DC, D], F32)]
        self.bcol = sb("bcol", [P, 2, DC, 6], F32)
        self.c_all = sb("c_all", [6, GATES * D], F32)
        self.piece = sb("piece", [6, 3, GATES * D], BF16)
        self.ps = ctx.enter_context(nc.psum_tensor("gw_ps", [P, 2, 2, CW], F32))
        self.psc = ctx.enter_context(nc.psum_tensor("gw_psc", [6, 2, CW], F32))
        self.landed = sem("landed")
        self.made = sem("made")
        self.taken = sem("taken")
        self.cmade = sem("cmade")
        self.pieces = sem("pieces")
        self.chain = sem("chain")
        self.count = 0

    def load(self, sp):
        for s, n in enumerate(("in", "out")):
            sp.dma_start(self.W[s][:], self.ins[f"L1_gnn_{n}_W"].rearrange("(c p) f -> p c f", p=P)
                         ).then_inc(self.landed, 16)

    def products(self, pe):
        nc, EACH, Gflat = self.nc, self.EACH, self.Gflat
        pe.wait_ge(self.chain, 2)
        for half in range(2):
            for s in range(2):
                for kc in range(DC):
                    last = nc.tensor.matmul(self.psc[:, half, 0:EACH], self.bcol[:, s, kc, :],
                                            Gflat[:, s * DC + kc, half * EACH:(half + 1) * EACH],
                                            start=(s == 0 and kc == 0), stop=(s == 1 and kc == DC - 1))
        last.then_inc(self.cmade, 1)
        pe.wait_ge(self.landed, 16 * 2)
        for n in range(2 * DC):
            s, fc = divmod(n, DC)
            if n >= 2:
                pe.wait_ge(self.taken, n - 1)
            for half in range(2):
                for kc in range(DC):
                    last = nc.tensor.matmul(self.ps[:, n % 2, half, 0:EACH], self.W[s][:, kc, fc * P:(fc + 1) * P],
                                            Gflat[:, s * DC + kc, half * EACH:(half + 1) * EACH],
                                            start=(kc == 0), stop=(kc == DC - 1))
            last.then_inc(self.made, 1)

    def copy_biases(self, act):
        act.wait_ge(self.cmade, 1)
        for dst in (self.c_all[:], self.piece[:, 0, :]):
            self.nc.scalar.activation(dst.rearrange("p (a e) -> p a e", a=2), self.psc[:, :, 0:self.EACH], ACT.Copy
                                      ).then_inc(self.pieces, 1)

    def copies(self, act):
        for n in range(2 * DC):
            act.wait_ge(self.made, DC * (n // DC + 1))
            self.nc.scalar.activation(self.Gflat[:, n, :].rearrange("p (a e) -> p a e", a=2),
                                      self.ps[:, n % 2, :, 0:self.EACH], ACT.Copy).then_inc(self.taken, 1)

    def link(self, dve, ins):
        ins.then_inc(self.chain, 1)
        self.count += 1
        dve.wait_ge(self.chain, self.count)

    def bias_columns(self, dve):
        nc = self.nc
        self.link(dve, nc.vector.memset(self.bcol[:], 0.0))
        for s in range(2):
            b = self.bload[:, s, :].rearrange("p (c o) -> p c o", o=1).broadcast_to([P, DC, 3])
            ins = nc.vector.tensor_copy(self.bcol[:, s, :, 3 * s:3 * s + 3], b)
        self.link(dve, ins)

    def degree_parts(self, dve):
        nc, piece, sel, c_all = self.nc, self.piece, self.sel, self.c_all
        dve.wait_ge(self.pieces, 2)
        self.link(dve, nc.vector.tensor_tensor(c_all[:], c_all[:], piece[:, 0, :], ALU.subtract))
        self.link(dve, nc.vector.tensor_copy(piece[:, 1, :], c_all[:]))
        self.link(dve, nc.vector.tensor_tensor(piece[:, 2, :], c_all[:], piece[:, 1, :], ALU.subtract))
        self.link(dve, nc.vector.tensor_scalar(c_all[:], piece[:, 0, :], sel[:, 0:1], None, ALU.mult))
        self.link(dve, nc.vector.scalar_tensor_tensor(c_all[:], piece[:, 1, :], sel[:, 1:2], c_all[:],
                                                      ALU.mult, ALU.add))
        nc.vector.scalar_tensor_tensor(self.cparts[:], piece[:, 2, :], sel[:, 2:3], c_all[:], ALU.mult, ALU.add)


def soft_inputs(nc, xT, x2T, v, adj, adj_in, ks_stack, qs_stack, vs, in_scale, consts):
    with ExitStack() as ctx:
        def sb(n, shape, dt):
            return ctx.enter_context(nc.sbuf_tensor("si_" + n, shape, dt))

        def sem(n):
            return ctx.enter_context(nc.semaphore("si_" + n))

        raw = [sb(f"raw{n}", [P, DC, N], F32) for n in range(2)]
        raw_v = sb("raw_v", [P, NT * H, HD], F32)
        landed = [[sem(f"landed{n}_{fc}") for fc in range(DC)] for n in range(2)]
        v_landed = sem("v_landed")
        adj_landed = sem("adj_landed")
        consts_landed = sem("consts_landed")
        hi_done = [sem("hi_done"), 0]
        halves_done = sem("halves_done")
        stacked = sem("stacked")
        block = ctx.enter_context(nc.Block())
        stacks = (ks_stack, qs_stack)

        @block.sync
        def _(sp):
            for fc in range(DC):
                for n, src in enumerate((x2T, xT)):
                    sp.dma_start(raw[n][:, fc, :], src[fc * P:(fc + 1) * P, :]).then_inc(landed[n][fc], 16)
            sp.dma_start(raw_v[:].rearrange("p (t h) d -> p t (h d)", h=H),
                         v.rearrange("(t p) d -> p t d", p=P)).then_inc(v_landed, 16)
            for dst, src in consts:
                sp.dma_start(dst, src).then_inc(consts_landed, 16)
            total = 0
            for n, stack in enumerate(stacks):
                sp.wait_ge(halves_done, n + 1)
                for h in range(2):
                    total += stack_head(sp, h, *stack, stacked)
            sp.dma_start(adj_in[:, 0, :], adj[0:P, :]).then_inc(adj_landed, 16)
            sp.wait_ge(stacked, total)
            sp.wait_ge(adj_landed, 16)
            sp.wait_ge(consts_landed, 16 * len(consts))

        @block.vector
        def _(dve):
            for fc in range(DC):
                for n, (stack, hi, lo, order) in enumerate(stacks):
                    dve.wait_ge(landed[n][fc], 16)
                    split_halves(nc, dve, hi[:, fc, :], lo[:, fc, :], raw[n][:, fc, :], in_scale, hi_done
                                 ).then_inc(halves_done, 1)
            dve.wait_ge(v_landed, 16)
            vv = vs[:].rearrange("p t h e -> p (t h) e")
            split_halves(nc, dve, vv[:, :, 0:HD], vv[:, :, HD:2 * HD], raw_v[:], in_scale, hi_done)


def build_adjacency(nc, adj, stage, A, AT, halves, kept, deg_rows, ident16):
    TPC = CW // P
    GROUP = P // NC
    TBANKS = 3
    with ExitStack() as ctx:
        row_sum = ctx.enter_context(nc.sbuf_tensor("ba_row_sum", [P, NT], F32))
        row_cols = ctx.enter_context(nc.sbuf_tensor("ba_row_cols", [P, NT, P], F16))
        ones_cols = ctx.enter_context(nc.sbuf_tensor("ba_ones_cols", [P, NC, P], F16))
        ps_T = ctx.enter_context(nc.psum_tensor("ba_ps", [P, TBANKS, 8 * P], F16))
        ps_deg = ctx.enter_context(nc.psum_tensor("ba_deg", [P, CW], F32))
        landed = [ctx.enter_context(nc.semaphore(f"ba_landed{b}")) for b in range(2)]
        cast = ctx.enter_context(nc.semaphore("ba_cast"))
        cleared = ctx.enter_context(nc.semaphore("ba_cleared"))
        cols_ready = ctx.enter_context(nc.semaphore("ba_cols"))
        flipped = ctx.enter_context(nc.semaphore("ba_flipped"))
        read = ctx.enter_context(nc.semaphore("ba_read"))
        summed = ctx.enter_context(nc.semaphore("ba_summed"))
        block = ctx.enter_context(nc.Block())
        adj_tiles = adj.rearrange("(t p) n -> t p n", p=P)

        @block.sync
        def _(sp):
            for t in range(NT):
                if t >= 2:
                    sp.wait_ge(cast, t - 1)
                sp.dma_start(stage[:, t % 2, :], adj_tiles[t]).then_inc(landed[t % 2], 16)

        @block.scalar
        def _(act):
            for t in range(NT):
                act.wait_ge(landed[t % 2], 16 * (t // 2 + 1))
                nc.scalar.activation(A[:, t, :], stage[:, t % 2, :], ACT.Copy, accum_out=row_sum[:, t:t + 1]
                                     ).then_inc(cast, 1)

        @block.tensor
        def _(pe):
            pe.wait_ge(cols_ready, 1)
            for t in range(NT):
                pe.wait_ge(cast, t + 1)
                for g in range(2):
                    n = 2 * t + g
                    if n >= TBANKS:
                        pe.wait_ge(read, n - TBANKS + 1)
                    for k in range(8):
                        last = nc.tensor.transpose(ps_T[:, n % TBANKS, k * P:(k + 1) * P],
                                                   A[:, t, (8 * g + k) * P:(8 * g + k + 1) * P], ident16[:])
                    last.then_inc(flipped, 1)
                for c in range(2):
                    for fc in range(DC):
                        for half in range(2):
                            nc.tensor.matmul(kept[:, c * DC + fc, :], halves[:, t, half, fc * P:(fc + 1) * P],
                                             A[:, t, c * CW:(c + 1) * CW], start=(t == 0 and half == 0),
                                             stop=(t == NT - 1 and half == 1))
                for row_t in ([t - 1] if 0 < t < NT - 1 else [t - 1, t] if t else []):
                    pe.wait_ge(cols_ready, row_t + 2)
                    k = row_t % TPC
                    nc.tensor.matmul(ps_deg[:, k * P:(k + 1) * P], row_cols[:, row_t, :], ident16[:],
                                     start=False, stop=False)
                for c in range(NC):
                    last = nc.tensor.matmul(ps_deg[:], ones_cols[:, c, :], A[:, t, c * CW:(c + 1) * CW],
                                            start=(t == 0 and c == 0), stop=(t == NT - 1 and c == NC - 1))
            last.then_inc(summed, 1)

        @block.vector
        def _(dve):
            nc.vector.memset(row_cols[:], 0.0).then_inc(cleared, 1)
            nc.vector.memset(ones_cols[:], 0.0).then_inc(cleared, 1)
            dve.wait_ge(cleared, 2)
            for c in range(NC):
                ones = nc.vector.memset(ones_cols[:, c, c * GROUP + 3:c * GROUP + 6], 1.0)
            ones.then_inc(cols_ready, 1)
            for t in range(NT):
                at = t // TPC * GROUP
                dve.wait_ge(cast, t + 1)
                nc.vector.tensor_copy(row_cols[:, t, at:at + 3], row_sum[:, t:t + 1].broadcast_to([P, 3])
                                      ).then_inc(cols_ready, 1)
                for g in range(2):
                    n = 2 * t + g
                    dve.wait_ge(flipped, n + 1)
                    nc.vector.tensor_copy(AT[:, 8 * g:8 * g + 8, t * P:(t + 1) * P],
                                          ps_T[:, n % TBANKS, :].rearrange("p (k i) -> p k i", i=P)
                                          ).then_inc(read, 1)
            dve.wait_ge(summed, 1)
            for c in range(NC):
                nc.vector.tensor_copy(deg_rows[:, c * CW:(c + 1) * CW], ps_deg[c * GROUP:c * GROUP + 6, :])


def gated_steps(nc, A, AT, ST, halves, G, cparts, deg_rows, gate_bias, ident, work, kept):
    with ExitStack() as ctx:
        def sb(n, shape, dt):
            return ctx.enter_context(nc.sbuf_tensor("gs_" + n, shape, dt))

        def sem(n):
            return ctx.enter_context(nc.semaphore("gs_" + n))

        flat = work.rearrange("p (b w) -> p b w", w=CW)
        msg = flat[:, 0:2 * DC, :]
        r = flat[:, 2 * DC:3 * DC, :]
        z = flat[:, 3 * DC:4 * DC, :]
        cand = sb("cand", [P, DC, CW], F32)
        ps_fwd = ctx.enter_context(nc.psum_tensor("gs_ps_fwd", [P, DC, CW], F32))
        ps_msg = [ps_fwd[:, m, :] for m in range(DC)] + [kept[:, m, :] for m in range(DC)]
        ps_gate = ctx.enter_context(nc.psum_tensor("gs_ps_gate", [P, 2, CW], F32))
        ps_T = kept[:, DC:2 * DC, :]
        summed = sem("summed")
        msg_ready = sem("msg_ready")
        gate_ready = sem("gate_ready")
        gate_read = sem("gate_read")
        rs_ready = sem("rs_ready")
        delta = sem("delta")
        passed_pe = sem("passed_pe")
        flipped = sem("flipped")
        hi_done = sem("hi_done")
        lo_done = sem("lo_done")
        block = ctx.enter_context(nc.Block())
        MB = 2 * DC
        GB = GATES * DC
        TB = NT // 2
        TC = TB // NC
        LATE = list(range(TB - TC, TB))
        EARLY = list(range(TB - TC))
        READY_TILES = 2 * len(EARLY)

        def steps(eng, chunk):
            for c in range(NC):
                chunk(0, c, c, False, c == NC - 1)
            with eng.Fori(1, STEPS) as s:
                chunk(s, 0, s * NC, True, False)
                with eng.Fori(1, NC - 1) as c:
                    chunk(s, c, s * NC + c, False, False)
                chunk(s, NC - 1, s * NC + (NC - 1), False, True)

        def turn(s, late, x):
            return TB * s + x - (len(LATE) if late else 0)

        def summed_before(s, c, m):
            return kept[:, c * DC + m - DC, :] if isinstance(s, int) and c < 2 and m >= DC else None

        def columns(c):
            return slice(c * CW, (c + 1) * CW) if isinstance(c, int) else bass.ds(c * CW, CW)

        @block.tensor
        def _(pe):
            pe.sem_inc(gate_read, 2)
            pe.sem_inc(gate_ready, 1)

            def flip(s, banks, late):
                for x, b in enumerate(banks):
                    k = turn(s, late, x)
                    pe.wait_ge(lo_done, k + 1)
                    for i in range(2):
                        for fc in range(DC):
                            at, t = (i * DC + fc) * P, 2 * b + i
                            last = nc.tensor.transpose(ps_T[:, b % 2, at:at + P], ST[:, fc, t * P:(t + 1) * P],
                                                       ident[:])
                    last.then_inc(flipped, 1)

            def chunk(s, c, n, first, last_chunk):
                if first:
                    pe.wait_ge(lo_done, 2 + TB * s - len(LATE))
                pe.wait_ge(msg_ready, 1 + MB * n)
                for m in range(MB):
                    if summed_before(s, c, m) is not None:
                        continue
                    src, fc = (AT, A)[m // DC], m % DC
                    for t in range(NT):
                        if first and m == 0 and t == READY_TILES:
                            pe.wait_ge(delta, 1 + 3 * NC * s)
                            flip(s, LATE, True)
                            pe.wait_ge(lo_done, 2 + TB * s)
                        for half in range(2):
                            last = nc.tensor.matmul(ps_msg[m], halves[:, t, half, fc * P:(fc + 1) * P],
                                                    src[:, t, columns(c)], start=(t == 0 and half == 0),
                                                    stop=(t == NT - 1 and half == 1))
                    last.then_inc(summed, 1)
                for g in range(GATES):
                    if last_chunk and g == GATES - 1:
                        pe.wait_ge(delta, 1 + 3 * n)
                        flip(s, EARLY, False)
                    for oc in range(DC):
                        k = g * DC + oc
                        pe.wait_ge(gate_read, GB * n + k + 1)
                        pe.sem_inc(passed_pe, 1)
                        out = ps_gate[:, k % 2, :]
                        cols = slice(oc * P, (oc + 1) * P)
                        nc.tensor.matmul(out, cparts[:, g * D + oc * P:g * D + (oc + 1) * P],
                                         deg_rows[:, columns(c)], start=True, stop=False)
                        if g < 2:
                            for kc in range(DC):
                                nc.tensor.matmul(out, G[:, 2 * DC + kc, g, cols], ST[:, kc, columns(c)],
                                                 start=False, stop=False)
                        for m in range(MB):
                            pe.wait_ge(msg_ready, 1 + MB * n + m + 1)
                            last = nc.tensor.matmul(out, G[:, m, g, cols], msg[:, m, :], start=False,
                                                    stop=(g < 2 and m == MB - 1))
                        if g == 2:
                            pe.wait_ge(rs_ready, DC * (n + 1))
                            for kc in range(DC):
                                last = nc.tensor.matmul(out, G[:, 2 * DC + kc, g, cols], r[:, kc, :],
                                                        start=False, stop=(kc == DC - 1))
                        last.then_inc(gate_ready, 1)

            steps(pe, chunk)

        @block.scalar
        def _(act):
            act.sem_inc(msg_ready, 1)

            def high(s, banks, late):
                for x, b in enumerate(banks):
                    act.wait_ge(flipped, turn(s, late, x) + 1)
                    nc.scalar.activation(halves[:, 2 * b:2 * b + 2, 0, :],
                                         ps_T[:, b % 2, :].rearrange("p (k f) -> p k f", k=2), ACT.Copy,
                                         scale=STATE_SCALE).then_inc(hi_done, 1)

            def chunk(s, c, n, first, last_chunk):
                if first:
                    high(s, LATE, True)
                for m in range(MB):
                    before = summed_before(s, c, m)
                    if before is None:
                        act.wait_ge(summed, MB * n + m + 1)
                    else:
                        act.sem_inc(summed, 1)
                    if m == 0:
                        act.wait_ge(gate_ready, 1 + GB * n)
                    nc.scalar.activation(msg[:, m, :], ps_msg[m] if before is None else before, ACT.Copy, scale=1.0 / STATE_SCALE
                                         ).then_inc(msg_ready, 1)
                act.wait_ge(delta, 1 + 3 * n)
                for g, (out, func) in enumerate(((r, ACT.Sigmoid), (z, ACT.Sigmoid), (cand, ACT.Tanh))):
                    if last_chunk and g == GATES - 1:
                        high(s, EARLY, False)
                    for oc in range(DC):
                        k = g * DC + oc
                        act.wait_ge(gate_ready, 1 + GB * n + k + 1)
                        nc.scalar.activation(out[:, oc, :], ps_gate[:, k % 2, :], func,
                                             bias=gate_bias[:, g, oc:oc + 1], scale=1.0).then_inc(gate_read, 1)

            steps(act, chunk)

        @block.vector
        def _(dve):
            dve.sem_inc(delta, 1)
            dve.sem_inc(lo_done, 2)

            def low_half(s, banks, late):
                for x, b in enumerate(banks):
                    dve.wait_ge(hi_done, turn(s, late, x) + 1)
                    nc.vector.scalar_tensor_tensor(halves[:, 2 * b:2 * b + 2, 1, :],
                                                   ps_T[:, b % 2, :].rearrange("p (k f) -> p k f", k=2), STATE_SCALE,
                                                   halves[:, 2 * b:2 * b + 2, 0, :], ALU.mult, ALU.subtract
                                                   ).then_inc(lo_done, 1)

            def chunk(s, c, n, first, last_chunk):
                if first:
                    low_half(s, LATE, True)
                st = ST[:, :, columns(c)]
                for oc in range(DC):
                    dve.wait_ge(gate_read, 2 + GB * n + oc + 1)
                    nc.vector.tensor_tensor(r[:, oc, :], r[:, oc, :], ST[:, oc, columns(c)], ALU.mult
                                            ).then_inc(rs_ready, 1)
                if last_chunk:
                    low_half(s, EARLY, False)
                dve.wait_ge(gate_read, 2 + GB * (n + 1))
                nc.vector.tensor_tensor(cand[:], cand[:], st, ALU.subtract).then_inc(delta, 1)
                dve.wait_ge(delta, 1 + 3 * n + 1)
                nc.vector.tensor_tensor(cand[:], cand[:], z, ALU.mult).then_inc(delta, 1)
                dve.wait_ge(delta, 1 + 3 * n + 2)
                nc.vector.tensor_tensor(st, st, cand[:], ALU.add).then_inc(delta, 1)

            steps(dve, chunk)


def feature_matmul(nc, name, YT, jobs, funcs, beside=()):
    func, bias = funcs
    with ExitStack() as ctx:
        ps = ctx.enter_context(nc.psum_tensor(name + "ps", [P, 4, CW], F32))
        made = ctx.enter_context(nc.semaphore(name + "made"))
        read = ctx.enter_context(nc.semaphore(name + "read"))
        if beside:
            loaded = ctx.enter_context(nc.semaphore(name + "loaded"))
        block = ctx.enter_context(nc.Block())
        banks = [(c, oc) for c in range(NC) for oc in range(DC)]

        if beside:
            @block.sync
            def _(sp):
                for dst, src in beside:
                    sp.dma_start(dst, src).then_inc(loaded, 16)
                sp.wait_ge(loaded, 16 * len(beside))

        @block.tensor
        def _(pe):
            for n, (c, oc) in enumerate(banks):
                if n >= 4:
                    pe.wait_ge(read, n - 3)
                for k, (W, XT) in enumerate(jobs):
                    for kc in range(DC):
                        last = nc.tensor.matmul(ps[:, n % 4, :], W[:, kc, oc * P:(oc + 1) * P],
                                                XT[:, kc, c * CW:(c + 1) * CW], start=(k == 0 and kc == 0),
                                                stop=(k == len(jobs) - 1 and kc == DC - 1))
                last.then_inc(made, 1)

        @block.scalar
        def _(act):
            for n, (c, oc) in enumerate(banks):
                act.wait_ge(made, n + 1)
                nc.scalar.activation(YT[:, oc, c * CW:(c + 1) * CW], ps[:, n % 4, :], func,
                                     bias=bias[:, oc:oc + 1], scale=1.0).then_inc(read, 1)


class MeanWeights:

    def __init__(self, nc, ctx, srcs, Wx, Wa, bias):
        def sb(n, shape, dt):
            return ctx.enter_context(nc.sbuf_tensor("mw_" + n, shape, dt))

        self.nc, self.srcs, self.Wx, self.Wa, self.bias = nc, srcs, Wx, Wa, bias
        self.WT = [sb("WT0", [P, DC, D], F32), sb("WT1", [P, DC, D], F32)]
        self.C = sb("C", [P, 2 * DC, D], F32)
        self.b = sb("b", [P, 2, DC], F32)
        self.bc = sb("bc", [P, DC], F32)
        self.ps = ctx.enter_context(nc.psum_tensor("mw_ps", [P, 2, DC, D], F32))
        self.psb = ctx.enter_context(nc.psum_tensor("mw_psb", [P, DC], F32))
        self.landed = ctx.enter_context(nc.semaphore("mw_landed"))
        self.made = ctx.enter_context(nc.semaphore("mw_made"))

    def load(self, sp):
        W_selfT, b_self, W_nbT, b_nb, W_comb, b_comb = self.srcs
        for s, (w, bb) in enumerate(((W_selfT, b_self), (W_nbT, b_nb))):
            sp.dma_start(self.WT[s][:], w.rearrange("(c p) f -> p c f", p=P)).then_inc(self.landed, 16)
            sp.dma_start(self.b[:, s, :], bb).then_inc(self.landed, 16)
        sp.dma_start(self.C[:], W_comb.rearrange("(c p) f -> p c f", p=P)).then_inc(self.landed, 16)
        sp.dma_start(self.bc[:], b_comb).then_inc(self.landed, 16)

    def products(self, pe):
        nc, C = self.nc, self.C
        pe.wait_ge(self.landed, 16 * 6)
        for s in range(2):
            for fc in range(DC):
                for kc in range(DC):
                    nc.tensor.matmul(self.ps[:, s, fc, :], self.WT[s][:, kc, fc * P:(fc + 1) * P],
                                     C[:, s * DC + kc, :], start=(kc == 0), stop=(kc == DC - 1))
        for oc in range(DC):
            for s in range(2):
                for kc in range(DC):
                    last = nc.tensor.matmul(self.psb[:, oc:oc + 1], C[:, s * DC + kc, oc * P:(oc + 1) * P],
                                            self.b[:, s, kc:kc + 1], start=(s == 0 and kc == 0),
                                            stop=(s == 1 and kc == DC - 1))
        last.then_inc(self.made, 1)

    def copies(self, dve):
        nc = self.nc
        dve.wait_ge(self.made, 1)
        nc.vector.tensor_copy(self.Wx[:], self.ps[:, 0])
        nc.vector.tensor_copy(self.Wa[:], self.ps[:, 1])
        dve.wait_ge(self.landed, 16 * 6)
        nc.vector.tensor_tensor(self.bias[:], self.psb[:], self.bc[:], ALU.add)


def mean_neighbours(nc, AT, halves, agg, deg_rows, ones16, weights):
    with ExitStack() as ctx:
        rdeg = ctx.enter_context(nc.sbuf_tensor("mn_rdeg", [P, 2, CW], F32))
        top = ctx.enter_context(nc.sbuf_tensor("mn_top", [P, 2, CW], F32))
        ps = ctx.enter_context(nc.psum_tensor("mn_ps", [P, 2, DC, CW], F32))
        ps_deg = ctx.enter_context(nc.psum_tensor("mn_ps_deg", [P, CW], F32))
        mean_weights = MeanWeights(nc, ctx, *weights)
        degrees = ctx.enter_context(nc.semaphore("mn_degrees"))
        made = ctx.enter_context(nc.semaphore("mn_made"))
        read = ctx.enter_context(nc.semaphore("mn_read"))
        chain = ctx.enter_context(nc.semaphore("mn_chain"))
        block = ctx.enter_context(nc.Block())

        @block.sync
        def _(sp):
            mean_weights.load(sp)

        @block.tensor
        def _(pe):
            for c in range(NC):
                cols = slice(c * CW, (c + 1) * CW)
                if c >= 1:
                    pe.wait_ge(chain, 2 * c - 1)
                nc.tensor.matmul(ps_deg[:], ones16[0:1, :], deg_rows[0:1, cols], start=True, stop=True
                                 ).then_inc(degrees, 1)
                if c >= 2:
                    pe.wait_ge(read, DC * (c - 1))
                for fc in range(DC):
                    for t in range(NT):
                        for half in range(2):
                            last = nc.tensor.matmul(ps[:, c % 2, fc, :], halves[:, t, half, fc * P:(fc + 1) * P],
                                                    AT[:, t, cols], start=(t == 0 and half == 0),
                                                    stop=(t == NT - 1 and half == 1))
                    last.then_inc(made, 1)
                if c == 1:
                    mean_weights.products(pe)

        @block.vector
        def _(dve):
            for c in range(NC):
                dve.wait_ge(degrees, c + 1)
                nc.vector.tensor_scalar(top[:, c % 2, :], ps_deg[:], 1.0, STATE_SCALE, ALU.max, ALU.mult
                                        ).then_inc(chain, 1)
                dve.wait_ge(chain, 2 * c + 1)
                nc.vector.reciprocal(rdeg[:, c % 2, :], top[:, c % 2, :]).then_inc(chain, 1)
                dve.wait_ge(chain, 2 * c + 2)
                for fc in range(DC):
                    dve.wait_ge(made, DC * c + fc + 1)
                    nc.vector.tensor_tensor(agg[:, fc, c * CW:(c + 1) * CW], ps[:, c % 2, fc, :], rdeg[:, c % 2, :],
                                            ALU.mult).then_inc(read, 1)
                if c == 1:
                    mean_weights.copies(dve)


def hard_inputs(nc, XT, adj, adj_in, WQT, WK, WVT, we, be, qs, ks, vs, score_bias, q_scale, k_scale, v_scale):
    SCALING = float(HD) ** -0.5
    with ExitStack() as ctx:
        def sb(n, shape, dt):
            return ctx.enter_context(nc.sbuf_tensor("hi_" + n, shape, dt))

        def sem(n):
            return ctx.enter_context(nc.semaphore("hi_" + n))

        W = [sb("WQ", [P, DC, D], F32), WK, sb("WV", [P, DC, D], F32)]
        full = [sb(f"full{n}", [P, DC, N], F32) for n in range(2)]
        hi = [sb(f"hi{n}", [P, DC, N], F16) for n in range(2)]
        lo = [sb(f"lo{n}", [P, DC, N], F16) for n in range(2)]
        we_col = sb("we_col", [P, 2], F32)
        zero = sb("zero", [P, 1], F32)
        be_raw = sb("be_raw", [P, 1], F32)
        ps = ctx.enter_context(nc.psum_tensor("hi_ps", [P, 4, CW], F32))
        psv = ctx.enter_context(nc.psum_tensor("hi_psv", [P, 2, CW], F32))
        landed = sem("landed")
        w_landed = sem("w_landed")
        consts = sem("consts")
        made = sem("made")
        read = sem("read")
        hi_done = [sem("hi_done"), 0]
        high_done = sem("high_done")
        halves_done = sem("halves_done")
        stacked = sem("stacked")
        vmade = sem("vmade")
        vread = sem("vread")
        block = ctx.enter_context(nc.Block())
        banks = [(n, oc, c) for n in (1, 0) for oc in range(DC) for c in range(NC)]
        EACH = NC * DC
        LOADS = 5

        @block.sync
        def _(sp):
            for g in range(4):
                sp.dma_start(we_col[g * HD:(g + 1) * HD, 0:1], we).then_inc(landed, 16)
            sp.dma_start(be_raw[:], be.rearrange("(o d) -> o d", o=1).broadcast_to([P, 1])).then_inc(landed, 16)
            for dst, w in ((W[2], WVT), (W[0], WQT)):
                sp.dma_start(dst[:], w.rearrange("(c p) f -> p c f", p=P)).then_inc(w_landed, 16)
            total = 0
            sp.dma_start(adj_in[:, 0, :], adj[0:P, :]).then_inc(stacked, 16)
            total += 16
            sp.wait_ge(halves_done, EACH)
            for r in range(HG):
                total += stack_heads(sp, r, ks, hi[1], lo[1], K_ORDER, stacked)
            for oc in range(DC):
                sp.wait_ge(halves_done, EACH + NC * (oc + 1))
                for h in range(oc * HG, (oc + 1) * HG):
                    total += stack_head(sp, h, qs, hi[0], lo[0], Q_ORDER, stacked)
            sp.wait_ge(stacked, total)

        @block.tensor
        def _(pe):
            def project(ms):
                for m in ms:
                    n, oc, c = banks[m]
                    if m >= 4:
                        pe.wait_ge(read, m - 3)
                    for kc in range(DC):
                        last = nc.tensor.matmul(ps[:, m % 4, :], W[n][:, kc, oc * P:(oc + 1) * P],
                                                XT[:, kc, c * CW:(c + 1) * CW], start=(kc == 0),
                                                stop=(kc == DC - 1))
                    last.then_inc(made, 1)

            def values():
                for t in range(NT):
                    if t >= 2:
                        pe.wait_ge(vread, t - 1)
                    for kc in range(DC):
                        last = nc.tensor.matmul(psv[:, t % 2, 0:D], XT[:, kc, t * P:(t + 1) * P], W[2][:, kc, :],
                                                start=(kc == 0), stop=(kc == DC - 1))
                    last.then_inc(vmade, 1)

            project(range(EACH))
            pe.wait_ge(w_landed, 16 * 2)
            project(range(EACH, 2 * EACH))
            values()

        @block.scalar
        def _(act):
            act.wait_ge(consts, 1)
            for m, (n, oc, c) in enumerate(banks):
                act.wait_ge(made, m + 1)
                cols = slice(c * CW, (c + 1) * CW)
                nc.scalar.activation(full[n][:, oc, cols], ps[:, m % 4, :], ACT.Identity,
                                     bias=(zero[:] if n == 0 else we_col[:, 1:2]),
                                     scale=(q_scale if n == 0 else SCALING * k_scale)).then_inc(read, 1)
                act.wait_ge(read, m + 1)
                nc.scalar.activation(hi[n][:, oc, cols], full[n][:, oc, cols], ACT.Copy).then_inc(high_done, 1)

        @block.vector
        def _(dve):
            def low():
                for m, (n, oc, c) in enumerate(banks):
                    cols = slice(c * CW, (c + 1) * CW)
                    dve.wait_ge(high_done, m + 1)
                    nc.vector.tensor_tensor(lo[n][:, oc, cols], full[n][:, oc, cols], hi[n][:, oc, cols],
                                            ALU.subtract).then_inc(halves_done, 1)

            def values():
                for t in range(NT):
                    dve.wait_ge(vmade, t + 1)
                    pv = psv[:, t % 2, 0:D].rearrange("p (h d) -> p h d", h=H)
                    split_halves(nc, dve, vs[:, t, :, 0:HD], vs[:, t, :, HD:2 * HD], pv, v_scale, hi_done
                                 ).then_inc(vread, 1)

            dve.wait_ge(landed, 16 * LOADS)
            nc.vector.memset(zero[:], 0.0)
            nc.vector.tensor_scalar(score_bias[:], be_raw[:], q_scale * k_scale, None, ALU.mult)
            nc.vector.tensor_scalar(we_col[:, 1:2], we_col[:, 0:1], k_scale, None, ALU.mult).then_inc(consts, 1)
            low()
            values()


def resnorm_kernel(nc, ins, out, spill):
    rows = "(t p) d -> p t d"
    ctx = ExitStack()
    with ctx:
        def sb(scope, name, shape, dt):
            return scope.enter_context(nc.sbuf_tensor(name, shape, dt))

        ident = sb(ctx, "ident", [P, P], F32)
        ident16 = sb(ctx, "ident16", [P, P], F16)
        ones16 = sb(ctx, "ones16", [P, P], F16)
        sel = sb(ctx, "sel", [6, 3], F32)
        consts = [(ident[:], ins["c_ident"]), (ident16[:], ins["c_ident16"]), (ones16[:], ins["c_ones"]),
                  (sel[:], ins["c_sel"])]
        X = sb(ctx, "X", [P, NT, D], F32)
        work = X[:].rearrange("p t d -> p (t d)")
        saved = spill.rearrange(rows, p=P)

        G = sb(ctx, "G", [P, 3 * DC, GATES, D], F32)
        side = G[:].rearrange("p c g f -> p (c g f)")[:, 0:DC * N]
        WK = G[:].rearrange("p c g f -> p (c g f)")[:, DC * N:DC * (N + D)].rearrange("p (c f) -> p c f", c=DC)
        cparts = sb(ctx, "cparts", [6, GATES * D], BF16)
        gate_bias = sb(ctx, "gate_bias", [P, GATES, DC], F32)
        bload = sb(ctx, "bload", [P, 2, DC], F32)

        def two_halves(room):
            both = room.bitcast(F16).rearrange("p (s c n) -> p s c n", s=2, c=DC)
            return both[:, 0], both[:, 1]

        IN_SCALE = 16.0
        with ExitStack() as att:
            qs = sb(att, "qs0", [P, H, N], F16)
            ks = sb(att, "ks0", [P, H, N], F16)
            vs = sb(att, "vs0", [P, NT, H, 2 * HD], F16)
            adj_in = sb(att, "adj_in0", [P, 2, N], I32)
            k_hi, k_lo = two_halves(side)
            q_hi, q_lo = two_halves(work)
            stacks = ((ks, k_hi, k_lo, K_ORDER), (qs, q_hi, q_lo, Q_ORDER))
            soft_inputs(nc, ins["xT"], ins["x2T"], ins["L0_gnn_v"], ins["adj"], adj_in, *stacks, vs, IN_SCALE,
                        consts)
            masked_attention(nc, "a0_", qs, ks, vs, X, adj_in, ins["adj"], False,
                             float(HD) ** -0.5 / IN_SCALE ** 2, 1.0 / IN_SCALE, None, ident, stacks=stacks,
                             x_rows=ins["x"].rearrange(rows, p=P),
                             beside=gated_loads(ins, G, bload, gate_bias))

        with ExitStack() as graph:
            AT = sb(graph, "AT", [P, NT, N], F16)
            halves = sb(graph, "halves", [P, NT, 2, D], F16)
            ST = sb(graph, "ST", [P, DC, N], F32)
            deg_rows = sb(graph, "deg_rows", [6, N], F16)
            o1 = sb(graph, "o1", [P, DC, D], F32)
            ob = sb(graph, "ob", [P, 2, DC], F32)
            with ExitStack() as between:
                gated = GatedWeights(nc, between, ins, G, bload, cparts, sel)
                layer_norm(nc, "n0_", X, ident, ST, halves, saved, gated,
                           loads=[(o1[:], ins["o1T"].rearrange("(c p) f -> p c f", p=P)),
                                  (ob[:, 0, :], ins["L1_gnn_o1_b"]), (ob[:, 1, :], ins["L1_gnn_o2_b"])])
            with ExitStack() as propagation:
                A = sb(propagation, "A", [P, NT, N], F16)
                kept = propagation.enter_context(nc.psum_tensor("kept", [P, 2 * DC, CW], F32))
                build_adjacency(nc, ins["adj"], work.bitcast(I32).rearrange("p (b n) -> p b n", b=2), A, AT, halves,
                                kept, deg_rows, ident16)
                gated_steps(nc, A, AT, ST, halves, G, cparts, deg_rows, gate_bias, ident, work, kept)
            with ExitStack() as read_out:
                o2 = sb(read_out, "o2", [P, DC, D], F32)
                HT = sb(read_out, "HT", [P, DC, N], F32)
                feature_matmul(nc, "r1_", HT, [(o1, ST)], (ACT.Tanh, ob[:, 0, :]),
                               beside=[(o2[:], ins["o2T"].rearrange("(c p) f -> p c f", p=P)), (X[:], saved)])
                layer_norm(nc, "n1_", X, ident, ST, halves, update=([(o2, HT)], ACT.Identity, ob[:, 1, :], ST))
            with ExitStack() as mean:
                agg = sb(mean, "agg", [P, DC, N], F32)
                YT = sb(mean, "YT", [P, DC, N], F32)
                Wx = sb(mean, "Wx", [P, DC, D], F32)
                Wa = sb(mean, "Wa", [P, DC, D], F32)
                mb = sb(mean, "mb", [P, DC], F32)
                srcs = (ins["WselfT"], ins["L2_gnn_b_self"], ins["WnbT"], ins["L2_gnn_b_nb"],
                        ins["L2_gnn_W_comb"], ins["L2_gnn_b_comb"])
                mean_neighbours(nc, AT, halves, agg, deg_rows, ones16, (srcs, Wx, Wa, mb))
                XT = side.rearrange("p (c n) -> p c n", c=DC)
                layer_norm(nc, "n2_", X, ident, XT, update=([(Wx, ST), (Wa, agg)], ACT.Relu, mb, YT),
                           loads=[(WK, ins["WKT"].rearrange("(c p) f -> p c f", p=P))])

        Q_SCALE, K_SCALE, V_SCALE = 64.0, 256.0, 64.0
        with ExitStack() as att:
            qs = sb(att, "qs3", [P, H, N], F16)
            ks = sb(att, "ks3", [P, H, N], F16)
            vs = sb(att, "vs3", [P, NT, H, 2 * HD], F16)
            score_bias = sb(att, "score_bias", [P, 1], F32)
            adj_in = sb(att, "adj_in3", [P, 2, N], I32)
            hard_inputs(nc, XT, ins["adj"], adj_in, ins["WQT"], WK, ins["WVT"], ins["L3_gnn_we"],
                        ins["L3_gnn_be"], qs, ks, vs, score_bias, Q_SCALE, K_SCALE, V_SCALE)
            masked_attention(nc, "a3_", qs, ks, vs, X, adj_in, ins["adj"], True, 2.0 ** 66, 1.0 / (V_SCALE * H),
                             score_bias[:], ident16, hot=side.bitcast(F16).rearrange("p (b n) -> p b n", b=4))
        layer_norm(nc, "n3_", X, saved=out.rearrange(rows, p=P))


_T = {"xT": "x", "x2T": "L0_gnn_x2", "rWT": "L1_gnn_r_W", "zWT": "L1_gnn_z_W", "hWT": "L1_gnn_h_W",
      "o1T": "L1_gnn_o1_W", "o2T": "L1_gnn_o2_W", "WselfT": "L2_gnn_W_self", "WnbT": "L2_gnn_W_nb",
      "WQT": "L3_gnn_WQ", "WKT": "L3_gnn_WK", "WVT": "L3_gnn_WV"}
_PLAIN = ["x", "adj", "L0_gnn_v", "L1_gnn_in_W", "L1_gnn_in_b", "L1_gnn_out_W", "L1_gnn_out_b", "L1_gnn_r_b",
          "L1_gnn_z_b", "L1_gnn_h_b", "L1_gnn_o1_b", "L1_gnn_o2_b", "L2_gnn_b_self", "L2_gnn_b_nb",
          "L2_gnn_W_comb", "L2_gnn_b_comb", "L3_gnn_we", "L3_gnn_be"]


def kernel(**inputs):
    import numpy as _np
    import concourse.bacc as _bacc
    from concourse import mybir as _mybir
    from concourse.bass_utils import run_bass_kernel_spmd as _run

    host = {n: _np.ascontiguousarray(_np.asarray(inputs[n])) for n in _PLAIN}
    host.update({n: _np.ascontiguousarray(_np.asarray(inputs[s]).T) for n, s in _T.items()})
    for n, a in host.items():
        if a.shape == (256,):
            host[n] = _np.ascontiguousarray(a.reshape(2, 128).T)
    host["L3_gnn_we"] = host["L3_gnn_we"].reshape(32, 1)
    host["c_ident"] = _np.eye(128, dtype=_np.float32)
    host["c_ident16"] = _np.eye(128, dtype=_np.float16)
    host["c_ones"] = _np.ones((128, 128), _np.float16)
    host["c_sel"] = _np.concatenate([_np.eye(3, dtype=_np.float32)] * 2)

    nc = _bacc.Bacc("TRN2", target_bir_lowering=False, num_devices=1)
    arrays, args = {}, {}
    for n, a in host.items():
        arrays[f"in_{n}_dram"] = a
        args[n] = nc.dram_tensor(f"in_{n}_dram", a.shape, _mybir.dt.from_np(a.dtype), kind="ExternalInput").ap()
    out = nc.dram_tensor("out_0_dram", (2048, 256), _mybir.dt.float32, kind="ExternalOutput").ap()
    spill = nc.dram_tensor("spill_dram", (2048, 256), _mybir.dt.float32, kind="Internal").ap()
    resnorm_kernel(nc, args, out, spill)
    r = _run(nc, [arrays], core_ids=[0])
    return r.results[0]["out_0_dram"]
```
